# Optimizing a Trainium2 kernel written in Bass

```python
import numpy as np
import jax
import jax.numpy as jnp

def _softmax(x, axis=-1):
    return jax.nn.softmax(x, axis=axis)

def _gelu(x):
    return jax.nn.gelu(x, approximate=True)

def _silu(x):
    return jax.nn.silu(x)

def _sigmoid(x):
    return jax.nn.sigmoid(x)

def _layernorm(x, axis=-1, eps=1e-05):
    m = jnp.mean(x, axis=axis, keepdims=True)
    v = jnp.var(x, axis=axis, keepdims=True)
    return (x - m) / jnp.sqrt(v + eps)

def _scatter_add(tgt, idx, src, axis=0):
    return tgt.at[idx].add(src)

def _segment_sum(src, seg, n):
    return jax.ops.segment_sum(src, seg, n)
kernel_name = 'mk_gnn_ffn_d2_gnn_r32_b3ef15'

def setup_inputs(seed: int=0):
    np.random.seed(seed)
    _w = jnp.asarray

    def _rec_inputs():
        import jax
        import jax.numpy as jnp
        _gk = jax.random.key(seed)
        x = -0.0003929 + 0.9999 * jax.random.normal(jax.random.fold_in(_gk, 1), (3125, 256), jnp.float32)
        src = jax.random.randint(jax.random.fold_in(_gk, 2), (50000,), 0, 3125, jnp.int32)
        dst = jnp.minimum((3125 * jax.random.uniform(jax.random.fold_in(_gk, 3), (50000,)) ** 2.0).astype(jnp.int32), 99999)
        _o = jnp.argsort(dst, stable=True)
        src = src[_o]
        dst = dst[_o]
        edge_weight = 0.00540447 + 1.00226 * jax.random.normal(jax.random.fold_in(_gk, 13), (50000,), jnp.float32)
        return (x, src, dst, edge_weight)
    x, src, dst, edge_weight = _rec_inputs()

    def _L0_gnn_setup():
        import jax, jax.numpy as jnp
        import numpy as np
        from itertools import combinations
        NDIM = 256
        BATCH = 2048

        def _build_mat(rots, idx_i, idx_j, ndim):

            def step(mat, t):
                i, j, theta = t
                c = jnp.cos(theta)
                s = jnp.sin(theta)
                ri = mat[i]
                rj = mat[j]
                mat = mat.at[i].set(c * ri - s * rj)
                mat = mat.at[j].set(s * ri + c * rj)
                return (mat, None)
            mat0 = jnp.eye(ndim, dtype=rots.dtype)
            mat, _ = jax.lax.scan(step, mat0, (idx_i, idx_j, rots))
            return mat.T
        key = jax.random.key(seed)
        k1, k2 = jax.random.split(key)
        pairs = np.array(list(combinations(range(NDIM), 2)), dtype=np.int32)
        return {'x': jax.random.normal(k1, (BATCH, NDIM), dtype=jnp.float32), 'rots': jax.random.normal(k2, (pairs.shape[0],), dtype=jnp.float32), 'idx_i': jnp.asarray(pairs[:, 0]), 'idx_j': jnp.asarray(pairs[:, 1])}
    _L0_gnn_all = _L0_gnn_setup()
    _L0_gnn_in = {k: v for k, v in _L0_gnn_all.items() if k in ()}
    del _L0_gnn_all

    def _L0_ffn_setup():
        import jax, jax.numpy as jnp
        import numpy as np
        B, N, D = (16, 128, 256)
        NUM_EXPERTS, TOP_K, HEADS = (4, 2, 4)
        N_EDGES = 32768
        LN_EPS = 1e-05

        def _layernorm(x, g, b):
            mu = x.mean(-1, keepdims=True)
            var = ((x - mu) ** 2).mean(-1, keepdims=True)
            return (x - mu) * jax.lax.rsqrt(var + LN_EPS) * g + b

        def _forward(x, edge_index, W_gat, att_src, att_dst, b_gat, ln_gamma, ln_beta, W1, b1, W2, b2):
            Bc, Nc, Dc = x.shape
            M = Bc * Nc
            x_flat = x.reshape(M, Dc)
            h = (x_flat @ W_gat).reshape(M, HEADS, NUM_EXPERTS)
            loops = jnp.arange(M, dtype=edge_index.dtype)
            src = jnp.concatenate([edge_index[0], loops])
            dst = jnp.concatenate([edge_index[1], loops])
            a_src = (h * att_src).sum(-1)
            a_dst = (h * att_dst).sum(-1)
            e = jax.nn.leaky_relu(a_src[src] + a_dst[dst], negative_slope=0.2)
            e_max = jax.ops.segment_max(e, dst, num_segments=M)
            ee = jnp.exp(e - e_max[dst])
            denom = jax.ops.segment_sum(ee, dst, num_segments=M)
            alpha = ee / (denom[dst] + 1e-16)
            msg = h[src] * alpha[:, :, None]
            agg = jax.ops.segment_sum(msg, dst, num_segments=M).reshape(M, HEADS * NUM_EXPERTS) + b_gat
            scores = _layernorm(agg, ln_gamma, ln_beta).reshape(M, HEADS, NUM_EXPERTS).mean(1)
            scores = scores.reshape(Bc, Nc, NUM_EXPERTS)
            topk_s, topk_i = jax.lax.top_k(scores, TOP_K)
            w = jax.nn.softmax(topk_s, axis=-1)
            out = jnp.zeros_like(x)
            for ei in range(NUM_EXPERTS):
                g = jnp.where(topk_i == ei, w, 0.0).sum(-1)
                hh = jax.nn.gelu(x @ W1[ei] + b1[ei], approximate=False)
                out = out + g[..., None] * (hh @ W2[ei] + b2[ei])
            return out
        key = jax.random.key(seed)
        ks = jax.random.split(key, 8)
        s = 0.05
        return {'x': jax.random.normal(ks[0], (B, N, D), jnp.float32), 'W_gat': jax.random.normal(ks[1], (D, HEADS * NUM_EXPERTS), jnp.float32) * s, 'att_src': jax.random.normal(ks[2], (HEADS, NUM_EXPERTS), jnp.float32) * s, 'att_dst': jax.random.normal(ks[3], (HEADS, NUM_EXPERTS), jnp.float32) * s, 'b_gat': jnp.zeros((HEADS * NUM_EXPERTS,), jnp.float32), 'ln_gamma': jnp.ones((HEADS * NUM_EXPERTS,), jnp.float32), 'ln_beta': jnp.zeros((HEADS * NUM_EXPERTS,), jnp.float32), 'W1': jax.random.normal(ks[4], (NUM_EXPERTS, D, 2 * D), jnp.float32) * s, 'b1': jnp.zeros((NUM_EXPERTS, 2 * D), jnp.float32), 'W2': jax.random.normal(ks[5], (NUM_EXPERTS, 2 * D, D), jnp.float32) * s, 'b2': jnp.zeros((NUM_EXPERTS, D), jnp.float32), 'edge_index': jax.random.randint(ks[6], (2, N_EDGES), 0, B * N, jnp.int32)}
    _L0_ffn_all = _L0_ffn_setup()
    _L0_ffn_in = {k: v for k, v in _L0_ffn_all.items() if k in ('W_gat', 'att_src', 'att_dst', 'b_gat', 'ln_gamma', 'ln_beta', 'W1', 'b1', 'W2', 'b2', 'edge_index')}
    del _L0_ffn_all

    def _L1_gnn_setup():
        import jax, jax.numpy as jnp
        import numpy as np
        N_NODES = 3125
        N_EDGES = 100000
        D_IN = 256
        D_OUT = 256
        LEAKY_SLOPE = 0.01
        key = jax.random.key(seed)
        ks = jax.random.split(key, 8)
        s_in = 1.0 / np.sqrt(D_IN)
        s_out = 1.0 / np.sqrt(D_OUT)
        return {'features': jax.random.normal(ks[0], (N_NODES, D_IN), dtype=jnp.float32), 'indices': jax.random.randint(ks[1], (2, N_EDGES), 0, N_NODES, dtype=jnp.int64), 'W_layer': jax.random.uniform(ks[2], (D_OUT, D_IN), jnp.float32, -s_in, s_in), 'b_layer': jax.random.uniform(ks[3], (D_OUT,), jnp.float32, -s_in, s_in), 'w_a1': jax.random.uniform(ks[4], (1, D_OUT), jnp.float32, -s_out, s_out), 'b_a1': jax.random.uniform(ks[5], (1,), jnp.float32, -s_out, s_out), 'w_a2': jax.random.uniform(ks[6], (1, D_OUT), jnp.float32, -s_out, s_out), 'b_a2': jax.random.uniform(ks[7], (1,), jnp.float32, -s_out, s_out)}
    _L1_gnn_all = _L1_gnn_setup()
    _L1_gnn_in = {k: v for k, v in _L1_gnn_all.items() if k in ('W_layer', 'b_layer', 'w_a1', 'b_a1', 'w_a2', 'b_a2')}
    del _L1_gnn_all

    def _L1_ffn_setup():
        import math
        import jax, jax.numpy as jnp
        import numpy as np
        CAPACITY_FACTOR = 1.25
        key = jax.random.key(seed)
        ks = jax.random.split(key, 5)
        B, L, D, F, E = (8, 256, 256, 1024, 8)
        h = jax.random.normal(ks[0], (B, L, D), dtype=jnp.float32)
        gate_w = jax.random.normal(ks[1], (D, E), dtype=jnp.float32) * 0.02
        gate_b = jnp.zeros((E,), dtype=jnp.float32)
        w1 = jax.random.normal(ks[2], (E, D, F), dtype=jnp.float32) * (1.0 / math.sqrt(D))
        b1 = jnp.zeros((E, F), dtype=jnp.float32)
        w2 = jax.random.normal(ks[3], (E, F, D), dtype=jnp.float32) * (1.0 / math.sqrt(F))
        b2 = jnp.zeros((E, D), dtype=jnp.float32)
        return {'h': h, 'gate_w': gate_w, 'gate_b': gate_b, 'w1': w1, 'b1': b1, 'w2': w2, 'b2': b2}
    _L1_ffn_all = _L1_ffn_setup()
    _L1_ffn_in = {k: v for k, v in _L1_ffn_all.items() if k in ('gate_w', 'gate_b', 'w1', 'b1', 'w2', 'b2')}
    del _L1_ffn_all
    return {'x': x, 'src': src, 'dst': dst, 'edge_weight': edge_weight, 'L0_ffn_W_gat': _L0_ffn_in['W_gat'], 'L0_ffn_att_src': _L0_ffn_in['att_src'], 'L0_ffn_att_dst': _L0_ffn_in['att_dst'], 'L0_ffn_b_gat': _L0_ffn_in['b_gat'], 'L0_ffn_ln_gamma': _L0_ffn_in['ln_gamma'], 'L0_ffn_ln_beta': _L0_ffn_in['ln_beta'], 'L0_ffn_W1': _L0_ffn_in['W1'], 'L0_ffn_b1': _L0_ffn_in['b1'], 'L0_ffn_W2': _L0_ffn_in['W2'], 'L0_ffn_b2': _L0_ffn_in['b2'], 'L0_ffn_edge_index': _L0_ffn_in['edge_index'], 'L1_gnn_W_layer': _L1_gnn_in['W_layer'], 'L1_gnn_b_layer': _L1_gnn_in['b_layer'], 'L1_gnn_w_a1': _L1_gnn_in['w_a1'], 'L1_gnn_b_a1': _L1_gnn_in['b_a1'], 'L1_gnn_w_a2': _L1_gnn_in['w_a2'], 'L1_gnn_b_a2': _L1_gnn_in['b_a2'], 'L1_ffn_gate_w': _L1_ffn_in['gate_w'], 'L1_ffn_gate_b': _L1_ffn_in['gate_b'], 'L1_ffn_w1': _L1_ffn_in['w1'], 'L1_ffn_b1': _L1_ffn_in['b1'], 'L1_ffn_w2': _L1_ffn_in['w2'], 'L1_ffn_b2': _L1_ffn_in['b2']}

def reference(x, src, dst, edge_weight, L0_ffn_W_gat, L0_ffn_att_src, L0_ffn_att_dst, L0_ffn_b_gat, L0_ffn_ln_gamma, L0_ffn_ln_beta, L0_ffn_W1, L0_ffn_b1, L0_ffn_W2, L0_ffn_b2, L0_ffn_edge_index, L1_gnn_W_layer, L1_gnn_b_layer, L1_gnn_w_a1, L1_gnn_b_a1, L1_gnn_w_a2, L1_gnn_b_a2, L1_ffn_gate_w, L1_ffn_gate_b, L1_ffn_w1, L1_ffn_b1, L1_ffn_w2, L1_ffn_b2):
    import jax
    import jax.numpy as jnp

    def _L0_gnn_ref(x, rots, idx_i, idx_j):
        import jax, jax.numpy as jnp
        import numpy as np
        from itertools import combinations
        NDIM = 256
        BATCH = 2048

        def _build_mat(rots, idx_i, idx_j, ndim):

            def step(mat, t):
                i, j, theta = t
                c = jnp.cos(theta)
                s = jnp.sin(theta)
                ri = mat[i]
                rj = mat[j]
                mat = mat.at[i].set(c * ri - s * rj)
                mat = mat.at[j].set(s * ri + c * rj)
                return (mat, None)
            mat0 = jnp.eye(ndim, dtype=rots.dtype)
            mat, _ = jax.lax.scan(step, mat0, (idx_i, idx_j, rots))
            return mat.T
        m = _build_mat(rots, idx_i, idx_j, x.shape[-1])
        return x @ m

    def _L0_ffn_ref(x, W_gat, att_src, att_dst, b_gat, ln_gamma, ln_beta, W1, b1, W2, b2, edge_index):
        import jax, jax.numpy as jnp
        import numpy as np
        B, N, D = (16, 128, 256)
        NUM_EXPERTS, TOP_K, HEADS = (4, 2, 4)
        N_EDGES = 32768
        LN_EPS = 1e-05

        def _layernorm(x, g, b):
            mu = x.mean(-1, keepdims=True)
            var = ((x - mu) ** 2).mean(-1, keepdims=True)
            return (x - mu) * jax.lax.rsqrt(var + LN_EPS) * g + b

        def _forward(x, edge_index, W_gat, att_src, att_dst, b_gat, ln_gamma, ln_beta, W1, b1, W2, b2):
            Bc, Nc, Dc = x.shape
            M = Bc * Nc
            x_flat = x.reshape(M, Dc)
            h = (x_flat @ W_gat).reshape(M, HEADS, NUM_EXPERTS)
            loops = jnp.arange(M, dtype=edge_index.dtype)
            src = jnp.concatenate([edge_index[0], loops])
            dst = jnp.concatenate([edge_index[1], loops])
            a_src = (h * att_src).sum(-1)
            a_dst = (h * att_dst).sum(-1)
            e = jax.nn.leaky_relu(a_src[src] + a_dst[dst], negative_slope=0.2)
            e_max = jax.ops.segment_max(e, dst, num_segments=M)
            ee = jnp.exp(e - e_max[dst])
            denom = jax.ops.segment_sum(ee, dst, num_segments=M)
            alpha = ee / (denom[dst] + 1e-16)
            msg = h[src] * alpha[:, :, None]
            agg = jax.ops.segment_sum(msg, dst, num_segments=M).reshape(M, HEADS * NUM_EXPERTS) + b_gat
            scores = _layernorm(agg, ln_gamma, ln_beta).reshape(M, HEADS, NUM_EXPERTS).mean(1)
            scores = scores.reshape(Bc, Nc, NUM_EXPERTS)
            topk_s, topk_i = jax.lax.top_k(scores, TOP_K)
            w = jax.nn.softmax(topk_s, axis=-1)
            out = jnp.zeros_like(x)
            for ei in range(NUM_EXPERTS):
                g = jnp.where(topk_i == ei, w, 0.0).sum(-1)
                hh = jax.nn.gelu(x @ W1[ei] + b1[ei], approximate=False)
                out = out + g[..., None] * (hh @ W2[ei] + b2[ei])
            return out
        return _forward(x, edge_index, W_gat, att_src, att_dst, b_gat, ln_gamma, ln_beta, W1, b1, W2, b2)

    def _L1_gnn_ref(features, indices, W_layer, b_layer, w_a1, b_a1, w_a2, b_a2):
        import jax, jax.numpy as jnp
        import numpy as np
        N_NODES = 3125
        N_EDGES = 100000
        D_IN = 256
        D_OUT = 256
        LEAKY_SLOPE = 0.01
        n = features.shape[0]
        h = features @ W_layer.T + b_layer
        a1 = (h @ w_a1.T + b_a1)[:, 0]
        a2 = (h @ w_a2.T + b_a2)[:, 0]
        row = indices[0]
        col = indices[1]
        v = jax.nn.leaky_relu(a1[row] + a2[col], negative_slope=LEAKY_SLOPE)
        m = jax.ops.segment_max(v, row, num_segments=n)
        ev = jnp.exp(v - m[row])
        s = jax.ops.segment_sum(ev, row, num_segments=n)
        att = ev / s[row]
        out = jax.ops.segment_sum(att[:, None] * h[col], row, num_segments=n)
        return out

    def _L1_ffn_ref(h, gate_w, gate_b, w1, b1, w2, b2):
        import math
        import jax, jax.numpy as jnp
        import numpy as np
        CAPACITY_FACTOR = 1.25
        B, L, D = h.shape
        E = gate_w.shape[1]
        T = B * L
        C = max(1, math.ceil(CAPACITY_FACTOR * T / E))
        x = h.reshape(T, D)
        logits = x @ gate_w + gate_b
        probs = jax.nn.softmax(logits, axis=-1)
        idx = jnp.argmax(probs, axis=-1)
        prb = jnp.take_along_axis(probs, idx[:, None], axis=1)[:, 0]
        one_hot = jax.nn.one_hot(idx, E, dtype=jnp.float32)
        pos = (jnp.cumsum(one_hot, axis=0) * one_hot).sum(-1).astype(jnp.int32) - 1
        kept = pos < C
        pos_safe = jnp.where(kept, pos, C)
        buf = jnp.zeros((E, C, D), dtype=h.dtype).at[idx, pos_safe].set(x, mode='drop')
        hmid = jax.nn.relu(jnp.einsum('ecd,edf->ecf', buf, w1) + b1[:, None, :])
        ybuf = jnp.einsum('ecf,efd->ecd', hmid, w2) + b2[:, None, :]
        pos_g = jnp.minimum(pos, C - 1)
        y_tok = ybuf[idx, pos_g] * (prb * kept)[:, None]
        y = y_tok.reshape(B, L, D)
        y = jnp.nan_to_num(y, nan=0.0, posinf=10000.0, neginf=-10000.0)
        return y
    edge_index = jnp.stack([src, dst])
    x = x + _L0_gnn_ref(_layernorm(x, axis=-1), edge_weight, src, dst)
    x = x + _L0_ffn_ref(_layernorm(x, axis=-1)[None], L0_ffn_W_gat, L0_ffn_att_src, L0_ffn_att_dst, L0_ffn_b_gat, L0_ffn_ln_gamma, L0_ffn_ln_beta, L0_ffn_W1, L0_ffn_b1, L0_ffn_W2, L0_ffn_b2, L0_ffn_edge_index)[0]
    x = x + _L1_gnn_ref(_layernorm(x, axis=-1), edge_index, L1_gnn_W_layer, L1_gnn_b_layer, L1_gnn_w_a1, L1_gnn_b_a1, L1_gnn_w_a2, L1_gnn_b_a2)
    x = x + _L1_ffn_ref(_layernorm(x, axis=-1)[None], L1_ffn_gate_w, L1_ffn_gate_b, L1_ffn_w1, L1_ffn_b1, L1_ffn_w2, L1_ffn_b2)[0]
    return x

_drawn_inputs = setup_inputs


def setup_inputs(seed=0):
    import zlib

    import numpy as np

    out = dict(_drawn_inputs(seed))
    spreads = {'L0_ffn_b_gat': (0.0, 0.1),
     'L0_ffn_ln_gamma': (1.0, 0.2),
     'L0_ffn_ln_beta': (0.0, 0.1),
     'L0_ffn_b1': (0.0, 0.1),
     'L0_ffn_b2': (0.0, 0.1),
     'L1_ffn_gate_b': (0.0, 0.1),
     'L1_ffn_b1': (0.0, 0.647),
     'L1_ffn_b2': (0.0, 0.452)}
    factors = {'L1_gnn_w_a1': 3.108}
    for name, (base, spread) in spreads.items():
        noise = np.random.default_rng([zlib.crc32(name.encode()), seed]).standard_normal(out[name].shape)
        drawn = base * np.exp(spread * noise) if base else spread * noise
        out[name] = jnp.asarray(drawn.astype(out[name].dtype))
    for name, factor in factors.items():
        out[name] = (out[name] * factor).astype(out[name].dtype)
    return out
```

```python
from contextlib import ExitStack

import concourse.bass as bass
from concourse import mybir

F32 = mybir.dt.float32
BF16 = mybir.dt.bfloat16
I32 = mybir.dt.int32
I16 = mybir.dt.int16
ALU = mybir.AluOpType
ACT = mybir.ActivationFunctionType
X = mybir.AxisListType.X
XY = mybir.AxisListType.XY

P = 128
N = 3125
D = 256
H2 = D // P
T = -(-N // P)
NFULL = N // P
NREST = N - NFULL * P
EPS = 1e-5
BIG = 2.0 ** 100

G = 4
GE = G * P
E0 = 32768
E1 = 50000
NG0 = (E0 + T * (GE - 1)) // GE
NG1 = (E1 + T * (GE - 1)) // GE

CH = P
NCH = -(-E1 // CH)
CB = -(-NCH // P)
OWN = P - 1
BU = 4
NTURN = -(-(2 * E1) // (OWN * BU))
WIN = 3
NF = 10
TWO_PI = 6.283185307179586
TWO_PI_HI = 6.28125
TWO_PI_LO = TWO_PI - TWO_PI_HI
PI_SAFE = 3.1415925
MAGIC = 1.5 * 2.0 ** 23


class Count:

    def __init__(self, sem):
        self.sem, self.n, self.turn, self.per = sem, 0, None, 0

    def mark(self, ins, by=1):
        ins.then_inc(self.sem, by)
        self.n += by
        return self.value()

    def value(self):
        return self.n if self.turn is None else self.turn * self.per + self.n

    def enter(self, turn, per):
        self.turn, self.per, self.start = turn, per, self.n

    def leave(self, turns):
        assert self.n - self.start == self.per, (self.n - self.start, self.per)
        self.n = self.start + self.per * turns
        self.turn = None


def build(nc, A, out, dump=None, upto=99):
    with ExitStack() as ctx:
        nsem = [0]

        def sb(name, shape, dt, where=ctx):
            return where.enter_context(nc.sbuf_tensor(name, shape, dt))

        def pb(name, shape, where):
            return where.enter_context(nc.psum_tensor(name, shape, F32))

        live = []

        def sem(name):
            live.append(nc.alloc_semaphore(name=name))
            return live[-1]

        def recycle():
            nc.all_engine_barrier()
            nc.clear_and_free_semaphores(list(live))
            nc.all_engine_barrier()
            live.clear()

        g = {"recycle": recycle}
        g |= {}
        g["x"] = sb("x_nodes", [P, T, D], F32)
        g["iota"] = sb("iota_row", [P, WIN * P], F32)
        g["iota16"] = sb("iota_row16", [P, WIN * P], I16)
        g["pidx"] = sb("partition_index", [P, 1], F32)
        g["ident"] = sb("identity", [P, P], F32)
        g["identb"] = sb("identity_bf", [P, P], BF16)
        g["before"] = sb("row_before_column", [P, P], F32)
        g["ones"] = sb("ones", [P, P], F32)
        g["group_tile0"] = sb("group_tile0", [1, P], I32)
        g["group_tile1"] = sb("group_tile1", [1, P], I32)
        g["rot"] = sb("rotation_matrix", [P, H2, D], F32)
        g["list0"] = nc.dram_tensor("edges_by_tile0", (P * G * NG0, 2), F32).ap()
        g["list1"] = nc.dram_tensor("edges_by_tile1", (P * G * NG1, 2), F32).ap()
        g["window_dram"] = nc.dram_tensor("window_of_chunk", (CB * P,), I32).ap()
        constants(nc, A, g, sem)
        rotations(nc, A, g, sem, sb, pb, dump, upto)
        if upto <= 2:
            return
        recycle()
        rest(nc, A, g, sem, sb, pb, out, dump, upto)


def constants(nc, A, g, sem):
    x_loaded, iota_done, const_done, zeroed = sem("x_loaded"), sem("iota_done"), sem("const_done"), sem("x_padding_zeroed")
    with nc.Block() as block:
        @block.sync
        def _(sp):
            sp.dma_start(g["x"][:, 0:NFULL, :], A["x"][0:NFULL * P, :].rearrange("(t p) d -> p t d", p=P)).then_inc(x_loaded, 16)
            sp.wait_ge(zeroed, 1)
            sp.dma_start(g["x"][0:NREST, NFULL, :], A["x"][NFULL * P:N, :]).then_inc(x_loaded, 16)
            sp.wait_ge(x_loaded, 32)

        @block.gpsimd
        def _(pool):
            nc.gpsimd.iota(g["iota"][:], [[1, WIN * P]], base=0, channel_multiplier=0,
                           allow_small_or_imprecise_dtypes=True).then_inc(iota_done, 1)
            nc.gpsimd.iota(g["iota16"][:], [[1, WIN * P]], base=0, channel_multiplier=0,
                           allow_small_or_imprecise_dtypes=True).then_inc(iota_done, 1)
            nc.gpsimd.iota(g["pidx"][:], [[0, 1]], base=0, channel_multiplier=1,
                           allow_small_or_imprecise_dtypes=True).then_inc(iota_done, 1)

        @block.vector
        def _(dve):
            nc.vector.memset(g["x"][:, NFULL, :], 0.0).then_inc(zeroed, 1)
            nc.vector.memset(g["ones"][:], 1.0).then_inc(const_done, 1)
            dve.wait_ge(iota_done, 3)
            row = g["iota"][:, 0:P]
            nc.vector.tensor_scalar(g["ident"][:], row, g["pidx"][:], None, ALU.is_equal).then_inc(const_done, 1)
            nc.vector.tensor_scalar(g["identb"][:], row, g["pidx"][:], None, ALU.is_equal).then_inc(const_done, 1)
            nc.vector.tensor_scalar(g["before"][:], row, g["pidx"][:], None, ALU.is_gt).then_inc(const_done, 1)


def rotations(nc, A, g, sem, sb, pb, dump, upto):
    with ExitStack() as sc:
        def t(name, shape, dt=F32):
            return sb(name, shape, dt, sc)

        lists = []
        for n, (rows, cols, key, other, ngroups) in enumerate((
                (P, E0 // P, A["ei"][1], A["ei"][0], NG0),
                (125, E1 // 125, A["src"], A["dst"], NG1))):
            lists.append(dict(
                n=n, R=rows, F=cols, key_in=key, other_in=other, NG=ngroups, NB=ngroups * G,
                key=t(f"key{n}", [rows, cols], I32), other=t(f"other{n}", [rows, cols], I32),
                tile=t(f"tile{n}", [rows, cols]), slot=t(f"slot{n}", [rows, cols], I32),
                rec=t(f"record{n}", [rows, cols, 2]), list=g[f"list{n}"], group_tile=g[f"group_tile{n}"]))
        FL = max(l["F"] for l in lists)
        tmp_i = t("tmp_i", [P, FL], I32)
        small = t("small", [P, 8, T])
        small_i = t("small_i", [P, T], I32)
        stage_rec = t("stage_rec", [P, 2, 8, 2])
        stage_slot = t("stage_slot", [P, 2, 8], I32)
        ia, ja = t("i_int", [P, CB, CH], I32), t("j_int", [P, CB, CH], I32)
        wa = t("w_a", [P, CB, CH])
        cs = t("chunk_small", [P, 8, CB])
        csi = t("chunk_small_i", [P, 2, CB], I32)
        window_row = t("window_row", [1, CB * P], I32)
        turns_i = t("turns_i", [1, 1], I32)
        NCOMP = BU * NTURN + WIN
        fieldsB = {k: t("rB_" + k, [P, CB * CH]) for k in ("i", "j", "w", "q")}
        comp = t("terms", [P, NCOMP, NF])

        s = {k: sem(k) for k in (
            "edges0_loaded", "edges1_loaded", "rot_loaded", "rot_padded", "fill_ready", "list_filled", "dve_step", "totals_ready",
            "prefix_ready", "prefix_read", "slots_ready", "pool_step", "pool_ok", "scattered", "window_out",
            "window_in", "fieldsA_ready", "fieldsB_ready", "sin_in", "sin_out", "onehot_ready",
            "chunk_summed", "chunk_added", "comp_zeroed", "compact_done", "act_step")}
        block = nc.Block()
        with ExitStack() as inner:
            wk = ExitStack()
            mask = wk.enter_context(nc.sbuf_tensor("tile_mask", [P, T * FL], F32))
            scan = wk.enter_context(nc.sbuf_tensor("tile_scan", [P, T * FL], F32))
            fill = wk.enter_context(nc.sbuf_tensor("list_fill", [P, G * NG1, 2], F32))
            pre = pb("prefix_ps", [P, 512], wk)
            Fa = {k: wk.enter_context(nc.sbuf_tensor("rA_" + k, [P, CB, CH], F32)) for k in ("i", "j", "a", "b", "f", "scan", "q")}
            tp = wk.enter_context(nc.psum_tensor("fields_ps", [P, 4, CB * CH], F32))
            with nc.Block() as block:
                @block.sync
                def _(sp):
                    for l in lists:
                        sp.dma_start(l["key"][:], l["key_in"].rearrange("(p f) -> p f", p=l["R"])).then_inc(s[f"edges{l['n']}_loaded"], 16)
                        sp.dma_start(l["other"][:], l["other_in"].rearrange("(p f) -> p f", p=l["R"])).then_inc(s[f"edges{l['n']}_loaded"], 16)
                    sp.wait_ge(s["rot_padded"], 3)
                    full, last = E1 // (P * CH), E1 % CH
                    more = NCH - 1 - full * P
                    for tile_, src in ((ia, A["src"]), (ja, A["dst"]), (wa, A["w"])):
                        sp.dma_start(tile_[:, 0:full, :], src[0:full * P * CH].rearrange("(b p s) -> p b s", p=P, s=CH)).then_inc(s["rot_loaded"], 16)
                        sp.dma_start(tile_[0:more, full, :], src[full * P * CH:(NCH - 1) * CH].rearrange("(p s) -> p s", s=CH)).then_inc(s["rot_loaded"], 16)
                        sp.dma_start(tile_[more:more + 1, full, 0:last], src[(NCH - 1) * CH:E1].rearrange("(a s) -> a s", a=1)).then_inc(s["rot_loaded"], 16)
                    sp.wait_ge(s["fill_ready"], 2)
                    for l in lists:
                        sp.dma_start(l["list"].rearrange("(p c) k -> p c k", p=P), fill[:, 0:l["NB"], :]).then_inc(s["list_filled"], 16)
                    sp.wait_ge(s["window_out"], 1)
                    sp.dma_start(g["window_dram"].rearrange("(b p) -> p b", p=P), csi[:, 0, :], allow_slow_non_contiguous=True).then_inc(s["window_in"], 16)
                    sp.wait_ge(s["window_in"], 16)
                    sp.dma_start(window_row[:], g["window_dram"].rearrange("(a c) -> a c", a=1)).then_inc(s["window_in"], 16)
                    sp.wait_ge(s["window_in"], 32)
                    sp.wait_ge(s["list_filled"], 32)

                @block.gpsimd
                def _(pool):
                    nc.gpsimd.memset(ia[:], 99999).then_inc(s["rot_padded"], 1)
                    nc.gpsimd.memset(ja[:], 99999).then_inc(s["rot_padded"], 1)
                    nc.gpsimd.memset(wa[:], 0.0).then_inc(s["rot_padded"], 1)
                    nc.gpsimd.memset(fill[:, :, 0:1].bitcast(I32), N).then_inc(s["fill_ready"], 1)
                    nc.gpsimd.memset(fill[:, :, 1:2], -1.0).then_inc(s["fill_ready"], 1)
                    nc.gpsimd.memset(comp[:], 0.0).then_inc(s["comp_zeroed"], 1)
                    pool.wait_ge(s["comp_zeroed"], 1)

                @block.vector
                def _(dve):
                    c = Count(s["dve_step"])

                    def link(ins):
                        dve.wait_ge(c.sem, c.mark(ins))

                    for l in lists:
                        R, F, NB = l["R"], l["F"], l["NB"]
                        m3 = mask[0:R, 0:T * F].rearrange("p (b f) -> p b f", b=T)
                        s3 = scan[0:R, 0:T * F].rearrange("p (b f) -> p b f", b=T)
                        tot, cnt, ngr, gst, sta = (small[:, k, :] for k in range(5))
                        dve.wait_ge(s[f"edges{l['n']}_loaded"], 32)
                        link(nc.vector.tensor_single_scalar(tmp_i[0:R, 0:F], l["key"][:], 7, ALU.logical_shift_right))
                        link(nc.vector.tensor_copy(l["tile"][:], tmp_i[0:R, 0:F]))
                        link(nc.vector.tensor_single_scalar(tmp_i[0:R, 0:F], l["key"][:], P - 1, ALU.bitwise_and))
                        link(nc.vector.tensor_copy(l["rec"][:, :, 1], tmp_i[0:R, 0:F]))
                        link(nc.vector.tensor_copy(l["rec"][:, :, 0].bitcast(I32), l["other"][:]))
                        link(nc.vector.tensor_tensor(m3, l["tile"][:].unsqueeze(1).broadcast_to([R, T, F]),
                                                     g["iota"][0:R, 0:T].unsqueeze(2).broadcast_to([R, T, F]), ALU.is_equal))
                        link(nc.vector.tensor_tensor_scan(scan[0:R, 0:T * F], g["ones"][0:R, 0:1].broadcast_to([R, T * F]),
                                                          mask[0:R, 0:T * F], 0.0, ALU.mult, ALU.add))
                        link(nc.vector.tensor_copy(tot[0:R, 0:1], s3[:, 0, F - 1:F]))
                        nc.vector.tensor_tensor(tot[0:R, 1:T], s3[:, 1:T, F - 1], s3[:, 0:T - 1, F - 1], ALU.subtract).then_inc(s["totals_ready"], 1)
                        dve.wait_ge(s["prefix_ready"], 1 + 2 * l["n"])
                        link(nc.vector.tensor_scalar(cnt, pre[:, T:2 * T], float(GE - 1), None, ALU.add))
                        link(nc.vector.tensor_copy(small_i[:], cnt))
                        link(nc.vector.tensor_single_scalar(small_i[:], small_i[:], 9, ALU.logical_shift_right))
                        link(nc.vector.tensor_copy(ngr, small_i[:]))
                        link(nc.vector.tensor_tensor_scan(gst, g["ones"][:, 0:T], ngr, 0.0, ALU.mult, ALU.add))
                        link(nc.vector.tensor_tensor(gst, gst, ngr, ALU.subtract))
                        link(nc.vector.scalar_tensor_tensor(sta, gst, float(GE), pre[:, 0:T], ALU.mult, ALU.add))
                        link(nc.vector.tensor_tensor(sta[0:R], sta[0:R], tot[0:R], ALU.add))
                        link(nc.vector.tensor_tensor(sta[0:R], sta[0:R], s3[:, :, F - 1], ALU.subtract))
                        link(nc.vector.tensor_scalar(sta[0:R], sta[0:R], -1.0, None, ALU.add))
                        link(nc.vector.tensor_scalar(small[:, 5, 1:T], gst[:, 1:T], g["pidx"][:], None, ALU.is_le))
                        nc.vector.tensor_reduce(small[:, 6, 0:1], small[:, 5, 1:T], X, ALU.add).then_inc(s["totals_ready"], 1)
                        link(nc.vector.tensor_tensor(s3, s3, sta[0:R].unsqueeze(2).broadcast_to([R, T, F]), ALU.add))
                        link(nc.vector.tensor_tensor(s3, s3, m3, ALU.mult))
                        link(nc.vector.tensor_reduce(l["tile"][:], s3.rearrange("p b f -> p f b"), X, ALU.add))
                        link(nc.vector.tensor_copy(l["key"][:], l["tile"][:]))
                        link(nc.vector.tensor_single_scalar(tmp_i[0:R, 0:F], l["key"][:], P - 1, ALU.bitwise_and))
                        link(nc.vector.tensor_single_scalar(l["key"][:], l["key"][:], 7, ALU.logical_shift_right))
                        link(nc.vector.scalar_tensor_tensor(l["slot"][:], tmp_i[0:R, 0:F], float(NB), l["key"][:], ALU.mult, ALU.add))
                        dve.wait_ge(s["prefix_ready"], 2 + 2 * l["n"])
                        nc.vector.tensor_copy(l["group_tile"][:], pre[0:1, 64:64 + P]).then_inc(s["prefix_read"], 1)
                    flat = lambda a: a[:].rearrange("p b s -> p (b s)")
                    dve.wait_ge(s["rot_loaded"], 144)
                    fi, fj, aa, bb, ff, sc_, q = (flat(Fa[k]) for k in ("i", "j", "a", "b", "f", "scan", "q"))
                    link(nc.vector.tensor_copy(fi, flat(ia)))
                    link(nc.vector.tensor_copy(fj, flat(ja)))
                    link(nc.vector.tensor_tensor(aa, fi, fj, ALU.not_equal))
                    link(nc.vector.scalar_tensor_tensor(aa, fi, float(D), aa, ALU.is_lt, ALU.mult))
                    link(nc.vector.scalar_tensor_tensor(ff, fj, float(D), aa, ALU.is_lt, ALU.add))
                    for b in range(CB):
                        link(nc.vector.tensor_tensor_scan(Fa["scan"][:, b, :], g["ones"][:, 0:CH], Fa["f"][:, b, :], 0.0, ALU.mult, ALU.add))
                    nc.vector.tensor_copy(cs[:, 0, :], Fa["scan"][:, :, CH - 1]).then_inc(s["totals_ready"], 1)
                    dve.wait_ge(s["prefix_ready"], 5)
                    link(nc.vector.tensor_copy(cs[:, 7, :], pre[:, CB:2 * CB]))
                    link(nc.vector.tensor_tensor_scan(cs[:, 1, :], g["ones"][:, 0:CB], cs[:, 7, :], 0.0, ALU.mult, ALU.add))
                    link(nc.vector.tensor_tensor(cs[:, 2, :], cs[:, 1, :], cs[:, 7, :], ALU.subtract))
                    link(nc.vector.tensor_tensor(cs[:, 2, :], cs[:, 2, :], pre[:, 0:CB], ALU.add))

                    def whole(dst, src, by, plus):
                        link(nc.vector.tensor_scalar(dst, src, plus + 0.5, 1.0 / by, ALU.add, ALU.mult))
                        link(nc.vector.tensor_scalar(dst, dst, -0.5, None, ALU.add))
                        link(nc.vector.tensor_scalar(dst, dst, MAGIC, None, ALU.add))
                        link(nc.vector.tensor_scalar(dst, dst, -MAGIC, None, ALU.add))

                    whole(cs[:, 3, :], cs[:, 2, :], OWN, 0.0)
                    link(nc.vector.tensor_tensor(cs[:, 4, :], cs[:, 2, :], cs[:, 3, :], ALU.add))
                    link(nc.vector.tensor_copy(csi[:, 1, :], cs[:, 4, :]))
                    link(nc.vector.tensor_single_scalar(csi[:, 0, :], csi[:, 1, :], 7, ALU.logical_shift_right))
                    link(nc.vector.tensor_copy(cs[:, 5, :], csi[:, 0, :]))
                    link(nc.vector.tensor_single_scalar(csi[:, 0, :], csi[:, 0, :], NF, ALU.mult))
                    nc.vector.tensor_scalar(cs[:, 6, :], cs[:, 5, :], float(P), None, ALU.mult).then_inc(s["window_out"], 1)
                    dve.wait_ge(s["window_out"], 1)
                    link(nc.vector.tensor_tensor(aa, sc_, ff, ALU.subtract))
                    link(nc.vector.tensor_tensor(Fa["a"][:], Fa["a"][:], cs[:, 2, :].unsqueeze(2).broadcast_to([P, CB, CH]), ALU.add))
                    whole(bb, aa, OWN, 0.0)
                    link(nc.vector.tensor_tensor(q, aa, bb, ALU.add))
                    nc.vector.tensor_tensor(Fa["q"][:], Fa["q"][:], cs[:, 6, :].unsqueeze(2).broadcast_to([P, CB, CH]), ALU.subtract).then_inc(s["fieldsA_ready"], 1)
                    whole(cs[0:1, 7, 0:1], cs[0:1, 1, CB - 1:CB], OWN * BU, float(OWN * BU - 1))
                    link(nc.vector.tensor_scalar(cs[0:1, 7, 0:1], cs[0:1, 7, 0:1], 1.0, None, ALU.max))
                    link(nc.vector.tensor_copy(turns_i[:], cs[0:1, 7, 0:1]))
                    dve.wait_ge(s["prefix_read"], 2)

                @block.scalar
                def _(act):
                    act.wait_ge(s["fieldsB_ready"], 1)
                    for k, f in enumerate(("i", "j", "w", "q")):
                        nc.scalar.copy(fieldsB[f][:], tp[:, k, :])

                @block.tensor
                def _(pe):
                    for l in lists:
                        R = l["R"]
                        pe.wait_ge(s["totals_ready"], 1 + 2 * l["n"])
                        if l["n"]:
                            pe.wait_ge(s["prefix_read"], l["n"])
                        nc.tensor.matmul(pre[:, 0:T], g["before"][0:R, :], small[0:R, 0, :], start=True, stop=True)
                        nc.tensor.matmul(pre[:, T:2 * T], g["ones"][0:R, :], small[0:R, 0, :], start=True, stop=True).then_inc(s["prefix_ready"], 1)
                        pe.wait_ge(s["totals_ready"], 2 + 2 * l["n"])
                        nc.tensor.matmul(pre[0:1, 64:64 + P], small[:, 6, 0:1], g["ident"][:], start=True, stop=True).then_inc(s["prefix_ready"], 1)
                    pe.wait_ge(s["totals_ready"], 5)
                    pe.wait_ge(s["prefix_read"], 2)
                    nc.tensor.matmul(pre[:, 0:CB], g["before"][:], cs[:, 0, :], start=True, stop=True)
                    nc.tensor.matmul(pre[:, CB:2 * CB], g["ones"][:], cs[:, 0, :], start=True, stop=True).then_inc(s["prefix_ready"], 1)
                    pe.wait_ge(s["fieldsA_ready"], 1)
                    for k, f in enumerate((Fa["i"], Fa["j"], wa, Fa["q"])):
                        for b in range(CB):
                            ins = nc.tensor.transpose(tp[:, k, b * CH:(b + 1) * CH], f[:, b, :], g["ident"][:])
                    ins.then_inc(s["fieldsB_ready"], 1)
                    pe.wait_ge(s["fieldsB_ready"], 1)
            if dump and upto == 1:
                dump_stage(nc, sem, dump, [lists[0]["slot"][:], lists[1]["slot"][:], g["group_tile0"][:], g["group_tile1"][:], cs[:, 2, :], turns_i[:], window_row[:]])
            wk.close()
        if upto == 1:
            return
        multiply(nc, g, sem, t, pb, sc, lists, comp, NCOMP, fieldsB, window_row, turns_i, stage_rec, stage_slot, dump, upto)


SCAT = 8


def multiply(nc, g, sem, t, pb, sc, lists, comp, NCOMP, fieldsB, window_row, turns_i, stage_rec, stage_slot, dump, upto):
    names = (
        "lot_staged", "held", "lot_scattered_a", "lot_scattered_b", "step", "angle_ready", "sine_ready",
        "onehot_ready", "window_summed", "window_added", "terms_packed", "v_ready", "vt_ready", "vt_copied",
        "l_ready", "n_ready", "tx_ready", "tx_added", "q_ready", "q_copied", "zy_ready", "zy_copied",
        "dm_ready", "m_added", "m_ready")
    s = {k: sem("rot_" + k) for k in names}
    NC4 = CB * CH
    rec = [t(f"term_records{k}", [P, NC4, NF], BF16) for k in range(2)]
    pos = [t(f"term_position{k}", [P, NC4]) for k in range(2)]
    fi, fj, w1, w2, sn, cn = (t("rB_tmp%d" % k, [P, NC4]) for k in range(6))
    part = t("part_bf", [P, NC4], BF16)
    onehot = t("onehot", [P, 2, 2, WIN * P], BF16)
    below, level, nshift = g["before"], t("level_masks", [P, 7, P]), t("next_column", [P, P])
    xor_i, xs_i = t("xor_i", [P, P], I32), t("xor_shifted", [P, P], I32)
    row_i, col_i = t("row_i", [P, P], I32), t("col_i", [P, P], I32)
    cf = t("coefficients", [P, BU, NF])
    U, V, V2 = t("U", [P, BU, D]), t("V", [P, BU, D]), t("V2", [P, BU, D])
    VT, UT = t("VT", [P, BU, H2, P]), t("UT", [P, BU, H2, P])
    pair_mask = t("pair_mask", [P, BU, P])
    LT = t("LT", [P, BU, P])
    NK = t("NK", [P, 7, BU, P])
    TX = t("TX", [P, BU, 2, P])
    QS = t("QS", [P, BU, P])
    ZS, YS = t("ZS", [P, D]), t("YS", [P, D])
    M = g["rot"]
    ps_a = pb("ps_a", [P, BU, H2, P], sc)
    ps_b = pb("ps_b", [P, BU, H2, P], sc)
    ps_l = pb("ps_l", [P, BU, P], sc)
    ps_q = pb("ps_q", [P, BU, P], sc)
    ps_z = pb("ps_zy", [P, 2, D], sc)
    ps_m = pb("ps_m", [P, H2, D], sc)
    ps_w = [ps_q, ps_m]

    def window(b, w=None):
        flat = ps_q[:].rearrange("p a c -> p (a c)") if b == 0 else ps_m[:].rearrange("p a c -> p (a c)")
        return flat[:, 0:WIN * NF] if w is None else flat[:, w * NF:(w + 1) * NF]

    before_loop = {}
    with nc.Block() as block:
        @block.gpsimd
        def _(pool):
            nc.gpsimd.iota(row_i[:], [[0, P]], base=0, channel_multiplier=1).then_inc(s["m_ready"], 1)
            nc.gpsimd.iota(col_i[:], [[1, P]], base=0, channel_multiplier=0).then_inc(s["m_ready"], 1)
            staged = Count(s["lot_staged"])
            done = [s["lot_scattered_a"], s["lot_scattered_b"]]
            base = [0, 0]
            for l in lists:
                R, F = l["R"], l["F"]

                def lot(turn, b, first):
                    if not first:
                        pool.wait_ge(done[b], base[b] + turn * (SCAT * 16))
                        pool.sem_inc(s["held"], 1)
                    at = (turn * 2 + b) * SCAT
                    cols = slice(at, at + SCAT) if isinstance(at, int) else bass.ds(at, SCAT)
                    staged.mark(nc.gpsimd.tensor_copy(stage_rec[0:R, b], l["rec"][:, cols, :]))
                    v = staged.mark(nc.gpsimd.tensor_copy(stage_slot[0:R, b], l["slot"][:, cols]))
                    pool.wait_ge(staged.sem, v)
                    pool.sem_inc(s["held"], 1)
                    for k in range(SCAT):
                        nc.gpsimd.indirect_dma_start(l["list"][:, :], bass.IndirectOffsetOnAxis(ap=stage_slot[0:R, b, k:k + 1], axis=0),
                                                     stage_rec[0:R, b, k, :], None).then_inc(done[b], 16)

                turns = F // (2 * SCAT)
                for b in range(2):
                    lot(0, b, l["n"] == 0)
                with pool.Fori(1, turns) as i:
                    staged.enter(i - 1, 4)
                    for b in range(2):
                        lot(i, b, False)
                    staged.leave(turns - 1)
                base = [b + turns * SCAT * 16 for b in base]
            for b in range(2):
                pool.wait_ge(done[b], base[b])
            nc.gpsimd.memset(stage_slot[0:1, 0, 0:1], 0)

        @block.scalar
        def _(act):
            act.wait_ge(s["angle_ready"], 1)
            nc.scalar.activation(sn[:], w1[:], ACT.Sin).then_inc(s["sine_ready"], 1)
            nc.scalar.activation(cn[:], w2[:], ACT.Sin).then_inc(s["sine_ready"], 1)
            act.wait_ge(s["terms_packed"], 1)
            trips = act.value_load(turns_i[0:1, 0:1], min_val=1, max_val=NTURN)
            vt, vtc, q, qc, z, zc = (Count(s[k]) for k in ("vt_ready", "vt_copied", "q_ready", "q_copied", "zy_ready", "zy_copied"))
            with act.Fori(0, trips) as i:
                for c_, per in ((vt, 2), (vtc, 2), (q, 6), (qc, 6), (z, 2 * BU), (zc, 2 * BU)):
                    c_.enter(i, per)
                for dst, src in ((VT, ps_a), (UT, ps_b)):
                    vt.n += 1
                    act.wait_ge(vt.sem, vt.value())
                    vtc.mark(nc.scalar.copy(dst[:].rearrange("p u h c -> p (u h c)"), src[:].rearrange("p u h c -> p (u h c)")))
                for k in range(1, 7):
                    q.n += 1
                    act.wait_ge(q.sem, q.value())
                    qc.mark(nc.scalar.copy(QS[:].rearrange("p u c -> p (u c)"), ps_q[:].rearrange("p u c -> p (u c)")))
                for u in range(BU):
                    for k, dst in enumerate((ZS, YS)):
                        z.n += 1
                        act.wait_ge(z.sem, z.value())
                        zc.mark(nc.scalar.copy(dst[:], ps_z[:, k, :]))

        @block.vector
        def _(dve):
            c = Count(s["step"])

            def link(ins):
                dve.wait_ge(c.sem, c.mark(ins))

            dve.wait_ge(s["m_ready"], 2)
            link(nc.vector.tensor_tensor(xor_i[:], row_i[:], col_i[:], ALU.bitwise_xor))
            for k in range(7):
                link(nc.vector.tensor_single_scalar(xs_i[:], xor_i[:], k, ALU.logical_shift_right))
                link(nc.vector.scalar_tensor_tensor(level[:, k, :], xs_i[:], 1.0, below[:], ALU.is_equal, ALU.mult))
            link(nc.vector.tensor_scalar(nshift[:], g["iota"][:, 0:P], -1.0, g["pidx"][:], ALU.add, ALU.is_equal))
            link(nc.vector.tensor_scalar(nshift[:], nshift[:], -1.0, None, ALU.mult))
            for h in range(H2):
                link(nc.vector.tensor_scalar(M[:, h, :], g["iota"][:, 0:D], float(-h * P), g["pidx"][:], ALU.add, ALU.is_equal))
            B = {k: v[:] for k, v in fieldsB.items()}
            link(nc.vector.tensor_scalar(w1[:], B["w"], 1.0 / TWO_PI, None, ALU.mult))
            link(nc.vector.tensor_scalar(w1[:], w1[:], MAGIC, None, ALU.add))
            link(nc.vector.tensor_scalar(w1[:], w1[:], -MAGIC, None, ALU.add))
            link(nc.vector.scalar_tensor_tensor(w2[:], w1[:], -TWO_PI_HI, B["w"], ALU.mult, ALU.add))
            link(nc.vector.scalar_tensor_tensor(w1[:], w1[:], -TWO_PI_LO, w2[:], ALU.mult, ALU.add))
            link(nc.vector.tensor_scalar(w1[:], w1[:], PI_SAFE, -PI_SAFE, ALU.min, ALU.max))
            link(nc.vector.scalar_tensor_tensor(w2[:], w1[:], -1.0, w1[:], ALU.mult, ALU.max))
            link(nc.vector.tensor_scalar(w2[:], w2[:], -1.0, TWO_PI / 4, ALU.mult, ALU.add))
            dve.sem_inc(s["angle_ready"], 1)
            link(nc.vector.tensor_tensor(fi[:], B["i"], B["j"], ALU.not_equal))
            link(nc.vector.scalar_tensor_tensor(fi[:], B["i"], float(D), fi[:], ALU.is_lt, ALU.mult))
            link(nc.vector.tensor_scalar(fj[:], B["j"], float(D), None, ALU.is_lt))
            link(nc.vector.scalar_tensor_tensor(pos[0][:], B["q"], 1.0, fi[:], ALU.add, ALU.mult))
            link(nc.vector.tensor_scalar(pos[0][:], pos[0][:], -1.0, None, ALU.add))
            link(nc.vector.scalar_tensor_tensor(pos[1][:], B["q"], 1.0, fi[:], ALU.add, ALU.add))
            link(nc.vector.tensor_tensor(pos[1][:], pos[1][:], fj[:], ALU.mult))
            link(nc.vector.tensor_scalar(pos[1][:], pos[1][:], -1.0, None, ALU.add))
            for k, f in enumerate(("i", "j")):
                link(nc.vector.tensor_scalar(rec[k][:, :, 0], B[f], float(D - 1), 1.0, ALU.min, ALU.add))
                for r in rec:
                    link(nc.vector.tensor_scalar(r[:, :, 1 + k], B[f], float(D - 1), None, ALU.min))
            link(nc.vector.tensor_tensor(rec[0][:, :, 3], fi[:], fj[:], ALU.mult))
            link(nc.vector.memset(rec[1][:, :, 3], 0.0))
            dve.wait_ge(s["sine_ready"], 2)
            for v, places in ((cn, ((0, 4, 1.0), (1, 7, 1.0))), (sn, ((0, 7, -1.0), (1, 4, 1.0)))):
                for k in range(3):
                    link(nc.vector.tensor_copy(part[:], v[:]))
                    for r, at, sign in places:
                        link(nc.vector.tensor_scalar(rec[r][:, :, at + k], part[:], sign, None, ALU.mult))
                    if k < 2:
                        link(nc.vector.tensor_tensor(v[:], v[:], part[:], ALU.subtract))
            ready, added = Count(s["onehot_ready"]), Count(s["window_added"])
            dve.sem_inc(s["window_added"], 2)
            added.n = 2

            def onehots(c_, b):
                for k in range(2):
                    ready.mark(nc.vector.tensor_scalar(onehot[:, b, k, :], g["iota16"][:], pos[k][:, bass.ds(c_, 1)], None, ALU.is_equal))

            onehots(0, 0)
            summed = Count(s["window_summed"])
            flat = comp[:].rearrange("p n f -> p (n f)")
            with dve.Fori(0, (NCH + 1) // 2) as i:
                added.enter(i, 2)
                summed.enter(i, 2)
                for b in range(2):
                    at = dve.value_load(window_row[0:1, bass.ds(i * 2 + b, 1)], min_val=0, max_val=(NCOMP - WIN) * NF)
                    onehots(i * 2 + b + 1, 1 - b)
                    summed.n += 1
                    dve.wait_ge(summed.sem, summed.value())
                    dve.wait_ge(added.sem, added.value())
                    added.mark(nc.vector.tensor_tensor(flat[:, bass.ds(at, WIN * NF)], flat[:, bass.ds(at, WIN * NF)], window(b), ALU.add))
                added.leave((NCH + 1) // 2)
            dve.wait_ge(added.sem, added.value())
            link(nc.vector.tensor_tensor(comp[:, :, 4:10:3], comp[:, :, 4:10:3], comp[:, :, 5:10:3], ALU.add))
            link(nc.vector.tensor_tensor(comp[:, :, 4:10:3], comp[:, :, 4:10:3], comp[:, :, 6:10:3], ALU.add))
            dve.sem_inc(s["terms_packed"], 1)
            trips = dve.value_load(turns_i[0:1, 0:1], min_val=1, max_val=NTURN)
            step = Count(c.sem)
            step.n = before_loop["step"] = c.n
            vr, lr, nr, tr, ta, dm, ma = (Count(s[k]) for k in ("v_ready", "l_ready", "n_ready", "tx_ready", "tx_added", "dm_ready", "m_added"))
            f3 = lambda a: a[:].rearrange("p u c -> p (u c)")
            with dve.Fori(0, trips) as i:
                for c_, per in ((step, STEPS), (vr, 2), (lr, 1), (nr, 1), (tr, 7), (ta, 7), (dm, BU), (ma, BU)):
                    c_.enter(i, per)

                def slink(ins):
                    dve.wait_ge(step.sem, step.mark(ins))

                slink(move(nc, f3(cf), flat[:, bass.ds(i * (BU * NF), BU * NF)]))
                for u in range(BU):
                    f = lambda k: cf[:, u, k:k + 1]
                    step.mark(nc.vector.tensor_scalar(U[:, u, :], g["iota"][:, 1:D + 1], f(0), None, ALU.is_equal))
                    step.mark(nc.vector.tensor_scalar(V[:, u, :], g["iota"][:, 0:D], f(1), f(4), ALU.is_equal, ALU.mult))
                    step.mark(nc.vector.tensor_scalar(V2[:, u, :], g["iota"][:, 0:D], f(2), f(7), ALU.is_equal, ALU.mult))
                    step.mark(nc.vector.scalar_tensor_tensor(pair_mask[:, u, :], nshift[:], f(3), below[:], ALU.mult, ALU.add))
                dve.wait_ge(step.sem, step.value())
                slink(nc.vector.tensor_tensor(f3(V), f3(V), f3(V2), ALU.add))
                vr.mark(nc.vector.tensor_tensor(f3(V), f3(V), f3(U), ALU.subtract))
                vr.n += 1
                dve.sem_inc(vr.sem, 1)
                lr.n += 1
                dve.wait_ge(lr.sem, lr.value())
                slink(nc.vector.tensor_tensor(LT[:], ps_l[:], pair_mask[:], ALU.mult))
                for k in range(7):
                    ins = nc.vector.tensor_tensor(NK[:, k], LT[:], level[:, k, :].unsqueeze(1).broadcast_to([P, BU, P]), ALU.mult)
                    if k == 0:
                        slink(ins)
                        ta.mark(nc.vector.tensor_tensor(TX[:, :, 0, :], NK[:, 0], g["ident"][:].unsqueeze(1).broadcast_to([P, BU, P]), ALU.add))
                nr.mark(ins)
                tr.n += 1
                dve.wait_ge(tr.sem, tr.value())
                ta.mark(nc.vector.tensor_copy(TX[:, :, 1, :], ps_l[:]))
                for k in range(1, 7):
                    tr.n += 1
                    dve.wait_ge(tr.sem, tr.value())
                    dve.wait_ge(ta.sem, ta.value())
                    w = slice(0, 2) if k < 6 else slice(0, 1)
                    ins = nc.vector.tensor_tensor(TX[:, :, w, :], TX[:, :, w, :], ps_a[:, :, w, :], ALU.add)
                    if k < 6:
                        ta.mark(ins)
                    else:
                        step.mark(ins)
                dve.wait_ge(step.sem, step.value())
                for u in range(BU):
                    dm.n += 1
                    dve.wait_ge(dm.sem, dm.value())
                    ma.mark(nc.vector.tensor_tensor(M[:], M[:], ps_m[:], ALU.add))
                    if u < BU - 1:
                        continue
                dve.wait_ge(ma.sem, ma.value())

        @block.tensor
        def _(pe):
            ready, added, summed = Count(s["onehot_ready"]), Count(s["window_added"]), Count(s["window_summed"])
            with pe.Fori(0, (NCH + 1) // 2) as i:
                for c_, per in ((ready, 4), (added, 2), (summed, 2)):
                    c_.enter(i, per)
                for b in range(2):
                    ready.n += 2
                    added.n += 1
                    pe.wait_ge(ready.sem, ready.value())
                    pe.wait_ge(added.sem, added.value())
                    for w in range(WIN):
                        for k in range(2):
                            ins = nc.tensor.matmul(window(b, w), onehot[:, b, k, w * P:(w + 1) * P],
                                                   rec[k][:, bass.ds(i * 2 + b, 1), :].rearrange("p a f -> p (a f)"), start=(k == 0), stop=(k == 1))
                    summed.mark(ins)
            pe.wait_ge(s["terms_packed"], 1)
            trips = pe.value_load(turns_i[0:1, 0:1], min_val=1, max_val=NTURN)
            vr, vt, vtc, lr, nr, tr, ta, q, qc, z, zc, dm, ma = (Count(s[k]) for k in (
                "v_ready", "vt_ready", "vt_copied", "l_ready", "n_ready", "tx_ready", "tx_added", "q_ready", "q_copied",
                "zy_ready", "zy_copied", "dm_ready", "m_added"))
            with pe.Fori(0, trips) as i:
                for c_, per in ((vr, 2), (vt, 2), (vtc, 2), (lr, 1), (nr, 1), (tr, 7), (ta, 7), (q, 6), (qc, 6),
                                (z, 2 * BU), (zc, 2 * BU), (dm, BU), (ma, BU)):
                    c_.enter(i, per)

                def need(c_, k=1):
                    c_.n += k
                    pe.wait_ge(c_.sem, c_.value())

                need(vr, 2)
                for src, dst in ((V, ps_a), (U, ps_b)):
                    for u in range(BU):
                        for h in range(H2):
                            ins = nc.tensor.transpose(dst[:, u, h, :], src[:, u, h * P:(h + 1) * P], g["ident"][:])
                    vt.mark(ins)
                need(vtc, 2)
                for u in range(BU):
                    for h in range(H2):
                        ins = nc.tensor.matmul(ps_l[:, u, :], UT[:, u, h, :], VT[:, u, h, :], start=(h == 0), stop=(h == 1))
                lr.mark(ins)
                need(ta)
                need(nr)
                for u in range(BU):
                    ins = nc.tensor.transpose(ps_l[:, u, :], TX[:, u, 0, :], g["ident"][:])
                tr.mark(ins)
                for k in range(1, 7):
                    need(ta)
                    for u in range(BU):
                        ins = nc.tensor.matmul(ps_q[:, u, :], NK[:, k, u, :], TX[:, u, 1, :], start=True, stop=True)
                    q.mark(ins)
                    need(qc)
                    for u in range(BU):
                        ins = nc.tensor.matmul(ps_a[:, u, 0, :], QS[:, u, :], TX[:, u, 0, :], start=True, stop=True)
                        if k < 6:
                            ins = nc.tensor.matmul(ps_a[:, u, 1, :], TX[:, u, 0, :], QS[:, u, :], start=True, stop=True)
                    tr.mark(ins)
                pe.wait_ge(s["step"], i * STEPS + (before_loop["step"] + STEPS))
                for u in range(BU):
                    if u:
                        need(ma)
                    for h in range(H2):
                        ins = nc.tensor.matmul(ps_z[:, 0, :], VT[:, u, h, :], M[:, h, :], start=(h == 0), stop=(h == 1))
                    z.mark(ins)
                    need(zc)
                    z.mark(nc.tensor.matmul(ps_z[:, 1, :], TX[:, u, 0, :], ZS[:], start=True, stop=True))
                    need(zc)
                    for h in range(H2):
                        ins = nc.tensor.matmul(ps_m[:, h, :], U[:, u, h * P:(h + 1) * P], YS[:], start=True, stop=True)
                    dm.mark(ins)
                need(ma)
    if dump and upto == 2:
        dump_stage(nc, sem, dump, [M[:], comp[:], g["list0"], g["list1"]])


HEADS, NE0, F0 = 4, 4, 512
NE1, F1 = 8, 1024
CAP = -(-5 * N // (4 * NE1))
SLOTS = -(-CAP // P) * P
TT = 5
NTT = T // TT
SLOPE0, SLOPE1 = 0.2, 0.01
W0, W1R = HEADS * NE0 + HEADS, D + 2


def rest(nc, A, g, sem, sb, pb, out, dump, upto):
    x = g["x"]
    g["xnT"] = sb("x_normed_T", [P, H2, T * P], F32)
    g["mv"] = sb("mean_var", [P, T, 2], F32)
    g["rstd"] = sb("rstd", [P, T], F32)
    g["a_dst"] = sb("a_dst", [P, T, HEADS], F32)
    g["a_src"] = sb("a_src", [P, T, HEADS], F32)
    g["a1"] = sb("a_target1", [P, T, 1], F32)
    tab0 = nc.dram_tensor("node_rows0", (N + 1, W0), F32).ap()
    tab1 = nc.dram_tensor("node_rows1", (N + 1, W1R), F32).ap()
    with ExitStack() as sc:
        def t(name, shape, dt=F32):
            return sb(name, shape, dt, sc)
        MT = t("rotation_T", [P, H2, D])
        transpose_rotation(nc, g, sem, pb, MT)

        def add_to_x(dve, i, k, ps, used):
            used.mark(nc.vector.tensor_tensor(one(x, i, k), one(x, i, k), ps, ALU.add))
        layernorm(nc, g, sem, sb, "n0")
        project(nc, g, sem, sb, pb, "mix", lambda h: MT[:, h, :], D, add_to_x)
    if dump and upto == 3:
        dump_stage(nc, sem, dump, [x[:]])
        return
    with ExitStack() as sc:
        def t(name, shape, dt=F32):
            return sb(name, shape, dt, sc)
        gates = t("gates", [P, T, NE0])
        with ExitStack() as s2:
            def t2(name, shape, dt=F32):
                return sb(name, shape, dt, s2)
            wg = t2("W_gat", [P, H2, 16])
            rows = t2("rows0", [P, T, W0])
            small = t2("att_small", [P, 5, 16])
            prod = t2("att_prod", [P, T, 16])
            load_small(nc, sem, [(wg[:], A["W_gat"].rearrange("(h p) f -> p h f", p=P))] + [
                (small[:, k, :], A[n].rearrange("a b -> (a b)").partition_broadcast(P) if n[:3] == "att" else A[n].partition_broadcast(P))
                for k, n in enumerate(("att_src", "att_dst", "b_gat", "ln_gamma", "ln_beta"))], "att")

            def keep_rows(dve, i, k, ps, used):
                used.mark(move(nc, rows[:, bass.ds(i * TT + k, 1), 0:16].rearrange("p a d -> p (a d)"), ps))
            layernorm(nc, g, sem, sb, "n1")
            project(nc, g, sem, sb, pb, "gat", lambda h: wg[:, h, :], 16, keep_rows, keep_T=g["xnT"])
            acc = t2("acc0", [P, T, HEADS, NE0 + 1])
            attention_scores0(nc, g, sem, rows, small, prod, acc, tab0)
            attend(nc, g, sem, sb, pb, "e0", g["list0"], tab0, g["group_tile0"], NG0, HEADS, W0, 16, SLOPE0, acc)
            route(nc, g, sem, sb, acc, small, gates)
        if dump and upto == 4:
            dump_stage(nc, sem, dump, [gates[:]])
            return
        g["recycle"]()
        experts0(nc, A, g, sem, sb, pb, gates)
    if dump and upto == 5:
        dump_stage(nc, sem, dump, [x[:]])
        return
    with ExitStack() as sc:
        def t(name, shape, dt=F32):
            return sb(name, shape, dt, sc)
        acc = t("acc1", [P, T, D + 1])
        with ExitStack() as s2:
            def t2(name, shape, dt=F32):
                return sb(name, shape, dt, s2)
            wl, bl = t2("W_layer", [P, H2, D]), t2("b_layer", [P, D])
            wa, ba = t2("w_a12", [P, 2, D]), t2("b_a", [P, 2])
            row = t2("rows1", [P, 3 * TT + 1, W1R])
            load_small(nc, sem, [(wl[:], A["W_layer"].rearrange("(h p) f -> p h f", p=P)), (bl[:], A["b_layer"].partition_broadcast(P)),
                                 (wa[:, 0, :], A["w_a1"].rearrange("a b -> (a b)").partition_broadcast(P)),
                                 (wa[:, 1, :], A["w_a2"].rearrange("a b -> (a b)").partition_broadcast(P)),
                                 (ba[:, 0:1], A["b_a1"].partition_broadcast(P)), (ba[:, 1:2], A["b_a2"].partition_broadcast(P))], "layer")
            layernorm(nc, g, sem, sb, "n2")
            g["scope"] = s2
            table1(nc, g, sem, sb, pb, wl, bl, wa, ba, row, acc, tab1)
        attend(nc, g, sem, sb, pb, "e1", g["list1"], tab1, g["group_tile1"], NG1, 1, W1R, D + 1, SLOPE1, acc)
        finish1(nc, g, sem, sb, acc)
    if dump and upto == 6:
        dump_stage(nc, sem, dump, [x[:]])
        return
    g["recycle"]()
    layernorm(nc, g, sem, sb, "n3")
    moe(nc, A, g, sem, sb, pb, out)


def load_small(nc, sem, pairs, tag):
    s = sem(tag + "_weights_loaded")
    with nc.Block() as block:
        @block.sync
        def _(sp):
            for dst, src in pairs:
                sp.dma_start(dst, src).then_inc(s, 16)
            sp.wait_ge(s, 16 * len(pairs))


def transpose_rotation(nc, g, sem, pb, MT):
    s, d = sem("rotation_turned"), sem("rotation_kept")
    with ExitStack() as sc:
        ps = pb("turn_ps", [P, H2, D], sc)
        with nc.Block() as block:
            @block.tensor
            def _(pe):
                for a in range(H2):
                    for b in range(H2):
                        ins = nc.tensor.transpose(ps[:, b, a * P:(a + 1) * P], g["rot"][:, a, b * P:(b + 1) * P], g["ident"][:])
                ins.then_inc(s, 1)

            @block.vector
            def _(dve):
                dve.wait_ge(s, 1)
                nc.vector.tensor_copy(MT[:], ps[:]).then_inc(d, 1)
                dve.wait_ge(d, 1)


def move(nc, dst, src):
    return nc.vector.tensor_scalar(dst, src, 1.0, None, ALU.mult)


def one(a, i, k):
    v = a[:, bass.ds(i * TT + k, 1)]
    return v.rearrange("p a d -> p (a d)") if len(a.shape) == 3 else v


def layernorm(nc, g, sem, sb, tag):
    c_, rooted = sem(tag + "_step"), sem(tag + "_rooted")
    x, mv, rstd = g["x"], g["mv"], g["rstd"]
    with ExitStack() as sc:
        st = sb(tag + "_stats", [P, T, 6], F32, sc)
        with nc.Block() as block:
            @block.vector
            def _(dve):
                c = Count(c_)

                def link(ins):
                    dve.wait_ge(c.sem, c.mark(ins))
                with dve.Fori(0, NTT) as i:
                    c.enter(i, TT)
                    for k in range(TT):
                        c.mark(nc.vector.bn_stats(one(st, i, k), one(x, i, k)))
                    c.leave(NTT)
                dve.wait_ge(c.sem, c.value())
                for k in range(T):
                    c.mark(nc.vector.bn_aggr(mv[:, k, :], st[:, k, :]))
                dve.wait_ge(c.sem, c.value())
                link(nc.vector.tensor_scalar(rstd[:], mv[:, :, 1], EPS, None, ALU.add))
                dve.wait_ge(rooted, 1)
                link(nc.vector.reciprocal(rstd[:], rstd[:]))

            @block.scalar
            def _(act):
                act.wait_ge(c_, 2 * T + 1)
                nc.scalar.sqrt(rstd[:], rstd[:]).then_inc(rooted, 1)


def project(nc, g, sem, sb, pb, tag, weight, width, use, keep_T=None, keep_x=None, per_use=1, rows_out=None, start=None):
    normed, turned, kept, made, used, persisted, step = (
        sem(f"{tag}_{k}") for k in ("normed", "turned", "kept", "made", "used", "persisted", "step"))
    with ExitStack() as sc:
        xs = sb(tag + "_xn", [P, TT, D], F32, sc)
        xt = sb(tag + "_xnT_tile", [P, TT, H2, P], F32, sc)
        pt = pb(tag + "_pt", [P, 2, 512], sc)
        py = pb(tag + "_py", [P, 2, 512], sc)
        with nc.Block() as block:
            if rows_out:
                rows_out(block, used)

            @block.tensor
            def _(pe):
                pe.sem_inc(kept, 1)
                pe.sem_inc(used, 1)
                with pe.Fori(0, NTT) as i:
                    def turn_tile(k):
                        pe.wait_ge(normed, i * TT + (k + 1))
                        if k != 1:
                            pe.wait_ge(kept, i * TT + (max(k - 1, 0) + 1))
                        for h in range(H2):
                            ins = nc.tensor.transpose(pt[:, k % 2, h * P:(h + 1) * P], xs[:, k, h * P:(h + 1) * P], g["ident"][:])
                        ins.then_inc(turned, 1)

                    def multiply_tile(k):
                        pe.wait_ge(kept, i * TT + (k + 2))
                        if k != 1:
                            pe.wait_ge(used, i * (TT * per_use) + (max(k - 1, 0) * per_use + 1))
                        for h in range(H2):
                            ins = nc.tensor.matmul(py[:, k % 2, 0:width], xt[:, k, h, :], weight(h), start=(h == 0), stop=(h == H2 - 1))
                        ins.then_inc(made, 1)

                    turn_tile(0)
                    turn_tile(1)
                    for k in range(TT):
                        multiply_tile(k)
                        if k + 2 < TT:
                            turn_tile(k + 2)

            @block.scalar
            def _(act):
                with act.Fori(0, NTT) as i:
                    for k in range(TT):
                        act.wait_ge(turned, i * TT + (k + 1))
                        nc.scalar.copy(xt[:, k].rearrange("p h c -> p (h c)"), pt[:, k % 2, 0:D]).then_inc(kept, 1)
                        if keep_T is not None:
                            act.wait_ge(kept, i * TT + (k + 2))
                            nc.scalar.copy(keep_T[:, :, bass.ds((i * TT + k) * P, P)], xt[:, k]).then_inc(persisted, 1)
                    if keep_T is not None:
                        act.wait_ge(persisted, i * TT + TT)

            @block.vector
            def _(dve):
                n, m, u, st = (Count(c) for c in (normed, made, used, step))
                if start:
                    start(dve)
                with dve.Fori(0, NTT) as i:
                    for c in (n, m):
                        c.enter(i, TT)
                    u.n = 1
                    u.enter(i, TT * per_use)
                    for k in range(TT):
                        args = (one(g["x"], i, k), g["mv"][:, bass.ds(i * TT + k, 1), 0], one(g["rstd"], i, k), ALU.subtract, ALU.mult)
                        n.mark(nc.vector.tensor_scalar(xs[:, k, :], *args))
                        if keep_x is not None:
                            nc.vector.tensor_scalar(one(keep_x, i, k), *args).then_inc(step, 1)
                    if keep_x is not None:
                        dve.wait_ge(step, i * TT + TT)
                    for k in range(TT):
                        m.n += 1
                        dve.wait_ge(m.sem, m.value())
                        use(dve, i, k, py[:, k % 2, 0:width], u)
                    dve.wait_ge(u.sem, u.value())


def gather_columns(a, n):
    return a


def attention_scores0(nc, g, sem, rows, small, prod, acc, tab0):
    c_, out_ = sem("scores0_step"), sem("rows0_written")
    with nc.Block() as block:
        @block.vector
        def _(dve):
            c = Count(c_)

            def link(ins):
                dve.wait_ge(c.sem, c.mark(ins))
            h = rows[:, :, 0:16]
            for k, dst in enumerate((g["a_src"], g["a_dst"])):
                link(nc.vector.tensor_tensor(prod[:], h, small[:, k, :].unsqueeze(1).broadcast_to([P, T, 16]), ALU.mult))
                link(nc.vector.tensor_reduce(dst[:], prod[:].rearrange("p t (h e) -> p t h e", e=NE0), X, ALU.add))
            link(nc.vector.tensor_copy(rows[:, :, 16:20], g["a_src"][:]))
            link(nc.vector.tensor_copy(acc[:, :, :, 0:NE0], h.rearrange("p t (h e) -> p t h e", e=NE0)))
            link(nc.vector.memset(acc[:, :, :, NE0:NE0 + 1], 1.0))
            nc.vector.memset(prod[:], 0.0).then_inc(c_, 1)

        @block.sync
        def _(sp):
            sp.wait_ge(c_, 8)
            sp.dma_start(tab0[0:NFULL * P, :].rearrange("(t p) d -> p t d", p=P), rows[:, 0:NFULL, :]).then_inc(out_, 16)
            sp.dma_start(tab0[NFULL * P:N, :], rows[0:NREST, NFULL, :]).then_inc(out_, 16)
            sp.dma_start(tab0[N:N + 1, :], prod[0:1, 0:2, :].rearrange("p a b -> p (a b)")[:, 0:W0]).then_inc(out_, 16)
            sp.wait_ge(out_, 48)


def attend(nc, g, sem, sb, pb, tag, edges, table, group_tile, NG, HN, W, acol, slope, acc):
    names = ("list_loaded", "index_staged", "index_ok", "rows_in_a", "rows_in_b", "rows_used", "onehot_ready", "step",
             "scores_ready", "target_ready", "target_in", "factor_in", "factor_out", "weight_in", "weight_out",
             "message_ready", "sum_ready", "sum_added", "started")
    s = {k: sem(f"{tag}_{k}") for k in names}
    AW = NE0 + 1 if HN > 1 else D + 1
    NM = HN * AW
    NB = NG * G
    with ExitStack() as sc:
        def t(name, shape, dt=F32):
            return sb(f"{tag}_{name}", shape, dt, sc)
        ed = t("edges", [P, NB, 2])
        idx = t("index", [P, 2, G], I32)
        rows = t("rows", [P, 2, G, W])
        E = t("onehot", [P, 2, G, P])
        NEG = t("not_target", [P, 2, G, P], BF16)
        ET = t("onehot_T", [P, G, P])
        EW = t("onehot_weighted", [P, G, P])
        mg, mn, fd, fac = (t(n, [P, HN]) for n in ("group_max", "new_max", "max_change", "factor"))
        tm = t("target_and_max", [P, 2, HN])
        v, v2, w = (t(n, [P, G, HN]) for n in ("score", "score2", "weight"))
        msg = t("message", [P, G, HN, NE0 + 1])
        top, act_top = t("top", [P, T, HN]), t("top_act", [P, T, HN])
        tmp = t("scaled", [P, HN, AW if HN > 1 else 1])
        ps = pb(tag + "_scores", [P, G, HN, P], sc)
        pe8_bank = pb(tag + "_at_edge", [P, 512], sc)
        pe8 = pe8_bank[:, 0:G * 2 * HN].rearrange("p (g h) -> p g h", g=G)
        psum_ = pb(tag + "_sum", [P, 512], sc)
        a_dst = g["a_dst"]
        with nc.Block() as block:
            @block.sync
            def _(sp):
                sp.dma_start(ed[:], edges.rearrange("(p b) k -> p b k", p=P)).then_inc(s["list_loaded"], 16)
                sp.wait_ge(s["list_loaded"], 16)

            @block.gpsimd
            def _(pool):
                pool.wait_ge(s["list_loaded"], 16)
                pool.sem_inc(s["rows_used"], 2)
                st = Count(s["index_staged"])
                with pool.Fori(0, NG // 2) as i:
                    st.enter(i, 2)
                    for b in range(2):
                        pool.wait_ge(s["rows_used"], i * 2 + b + 1)
                        pool.sem_inc(s["index_ok"], 1)
                        vv = st.mark(nc.gpsimd.tensor_copy(idx[:, b, :], ed[:, bass.ds((i * 2 + b) * G, G), 0].bitcast(I32)))
                        pool.wait_ge(st.sem, vv)
                        pool.sem_inc(s["index_ok"], 1)
                        for k in range(G):
                            nc.gpsimd.indirect_dma_start(rows[:, b, k, :], None, table[:, :],
                                                         bass.IndirectOffsetOnAxis(ap=idx[:, b, k:k + 1], axis=0)).then_inc(s[f"rows_in_{'ab'[b]}"], 16)

            @block.scalar
            def _(act):
                with act.Fori(0, NG // 2) as i:
                    for b in range(2):
                        act.wait_ge(s["factor_in"], i * 2 + b + 1)
                        nc.scalar.activation(fac[:], fd[:], ACT.Exp).then_inc(s["factor_out"], 1)
                        act.wait_ge(s["weight_in"], i * 2 + b + 1)
                        nc.scalar.activation(w[:], v[:], ACT.Exp).then_inc(s["weight_out"], 1)

            @block.vector
            def _(dve):
                c = Count(s["step"])

                def link(ins):
                    dve.wait_ge(c.sem, c.mark(ins))
                if HN > 1:
                    link(nc.vector.tensor_copy(top[:], g["a_src"][:]))
                    link(nc.vector.tensor_tensor(act_top[:], top[:], a_dst[:], ALU.add))
                else:
                    link(nc.vector.memset(top[:], -BIG))
                    link(nc.vector.memset(act_top[:], -BIG))
                    link(nc.vector.memset(acc[:], 0.0))
                link(nc.vector.scalar_tensor_tensor(act_top[:], act_top[:], slope, act_top[:], ALU.mult, ALU.max))
                dve.wait_ge(s["list_loaded"], 16)

                with dve.Fori(0, NG // 2) as i:
                    per_group = 18 if HN > 1 else 16
                    c.enter(i, 2 * per_group)
                    for b in range(2):
                        grp = i * 2 + b
                        tile = dve.value_load(group_tile[0:1, bass.ds(grp, 1)], min_val=0, max_val=T - 1)
                        at = lambda a: a[:, bass.ds(tile, 1)].rearrange("p a h -> p (a h)")
                        dl = ed[:, bass.ds(grp * G, G), 1].unsqueeze(2).broadcast_to([P, G, P])
                        link(nc.vector.tensor_tensor(E[:, b], g["iota"][:, 0:P].unsqueeze(1).broadcast_to([P, G, P]), dl, ALU.is_equal))
                        link(nc.vector.tensor_scalar(NEG[:, b], E[:, b], BIG, -BIG, ALU.mult, ALU.add))
                        dve.sem_inc(s["onehot_ready"], 1)
                        dve.wait_ge(s["scores_ready"], grp + 1)
                        link(nc.vector.tensor_reduce(mg[:], ps[:].rearrange("p g h e -> p h g e"), XY, ALU.max))
                        link(nc.vector.tensor_scalar(ET[:], ps[:, :, 0, :], -BIG / 2, None, ALU.is_gt))
                        link(nc.vector.tensor_tensor(mg[:], mg[:], at(top), ALU.max))
                        link(move(nc, at(top), mg[:]))
                        link(move(nc, tm[:, 0, :], at(a_dst)[:, 0:HN] if HN > 1 else at(g["a1"])))
                        link(nc.vector.tensor_tensor(mn[:], mg[:], tm[:, 0, :], ALU.add))
                        link(nc.vector.scalar_tensor_tensor(tm[:, 1, :], mn[:], slope, mn[:], ALU.mult, ALU.max))
                        dve.sem_inc(s["target_ready"], 1)
                        link(nc.vector.tensor_tensor(fd[:], at(act_top), tm[:, 1, :], ALU.subtract))
                        dve.sem_inc(s["factor_in"], 1)
                        link(move(nc, at(act_top), tm[:, 1, :]))
                        dve.wait_ge(s["target_in"], grp + 1)
                        link(nc.vector.tensor_tensor(v2[:], rows[:, b, :, acol:acol + HN], pe8[:, :, 0:HN], ALU.add))
                        link(nc.vector.scalar_tensor_tensor(v2[:], v2[:], slope, v2[:], ALU.mult, ALU.max))
                        link(nc.vector.tensor_tensor(v[:], v2[:], pe8[:, :, HN:2 * HN], ALU.subtract))
                        dve.sem_inc(s["weight_in"], 1)
                        dve.wait_ge(s["weight_out"], grp + 1)
                        if HN > 1:
                            link(nc.vector.tensor_tensor(msg[:, :, :, 0:NE0], rows[:, b, :, 0:HN * NE0].rearrange("p g (h e) -> p g h e", e=NE0),
                                                         w[:].unsqueeze(3).broadcast_to([P, G, HN, NE0]), ALU.mult))
                            link(nc.vector.tensor_copy(msg[:, :, :, NE0], w[:]))
                        else:
                            link(nc.vector.tensor_tensor(EW[:], E[:, b], w[:].broadcast_to([P, G, P]), ALU.mult))
                        dve.sem_inc(s["message_ready"], 1)
                        dve.wait_ge(s["factor_out"], grp + 1)
                        if HN > 1:
                            a4 = acc[:, bass.ds(tile, 1)].rearrange("p a h e -> p (a h) e")
                            link(nc.vector.tensor_tensor(tmp[:], a4, fac[:].unsqueeze(2).broadcast_to([P, HN, AW]), ALU.mult))
                            dve.wait_ge(s["sum_ready"], grp + 1)
                            link(nc.vector.tensor_tensor(a4, tmp[:], psum_[:, 0:NM].rearrange("p (h e) -> p h e", e=AW), ALU.add))
                        else:
                            dve.wait_ge(s["sum_ready"], grp + 1)
                            link(nc.vector.scalar_tensor_tensor(at(acc), at(acc), fac[:], psum_[:, 0:NM], ALU.mult, ALU.add))
                        dve.sem_inc(s["rows_used"], 1)
                    assert c.n - c.start == 2 * per_group, c.n - c.start

            @block.tensor
            def _(pe):
                with pe.Fori(0, NG // 2) as i:
                    for b in range(2):
                        grp = i * 2 + b
                        pe.wait_ge(s["onehot_ready"], grp + 1)
                        pe.wait_ge(s[f"rows_in_{'ab'[b]}"], i * (16 * G) + 16 * G)
                        for k in range(G):
                            for h in range(HN):
                                nc.tensor.matmul(ps[:, k, h, :], rows[:, b, k, acol + h:acol + h + 1].broadcast_to([P, P]), g["ident"][:], start=True, stop=False)
                                ins = nc.tensor.matmul(ps[:, k, h, :], NEG[:, b, k, :], g["identb"][:], start=False, stop=True)
                        ins.then_inc(s["scores_ready"], 1)
                        pe.wait_ge(s["target_ready"], grp + 1)
                        for k in range(G):
                            ins = nc.tensor.matmul(pe8[:, k, :], ET[:, k, :], tm[:].rearrange("p a h -> p (a h)"), start=True, stop=True)
                        ins.then_inc(s["target_in"], 1)
                        pe.wait_ge(s["message_ready"], grp + 1)
                        for k in range(G):
                            ins = nc.tensor.matmul(psum_[:, 0:NM], E[:, b, k, :] if HN > 1 else EW[:, k, :],
                                                   msg[:, k].rearrange("p h e -> p (h e)") if HN > 1 else rows[:, b, k, 0:NM], start=(k == 0), stop=(k == G - 1))
                        ins.then_inc(s["sum_ready"], 1)


def route(nc, g, sem, sb, acc, small, gates):
    c_, a_ = sem("route_step"), sem("route_act")
    with ExitStack() as sc:
        def t(name, shape):
            return sb("route_" + name, shape, F32, sc)
        agg, inv, m, sq = t("agg", [P, T, 16]), t("inv", [P, T, HEADS]), t("mean", [P, T]), t("sq", [P, T, 16])
        sco, cnt, cmp_, top, e = t("score", [P, T, NE0]), t("above", [P, T, NE0]), t("cmp", [P, T]), t("top", [P, T]), t("exp", [P, T, NE0])
        with nc.Block() as block:
            @block.vector
            def _(dve):
                c = Count(c_)

                def link(ins):
                    dve.wait_ge(c.sem, c.mark(ins))
                bc = lambda a, n: a.unsqueeze(2).broadcast_to([P, T, n])
                row = lambda k: small[:, k, :].unsqueeze(1).broadcast_to([P, T, 16])
                link(nc.vector.tensor_scalar(inv[:], acc[:, :, :, NE0], 1e-16, None, ALU.add))
                link(nc.vector.reciprocal(inv[:], inv[:]))
                link(nc.vector.tensor_tensor(agg[:].rearrange("p t (h e) -> p t h e", e=NE0), acc[:, :, :, 0:NE0],
                                             inv[:].unsqueeze(3).broadcast_to([P, T, HEADS, NE0]), ALU.mult))
                link(nc.vector.tensor_tensor(agg[:], agg[:], row(2), ALU.add))
                link(nc.vector.tensor_reduce(m[:], agg[:], X, ALU.add))
                link(nc.vector.tensor_scalar(m[:], m[:], 1.0 / 16, None, ALU.mult))
                link(nc.vector.tensor_tensor(agg[:], agg[:], bc(m[:], 16), ALU.subtract))
                link(nc.vector.tensor_tensor(sq[:], agg[:], agg[:], ALU.mult))
                link(nc.vector.tensor_reduce(m[:], sq[:], X, ALU.add))
                link(nc.vector.tensor_scalar(m[:], m[:], 1.0 / 16, EPS, ALU.mult, ALU.add))
                dve.sem_inc(a_, 1)
                dve.wait_ge(a_, 2)
                link(nc.vector.reciprocal(m[:], m[:]))
                link(nc.vector.tensor_tensor(agg[:], agg[:], bc(m[:], 16), ALU.mult))
                link(nc.vector.tensor_tensor(agg[:], agg[:], row(3), ALU.mult))
                link(nc.vector.tensor_tensor(agg[:], agg[:], row(4), ALU.add))
                link(nc.vector.tensor_reduce(sco[:], agg[:].rearrange("p t (h e) -> p t e h", e=NE0), X, ALU.add))
                link(nc.vector.tensor_scalar(sco[:], sco[:], 1.0 / HEADS, None, ALU.mult))
                link(nc.vector.tensor_reduce(top[:], sco[:], X, ALU.max))
                link(nc.vector.tensor_tensor(e[:], sco[:], bc(top[:], NE0), ALU.subtract))
                dve.sem_inc(a_, 1)
                link(nc.vector.memset(cnt[:], 0.0))
                for a in range(NE0):
                    for b in range(NE0):
                        if a != b:
                            link(nc.vector.tensor_tensor(cmp_[:], sco[:, :, b], sco[:, :, a], ALU.is_ge if b < a else ALU.is_gt))
                            link(nc.vector.tensor_tensor(cnt[:, :, a], cnt[:, :, a], cmp_[:], ALU.add))
                dve.wait_ge(a_, 4)
                link(nc.vector.scalar_tensor_tensor(e[:], cnt[:], 2.0, e[:], ALU.is_lt, ALU.mult))
                link(nc.vector.tensor_reduce(m[:], e[:], X, ALU.add))
                link(nc.vector.reciprocal(m[:], m[:]))
                link(nc.vector.tensor_tensor(gates[:], e[:], bc(m[:], NE0), ALU.mult))

            @block.scalar
            def _(act):
                act.wait_ge(a_, 1)
                nc.scalar.sqrt(m[:], m[:]).then_inc(a_, 1)
                act.wait_ge(a_, 3)
                nc.scalar.activation(e[:], e[:], ACT.Exp).then_inc(a_, 1)


def experts0(nc, A, g, sem, sb, pb, gates):
    s = {k: sem("ex0_" + k) for k in ("loaded", "up_ready", "hidden_ready", "down_ready", "added")}
    FT, HALF = F0 // P, TT * P // 2
    with ExitStack() as sc:
        def t(name, shape, dt=F32):
            return sb("ex0_" + name, shape, dt, sc)
        W1, W2 = t("W1", [P, NE0, H2, F0]), t("W2", [P, NE0, FT, D])
        b1, b2 = t("b1", [P, NE0 * FT]), t("b2", [1, NE0, D])
        hid = t("hidden", [P, 2, FT, TT * P])
        up = pb("ex0_up", [P, 2, 2, 512], sc)
        dn = pb("ex0_down", [P, 2, 512], sc)
        with nc.Block() as block:
            @block.sync
            def _(sp):
                for e in range(NE0):
                    sp.dma_start(W1[:, e], A["W1"][e].rearrange("(h p) f -> p h f", p=P)).then_inc(s["loaded"], 16)
                    sp.dma_start(W2[:, e], A["W2"][e].rearrange("(f p) d -> p f d", p=P)).then_inc(s["loaded"], 16)
                sp.dma_start(b1[:], A["b1"]).then_inc(s["loaded"], 16)
                sp.dma_start(b2[:], A["b2"].rearrange("(a e) d -> a e d", a=1)).then_inc(s["loaded"], 16)
                sp.wait_ge(s["loaded"], 16 * (2 * NE0 + 2))

            @block.tensor
            def _(pe):
                U, Hd, Dn, Ad = (Count(s[k]) for k in ("up_ready", "hidden_ready", "down_ready", "added"))
                pe.wait_ge(s["loaded"], 16 * (2 * NE0 + 2))
                nu, nd = NE0 * FT, NE0 * TT
                with pe.Fori(0, NTT) as i:
                    def up_(e):
                        for f in range(FT):
                            pe.wait_ge(Hd.sem, i * nu + (e * FT + f + 1))
                            for n in range(2):
                                for h in range(H2):
                                    ins = nc.tensor.matmul(up[:, f % 2, n, 0:HALF], W1[:, e, h, f * P:(f + 1) * P],
                                                           g["xnT"][:, h, bass.ds(i * (TT * P) + n * HALF, HALF)], start=(h == 0), stop=(h == 1))
                            ins.then_inc(U.sem, 1)

                    def down_(e):
                        pe.wait_ge(Hd.sem, i * nu + ((e + 1) * FT + 2))
                        for k in range(TT):
                            n = e * TT + k
                            pe.wait_ge(Ad.sem, i * nd + n + 1)
                            for f in range(FT):
                                nc.tensor.matmul(dn[:, n % 2, 0:D], hid[:, e % 2, f, k * P:(k + 1) * P], W2[:, e, f, :], start=(f == 0), stop=False)
                            nc.tensor.matmul(dn[:, n % 2, 0:D], g["ones"][0:1, :], b2[:, e, :], start=False, stop=True).then_inc(Dn.sem, 1)

                    up_(0)
                    for e in range(NE0):
                        if e + 1 < NE0:
                            up_(e + 1)
                        down_(e)

            @block.scalar
            def _(act):
                act.sem_inc(s["hidden_ready"], 2)
                act.wait_ge(s["loaded"], 16 * (2 * NE0 + 2))
                nu, nd = NE0 * FT, NE0 * TT
                act.sem_inc(s["down_ready"], TT)
                with act.Fori(0, NTT) as i:
                    for e in range(NE0):
                        act.wait_ge(s["down_ready"], i * nd + (e - 1) * TT + TT if e else i * nd + 0 + 1)
                        for f in range(FT):
                            act.wait_ge(s["up_ready"], i * nu + (e * FT + f + 1))
                            nc.scalar.activation(hid[:, e % 2, f, :].rearrange("p (n c) -> p n c", n=2), up[:, f % 2, :, 0:HALF],
                                                 ACT.Gelu, bias=b1[:, e * FT + f:e * FT + f + 1]).then_inc(s["hidden_ready"], 1)

            @block.vector
            def _(dve):
                dve.sem_inc(s["added"], 2)
                nd = NE0 * TT
                with dve.Fori(0, NTT) as i:
                    for e in range(NE0):
                        for k in range(TT):
                            n = e * TT + k
                            dve.wait_ge(s["down_ready"], i * nd + n + 1 + TT)
                            if e:
                                dve.wait_ge(s["added"], i * nd + n + 1 + 2 - TT)
                            tile = one(g["x"], i, k)
                            nc.vector.scalar_tensor_tensor(tile, dn[:, n % 2, 0:D], gates[:, bass.ds(i * TT + k, 1), e], tile,
                                                           ALU.mult, ALU.add).then_inc(s["added"], 1)
                dve.wait_ge(s["added"], NTT * nd + 2)


def table1(nc, g, sem, sb, pb, wl, bl, wa, ba, row, acc, tab1):
    out_, ready, zr = sem("rows1_out"), sem("rows1_ready"), sem("rows1_zero_ready")
    rows_s = sem("rows1_step")
    target = sb("rows1_target", [P, TT], F32, g["scope"])
    junk = row[:, TT:2 * TT, 0:D]

    def start(dve):
        nc.vector.memset(row[0:1, 2 * TT, :], 0.0).then_inc(zr, 1)
        nc.vector.memset(row[:, 0:TT, D:D + 1], 1.0).then_inc(zr, 1)
        dve.wait_ge(zr, 2)

    def use(dve, i, k, ps, used):
        if k == 0:
            dve.wait_ge(out_, i * (16 * TT) + 16)
        r = row[:, k, :]
        v = used.mark(nc.vector.tensor_tensor(r[:, 0:D], ps, bl[:], ALU.add))
        dve.wait_ge(used.sem, v)
        used.mark(nc.vector.tensor_tensor_reduce(junk[:, k, :], r[:, 0:D], wa[:, 1, :], 1.0, ba[:, 1:2], ALU.mult, ALU.add, r[:, D + 1:D + 2]))
        v = used.mark(nc.vector.tensor_tensor_reduce(row[:, 2 * TT + 1 + k, 0:D], r[:, 0:D], wa[:, 0, :], 1.0, ba[:, 0:1], ALU.mult, ALU.add,
                                                     target[:, k:k + 1]))
        if k == TT - 1:
            dve.wait_ge(used.sem, v)
            dve.sem_inc(ready, 1)
            move(nc, g["a1"][:, bass.ds(i * TT, TT), :].rearrange("p t a -> p (t a)"), target[:]).then_inc(rows_s, 1)
            dve.wait_ge(rows_s, i + 1)

    def rows_out(block, used):
        @block.sync
        def _(sp):
            sp.wait_ge(zr, 2)
            sp.dma_start(tab1[N:N + 1, :], row[0:1, 2 * TT, :]).then_inc(out_, 16)
            whole = NFULL // TT
            with sp.Fori(0, whole) as i:
                sp.wait_ge(ready, i + 1)
                for k in range(TT):
                    sp.dma_start(tab1[bass.ds((i * TT + k) * P, P), :], row[:, k, :]).then_inc(out_, 16)
            for i in range(whole, NTT):
                sp.wait_ge(ready, i + 1)
                for k in range(TT):
                    n0 = (i * TT + k) * P
                    n = min(P, N - n0)
                    sp.dma_start(tab1[n0:n0 + n, :], row[0:n, k, :]).then_inc(out_, 16)
            sp.wait_ge(out_, 16 * (T + 1))

    project(nc, g, sem, sb, pb, "layer", lambda h: wl[:, h, :], D, use, per_use=3, rows_out=rows_out, start=start)


def finish1(nc, g, sem, sb, acc):
    c_ = sem("finish1_step")
    with ExitStack() as sc:
        inv = sb("finish1_inv", [P, T], F32, sc)
        with nc.Block() as block:
            @block.vector
            def _(dve):
                c = Count(c_)

                def link(ins):
                    dve.wait_ge(c.sem, c.mark(ins))
                link(nc.vector.tensor_scalar(inv[:], acc[:, :, D], 1e-30, None, ALU.max))
                link(nc.vector.reciprocal(inv[:], inv[:]))
                with dve.Fori(0, NTT) as i:
                    for k in range(TT):
                        nc.vector.scalar_tensor_tensor(one(g["x"], i, k), one(acc, i, k)[:, 0:D], one(inv, i, k), one(g["x"], i, k),
                                                       ALU.mult, ALU.add).then_inc(c_, 1)
                dve.wait_ge(c_, 2 + T)


def moe(nc, A, g, sem, sb, pb, out):
    x, buf, ybuf = g["x"], nc.dram_tensor("expert_in", (NE1 * SLOTS, D), F32).ap(), nc.dram_tensor("expert_out", (NE1 * SLOTS, D), F32).ap()
    OUT = NE1 * SLOTS
    with ExitStack() as sc:
        def t(name, shape, dt=F32, where=sc):
            return sb("moe_" + name, shape, dt, where)
        slot, prob = t("slot", [P, T], I32), t("prob", [P, T])
        with ExitStack() as s2:
            xn = t("xn", [P, T, D], F32, s2)
            gw, gb = t("gate_w", [P, H2, NE1], F32, s2), t("gate_b", [P, NE1], F32, s2)
            lg = t("logits", [P, T, NE1], F32, s2)
            load_small(nc, sem, [(gw[:], A["gate_w"].rearrange("(h p) f -> p h f", p=P)), (gb[:], A["gate_b"].partition_broadcast(P))], "gate")

            def keep(dve, i, k, ps, used):
                used.mark(nc.vector.tensor_tensor(one(lg, i, k), ps, gb[:], ALU.add))
            project(nc, g, sem, sb, pb, "gate", lambda h: gw[:, h, :], NE1, keep, keep_x=xn)
            dispatch(nc, g, sem, sb, pb, lg, slot, prob, xn, buf, OUT)
        experts1(nc, A, g, sem, sb, pb, buf, ybuf)
        collect(nc, g, sem, sb, slot, prob, ybuf, OUT, out)


def dispatch(nc, g, sem, sb, pb, lg, slot, prob, xn, buf, OUT):
    c_, exp_in, exp_out, oh_ready, pre_ready, zeroed, cleared, slots, sent = (sem("dispatch_" + k) for k in (
        "step", "exp_in", "exp_out", "onehot_ready", "prefix_ready", "zero_ready", "cleared", "slots_ready", "sent"))
    with ExitStack() as sc:
        def t(name, shape, dt=F32):
            return sb("dispatch_" + name, shape, dt, sc)
        top, e, oh, taken, hit = t("top", [P, T]), t("exp", [P, T, NE1]), t("onehot", [P, T, NE1]), t("taken", [P, T]), t("hit", [P, T])
        pre, tot, inc, sl, base = t("prefix", [P, T, NE1]), t("totals", [P, T, NE1]), t("scan", [P, NE1, T]), t("slot_f", [P, T]), t("base", [P, NE1])
        sm, upto_ = t("sum", [P, T]), t("row_upto_column", [P, P])
        zero = t("zero", [P, 4 * D])
        ps = pb("dispatch_ps", [P, 2, 512], sc)
        bc = lambda a: a.unsqueeze(2).broadcast_to([P, T, NE1])
        with nc.Block() as block:
            @block.vector
            def _(dve):
                c = Count(c_)

                def link(ins):
                    dve.wait_ge(c.sem, c.mark(ins))
                nc.vector.memset(zero[:], 0.0).then_inc(zeroed, 1)
                link(nc.vector.tensor_scalar(upto_[:], g["iota"][:, 0:P], g["pidx"][:], None, ALU.is_ge))
                link(nc.vector.tensor_reduce(top[:], lg[:], X, ALU.max))
                link(nc.vector.tensor_tensor(e[:], lg[:], bc(top[:]), ALU.subtract))
                dve.sem_inc(exp_in, 1)
                dve.wait_ge(exp_out, 1)
                link(nc.vector.tensor_reduce(sm[:], e[:], X, ALU.add))
                link(nc.vector.reciprocal(sm[:], sm[:]))
                link(nc.vector.tensor_tensor(e[:], e[:], bc(sm[:]), ALU.mult))
                link(nc.vector.tensor_reduce(prob[:], e[:], X, ALU.max))
                link(nc.vector.memset(taken[:], 0.0))
                link(nc.vector.tensor_scalar(taken[:, T - 1:T], g["pidx"][:], float(NREST), None, ALU.is_ge))
                for k in range(NE1):
                    link(nc.vector.tensor_tensor(hit[:], e[:, :, k], prob[:], ALU.is_ge))
                    link(nc.vector.tensor_tensor(oh[:, :, k], hit[:], taken[:], ALU.is_gt))
                    link(nc.vector.tensor_tensor(taken[:], taken[:], oh[:, :, k], ALU.add))
                dve.sem_inc(oh_ready, 1)
                dve.wait_ge(pre_ready, 1)
                flat = lambda a: a[:].rearrange("p t e -> p (t e)")
                link(nc.vector.tensor_copy(flat(pre), ps[:, 0, 0:T * NE1]))
                link(nc.vector.tensor_copy(flat(tot), ps[:, 1, 0:T * NE1]))
                for k in range(NE1):
                    link(nc.vector.tensor_tensor_scan(inc[:, k, :], g["ones"][:, 0:T], tot[:, :, k], 0.0, ALU.mult, ALU.add))
                link(nc.vector.tensor_tensor(pre[:], pre[:], inc[:].rearrange("p e t -> p t e"), ALU.add))
                link(nc.vector.tensor_tensor(pre[:], pre[:], tot[:], ALU.subtract))
                link(nc.vector.tensor_tensor(pre[:], pre[:], oh[:], ALU.mult))
                link(nc.vector.tensor_reduce(sl[:], pre[:], X, ALU.add))
                link(nc.vector.tensor_scalar(base[:], g["iota"][:, 0:NE1], float(SLOTS), None, ALU.mult))
                link(nc.vector.tensor_tensor(e[:], oh[:], base[:].unsqueeze(1).broadcast_to([P, T, NE1]), ALU.mult))
                link(nc.vector.tensor_reduce(sm[:], e[:], X, ALU.add))
                link(nc.vector.tensor_tensor(sm[:], sm[:], sl[:], ALU.add))
                link(nc.vector.tensor_scalar(sm[:], sm[:], -1.0 - OUT, None, ALU.add))
                link(nc.vector.tensor_scalar(hit[:], sl[:], float(CAP), None, ALU.is_le))
                link(nc.vector.scalar_tensor_tensor(hit[:], sl[:], 0.0, hit[:], ALU.is_gt, ALU.mult))
                link(nc.vector.tensor_tensor(sm[:], sm[:], hit[:], ALU.mult))
                link(nc.vector.tensor_scalar(sm[:], sm[:], float(OUT), None, ALU.add))
                link(nc.vector.tensor_copy(slot[:], sm[:]))
                link(nc.vector.tensor_tensor(prob[:], prob[:], hit[:], ALU.mult))
                dve.sem_inc(slots, 1)

            @block.scalar
            def _(act):
                act.wait_ge(exp_in, 1)
                nc.scalar.activation(e[:], e[:], ACT.Exp).then_inc(exp_out, 1)

            @block.tensor
            def _(pe):
                pe.wait_ge(oh_ready, 1)
                flat = oh[:].rearrange("p t e -> p (t e)")
                nc.tensor.matmul(ps[:, 0, 0:T * NE1], upto_[:], flat, start=True, stop=True)
                nc.tensor.matmul(ps[:, 1, 0:T * NE1], g["ones"][:], flat, start=True, stop=True).then_inc(pre_ready, 1)

            @block.sync
            def _(sp):
                sp.wait_ge(zeroed, 1)
                for k in range(OUT // (4 * P)):
                    sp.dma_start(buf[k * 4 * P:(k + 1) * 4 * P, :].rearrange("(p a) d -> p (a d)", p=P), zero[:]).then_inc(cleared, 16)
                sp.wait_ge(cleared, 16 * (OUT // (4 * P)))

            @block.gpsimd
            def _(pool):
                pool.wait_ge(slots, 1)
                pool.wait_ge(cleared, 16 * (OUT // (4 * P)))
                for k in range(T):
                    nc.gpsimd.indirect_dma_start(buf[:, :], bass.IndirectOffsetOnAxis(ap=slot[:, k:k + 1], axis=0), xn[:, k, :], None,
                                                 bounds_check=OUT - 1, oob_is_err=False).then_inc(sent, 16)
                pool.wait_ge(sent, 16 * T)


def experts1(nc, A, g, sem, sb, pb, buf, ybuf):
    s = {k: sem("ex1_" + k) for k in ("in_a", "in_b", "bias_in", "turned", "turned_kept", "up_ready", "hidden_ready", "down_ready",
                                      "added", "out_a", "out_b", "w_free", "y_free")}
    KS, FT = SLOTS // P, F1 // P
    with ExitStack() as sc:
        def t(name, shape, dt=F32):
            return sb("ex1_" + name, shape, dt, sc)
        w1, w2 = t("w1", [P, 2, H2, F1]), t("w2", [P, 2, FT, D])
        xe, xT = t("x", [P, 2, KS, D]), t("xT", [P, H2, SLOTS])
        b1, b2 = t("b1", [P, NE1 * FT]), t("b2", [P, NE1, D])
        hid = t("hidden", [P, FT, SLOTS])
        y = t("y", [P, 2, KS, D])
        pt = pb("ex1_turn", [P, 2, 512], sc)
        up = pb("ex1_up", [P, 2, 512], sc)
        dn = pb("ex1_down", [P, 2, 512], sc)
        LOADS = 16 * 3
        with nc.Block() as block:
            @block.sync
            def _(sp):
                sp.dma_start(b1[:], A["b1m"]).then_inc(s["bias_in"], 16)
                sp.dma_start(b2[:], A["b2m"].partition_broadcast(P)).then_inc(s["bias_in"], 16)
                sp.sem_inc(s["w_free"], 2)
                for e in range(NE1):
                    b = e % 2
                    sp.wait_ge(s["w_free"], e + 1)
                    sp.dma_start(xe[:, b], buf[e * SLOTS:(e + 1) * SLOTS, :].rearrange("(k p) d -> p k d", p=P)).then_inc(s[f"in_{'ab'[b]}"], 16)
                    sp.dma_start(w1[:, b], A["w1"][e].rearrange("(h p) f -> p h f", p=P)).then_inc(s[f"in_{'ab'[b]}"], 16)
                    sp.dma_start(w2[:, b], A["w2"][e].rearrange("(f p) d -> p f d", p=P)).then_inc(s[f"in_{'ab'[b]}"], 16)

            @block.gpsimd
            def _(pool):
                for e in range(NE1):
                    pool.wait_ge(s["y_free"], e + 1)
                    pool.dma_start(ybuf[e * SLOTS:(e + 1) * SLOTS, :].rearrange("(k p) d -> p k d", p=P), y[:, e % 2]).then_inc(s[f"out_{'ab'[e % 2]}"], 16)
                for b in "ab":
                    pool.wait_ge(s["out_" + b], 16 * (NE1 // 2))

            @block.tensor
            def _(pe):
                pe.wait_ge(s["bias_in"], 32)
                for e in range(NE1):
                    b = e % 2
                    pe.wait_ge(s[f"in_{'ab'[b]}"], LOADS * (e // 2 + 1))
                    for h in range(H2):
                        if e:
                            pe.wait_ge(s["turned_kept"], H2 * e)
                        for k in range(KS):
                            ins = nc.tensor.transpose(pt[:, h, k * P:(k + 1) * P], xe[:, b, k, h * P:(h + 1) * P], g["ident"][:])
                        ins.then_inc(s["turned"], 1)
                    pe.wait_ge(s["turned_kept"], H2 * (e + 1))
                    for f in range(FT):
                        n = e * FT + f
                        if n >= 2:
                            pe.wait_ge(s["hidden_ready"], n - 1)
                        for h in range(H2):
                            ins = nc.tensor.matmul(up[:, f % 2, :], w1[:, b, h, f * P:(f + 1) * P], xT[:, h, :], start=(h == 0), stop=(h == 1))
                        ins.then_inc(s["up_ready"], 1)
                    pe.wait_ge(s["hidden_ready"], (e + 1) * FT)
                    for k in range(KS):
                        n = e * KS + k
                        if n >= 2:
                            pe.wait_ge(s["added"], n - 1)
                        for f in range(FT):
                            ins = nc.tensor.matmul(dn[:, k % 2, 0:D], hid[:, f, k * P:(k + 1) * P], w2[:, b, f, :], start=(f == 0), stop=(f == FT - 1))
                        ins.then_inc(s["down_ready"], 1)
                    pe.wait_ge(s["down_ready"], (e + 1) * KS)
                    pe.sem_inc(s["w_free"], 1)

            @block.scalar
            def _(act):
                act.wait_ge(s["bias_in"], 32)
                for e in range(NE1):
                    for h in range(H2):
                        act.wait_ge(s["turned"], H2 * e + h + 1)
                        nc.scalar.copy(xT[:, h, :], pt[:, h, :]).then_inc(s["turned_kept"], 1)
                    if e:
                        act.wait_ge(s["down_ready"], e * KS)
                    for f in range(FT):
                        n = e * FT + f
                        act.wait_ge(s["up_ready"], n + 1)
                        nc.scalar.activation(hid[:, f, :], up[:, f % 2, :], ACT.Relu, bias=b1[:, n:n + 1]).then_inc(s["hidden_ready"], 1)

            @block.vector
            def _(dve):
                dve.wait_ge(s["bias_in"], 32)
                for e in range(NE1):
                    if e >= 2:
                        dve.wait_ge(s[f"out_{'ab'[e % 2]}"], 16 * (e // 2))
                    for k in range(KS):
                        n = e * KS + k
                        dve.wait_ge(s["down_ready"], n + 1)
                        nc.vector.tensor_tensor(y[:, e % 2, k, :], dn[:, k % 2, 0:D], b2[:, e, :], ALU.add).then_inc(s["added"], 1)
                    dve.wait_ge(s["added"], (e + 1) * KS)
                    dve.sem_inc(s["y_free"], 1)


def collect(nc, g, sem, sb, slot, prob, ybuf, OUT, out):
    zeroed, got, c_, ready, done = (sem("collect_" + k) for k in ("zeroed", "rows_in", "step", "ready", "out"))
    x = g["x"]
    with ExitStack() as sc:
        def t(name, shape, dt=F32):
            return sb("collect_" + name, shape, dt, sc)
        y, m, lim = t("y", [P, T, D]), t("mask", [P, T, D]), t("limits", [P, 3])
        with nc.Block() as block:
            @block.vector
            def _(dve):
                c = Count(c_)

                def link(ins):
                    dve.wait_ge(c.sem, c.mark(ins))
                nc.vector.memset(y[:], 0.0).then_inc(zeroed, 1)
                for k, v in enumerate((0.0, 10000.0, -10000.0)):
                    link(nc.vector.memset(lim[:, k:k + 1], v))
                dve.wait_ge(got, 16 * T)
                bc = lambda a: a.unsqueeze(2).broadcast_to([P, T, D])
                link(nc.vector.tensor_tensor(y[:], y[:], bc(prob[:]), ALU.mult))
                flat = y[:].rearrange("p t d -> p (t d)")
                mf = m[:].rearrange("p t d -> p (t d)")
                big = 3.4028234e38
                for k, (op, v) in enumerate(((None, 0.0), (ALU.is_gt, big), (ALU.is_lt, -big))):
                    if op is None:
                        link(nc.vector.tensor_tensor(mf, flat, flat, ALU.not_equal))
                    else:
                        link(nc.vector.tensor_scalar(mf, flat, v, None, op))
                    link(nc.vector.copy_predicated(flat, mf.bitcast(I32), lim[:, k:k + 1].broadcast_to([P, T * D])))
                link(nc.vector.tensor_tensor(x[:], x[:], y[:], ALU.add))
                dve.sem_inc(ready, 1)

            @block.gpsimd
            def _(pool):
                pool.wait_ge(zeroed, 1)
                for k in range(T):
                    nc.gpsimd.indirect_dma_start(y[:, k, :], None, ybuf[:, :], bass.IndirectOffsetOnAxis(ap=slot[:, k:k + 1], axis=0),
                                                 bounds_check=OUT - 1, oob_is_err=False).then_inc(got, 16)

            @block.sync
            def _(sp):
                sp.wait_ge(ready, 1)
                sp.dma_start(out[0:NFULL * P, :].rearrange("(t p) d -> p t d", p=P), x[:, 0:NFULL, :]).then_inc(done, 16)
                sp.dma_start(out[NFULL * P:N, :], x[0:NREST, NFULL, :]).then_inc(done, 16)
                sp.wait_ge(done, 32)


STEPS = 1 + 4 * BU + 1 + 1 + 1 + 1


def dump_stage(nc, sem, dump, aps):
    d = sem("dumped")
    with nc.Block() as block:
        @block.sync
        def _(sp):
            for k, a in enumerate(aps):
                t = nc.dram_tensor(f"dump{k}", tuple(a.shape), a.dtype, kind="ExternalOutput").ap()
                sp.dma_start(t, a).then_inc(d, 16)
            sp.wait_ge(d, 16 * len(aps))


_INS = {"x": "x", "src": "src", "dst": "dst", "w": "edge_weight", "W_gat": "L0_ffn_W_gat", "att_src": "L0_ffn_att_src",
        "att_dst": "L0_ffn_att_dst", "b_gat": "L0_ffn_b_gat", "ln_gamma": "L0_ffn_ln_gamma", "ln_beta": "L0_ffn_ln_beta",
        "W1": "L0_ffn_W1", "b1": "L0_ffn_b1", "W2": "L0_ffn_W2", "b2": "L0_ffn_b2", "ei": "L0_ffn_edge_index",
        "W_layer": "L1_gnn_W_layer", "b_layer": "L1_gnn_b_layer", "w_a1": "L1_gnn_w_a1", "b_a1": "L1_gnn_b_a1",
        "w_a2": "L1_gnn_w_a2", "b_a2": "L1_gnn_b_a2", "gate_w": "L1_ffn_gate_w", "gate_b": "L1_ffn_gate_b",
        "w1": "L1_ffn_w1", "b1m": "L1_ffn_b1", "w2": "L1_ffn_w2", "b2m": "L1_ffn_b2"}


def kernel(_dump=None, _upto=99, **inputs):
    import numpy as _np
    import concourse.bacc as _bacc
    from concourse import mybir as _mybir
    from concourse.bass_utils import run_bass_kernel_spmd as _run

    nc = _bacc.Bacc("TRN2", target_bir_lowering=False, num_devices=1)
    arrays, aps = {}, {}
    for short, name in _INS.items():
        a = _np.asarray(inputs[name])
        if short == "W_layer":
            a = a.T
        if short in ("b1", "b1m"):
            a = a.reshape(-1, P).T
        a = _np.ascontiguousarray(a)
        arrays[f"in_{short}"] = a
        aps[short] = nc.dram_tensor(f"in_{short}", a.shape, _mybir.dt.from_np(a.dtype), kind="ExternalInput").ap()
    out = nc.dram_tensor("out_0", (N, D), F32, kind="ExternalOutput").ap()
    build(nc, aps, out, _dump, _upto)
    r = _run(nc, [arrays], core_ids=[0])
    return r.results[0]["out_0"]
```

```python
from contextlib import ExitStack

import concourse.bass as bass
from concourse import mybir

F32 = mybir.dt.float32
BF16 = mybir.dt.bfloat16
I32 = mybir.dt.int32
I16 = mybir.dt.int16
ALU = mybir.AluOpType
ACT = mybir.ActivationFunctionType
X = mybir.AxisListType.X
XY = mybir.AxisListType.XY

P = 128
N = 3125
D = 256
H2 = D // P
T = -(-N // P)
NFULL = N // P
NREST = N - NFULL * P
EPS = 1e-5
BIG = 2.0 ** 100

G = 4
GE = G * P
E0 = 32768
E1 = 50000
NBUF = 4


def groups(edges):
    return -(-((edges + T * (GE - 1)) // GE) // NBUF) * NBUF


NG0, NG1 = groups(E0), groups(E1)

CH = P
NCH = -(-E1 // CH)
CB = -(-NCH // P)
OWN = P - 1
BU = 4
NTURN = -(-(2 * E1) // (OWN * BU))
WIN = 3
NF = 10
TWO_PI = 6.283185307179586
TWO_PI_HI = 6.28125
TWO_PI_LO = TWO_PI - TWO_PI_HI
PI_SAFE = 3.1415925
MAGIC = 1.5 * 2.0 ** 23


class Count:

    def __init__(self, sem):
        self.sem, self.n, self.turn, self.per = sem, 0, None, 0

    def mark(self, ins, by=1):
        ins.then_inc(self.sem, by)
        self.n += by
        return self.value()

    def value(self):
        return self.n if self.turn is None else self.turn * self.per + self.n

    def enter(self, turn, per):
        self.turn, self.per, self.start = turn, per, self.n

    def leave(self, turns):
        assert self.n - self.start == self.per, (self.n - self.start, self.per)
        self.n = self.start + self.per * turns
        self.turn = None


def build(nc, A, out):
    with ExitStack() as ctx:
        nsem = [0]

        def sb(name, shape, dt, where=ctx):
            return where.enter_context(nc.sbuf_tensor(name, shape, dt))

        def pb(name, shape, where):
            return where.enter_context(nc.psum_tensor(name, shape, F32))

        live = []

        def sem(name):
            live.append(nc.alloc_semaphore(name=name))
            return live[-1]

        def recycle():
            nc.all_engine_barrier()
            nc.clear_and_free_semaphores(list(live))
            nc.all_engine_barrier()
            live.clear()

        g = {"recycle": recycle}
        g |= {}
        g["x"] = sb("x_nodes", [P, T, D], F32)
        g["iota"] = sb("iota_row", [P, WIN * P], F32)
        g["iota16"] = sb("iota_row16", [P, WIN * P], I16)
        g["pidx"] = sb("partition_index", [P, 1], F32)
        g["ident"] = sb("identity", [P, P], F32)
        g["identb"] = sb("identity_bf", [P, P], BF16)
        g["before"] = sb("row_before_column", [P, P], F32)
        g["ones"] = sb("ones", [P, P], F32)
        g["group_tile0"] = sb("group_tile0", [1, P], I32)
        g["group_tile1"] = sb("group_tile1", [1, P], I32)
        g["rot"] = sb("rotation_matrix", [P, H2, D], F32)
        g["list0"] = nc.dram_tensor("edges_by_tile0", (P * G * NG0, 2), F32).ap()
        g["list1"] = nc.dram_tensor("edges_by_tile1", (P * G * NG1, 2), F32).ap()
        g["window_dram"] = nc.dram_tensor("window_of_chunk", (CB * P,), I32).ap()
        constants(nc, A, g, sem)
        rotations(nc, A, g, sem, sb, pb)
        recycle()
        rest(nc, A, g, sem, sb, pb, out)


def constants(nc, A, g, sem):
    x_loaded, iota_done, const_done, zeroed = sem("x_loaded"), sem("iota_done"), sem("const_done"), sem("x_padding_zeroed")
    with nc.Block() as block:
        @block.sync
        def _(sp):
            sp.dma_start(g["x"][:, 0:NFULL, :], A["x"][0:NFULL * P, :].rearrange("(t p) d -> p t d", p=P)).then_inc(x_loaded, 16)
            sp.wait_ge(zeroed, 1)
            sp.dma_start(g["x"][0:NREST, NFULL, :], A["x"][NFULL * P:N, :]).then_inc(x_loaded, 16)
            sp.wait_ge(x_loaded, 32)

        @block.gpsimd
        def _(pool):
            nc.gpsimd.iota(g["iota"][:], [[1, WIN * P]], base=0, channel_multiplier=0,
                           allow_small_or_imprecise_dtypes=True).then_inc(iota_done, 1)
            nc.gpsimd.iota(g["iota16"][:], [[1, WIN * P]], base=0, channel_multiplier=0,
                           allow_small_or_imprecise_dtypes=True).then_inc(iota_done, 1)
            nc.gpsimd.iota(g["pidx"][:], [[0, 1]], base=0, channel_multiplier=1,
                           allow_small_or_imprecise_dtypes=True).then_inc(iota_done, 1)

        @block.vector
        def _(dve):
            nc.vector.memset(g["x"][:, NFULL, :], 0.0).then_inc(zeroed, 1)
            nc.vector.memset(g["ones"][:], 1.0).then_inc(const_done, 1)
            dve.wait_ge(iota_done, 3)
            row = g["iota"][:, 0:P]
            nc.vector.tensor_scalar(g["ident"][:], row, g["pidx"][:], None, ALU.is_equal).then_inc(const_done, 1)
            nc.vector.tensor_scalar(g["identb"][:], row, g["pidx"][:], None, ALU.is_equal).then_inc(const_done, 1)
            nc.vector.tensor_scalar(g["before"][:], row, g["pidx"][:], None, ALU.is_gt).then_inc(const_done, 1)


def rotations(nc, A, g, sem, sb, pb):
    with ExitStack() as sc:
        def t(name, shape, dt=F32):
            return sb(name, shape, dt, sc)

        lists = []
        for n, (rows, cols, key, other, ngroups) in enumerate((
                (P, E0 // P, A["ei"][1], A["ei"][0], NG0),
                (125, E1 // 125, A["src"], A["dst"], NG1))):
            lists.append(dict(
                n=n, R=rows, F=cols, key_in=key, other_in=other, NG=ngroups, NB=ngroups * G,
                key=t(f"key{n}", [rows, cols], I32), other=t(f"other{n}", [rows, cols], I32),
                tile=t(f"tile{n}", [rows, cols]), slot=t(f"slot{n}", [rows, cols], I32),
                rec=t(f"record{n}", [rows, cols, 2]), list=g[f"list{n}"], group_tile=g[f"group_tile{n}"]))
        FL = max(l["F"] for l in lists)
        tmp_i = t("tmp_i", [P, FL], I32)
        small = t("small", [P, 8, T])
        small_i = t("small_i", [P, T], I32)
        stage_rec = t("stage_rec", [P, 2, 8, 2])
        stage_slot = t("stage_slot", [P, 2, 8], I32)
        ia, ja = t("i_int", [P, CB, CH], I32), t("j_int", [P, CB, CH], I32)
        wa = t("w_a", [P, CB, CH])
        cs = t("chunk_small", [P, 8, CB])
        csi = t("chunk_small_i", [P, 2, CB], I32)
        window_row = t("window_row", [1, CB * P], I32)
        turns_i = t("turns_i", [1, 1], I32)
        NCOMP = BU * (NTURN + 1)
        fieldsB = {k: t("rB_" + k, [P, CB * CH]) for k in ("i", "j", "w", "q")}
        comp = t("terms", [P, NCOMP, NF])

        s = {k: sem(k) for k in (
            "edges0_loaded", "edges1_loaded", "rot_loaded", "rot_padded", "fill_ready", "list_filled", "dve_step", "totals_ready",
            "prefix_ready", "prefix_read", "slots_ready", "pool_step", "pool_ok", "scattered", "window_out",
            "window_in", "fieldsA_ready", "fieldsB_ready", "sin_in", "sin_out", "onehot_ready",
            "chunk_summed", "chunk_added", "comp_zeroed", "compact_done", "act_step")}
        block = nc.Block()
        with ExitStack() as inner:
            wk = ExitStack()
            mask = wk.enter_context(nc.sbuf_tensor("tile_mask", [P, T * FL], F32))
            scan = wk.enter_context(nc.sbuf_tensor("tile_scan", [P, T * FL], F32))
            fill = wk.enter_context(nc.sbuf_tensor("list_fill", [P, G * NG1, 2], F32))
            pre = pb("prefix_ps", [P, 512], wk)
            Fa = {k: wk.enter_context(nc.sbuf_tensor("rA_" + k, [P, CB, CH], F32)) for k in ("i", "j", "a", "b", "f", "scan", "q")}
            tp = wk.enter_context(nc.psum_tensor("fields_ps", [P, 4, CB * CH], F32))
            with nc.Block() as block:
                @block.sync
                def _(sp):
                    for l in lists:
                        sp.dma_start(l["key"][:], l["key_in"].rearrange("(p f) -> p f", p=l["R"])).then_inc(s[f"edges{l['n']}_loaded"], 16)
                        sp.dma_start(l["other"][:], l["other_in"].rearrange("(p f) -> p f", p=l["R"])).then_inc(s[f"edges{l['n']}_loaded"], 16)
                    sp.wait_ge(s["rot_padded"], 3)
                    full, last = E1 // (P * CH), E1 % CH
                    more = NCH - 1 - full * P
                    for tile_, src in ((ia, A["src"]), (ja, A["dst"]), (wa, A["w"])):
                        sp.dma_start(tile_[:, 0:full, :], src[0:full * P * CH].rearrange("(b p s) -> p b s", p=P, s=CH)).then_inc(s["rot_loaded"], 16)
                        sp.dma_start(tile_[0:more, full, :], src[full * P * CH:(NCH - 1) * CH].rearrange("(p s) -> p s", s=CH)).then_inc(s["rot_loaded"], 16)
                        sp.dma_start(tile_[more:more + 1, full, 0:last], src[(NCH - 1) * CH:E1].rearrange("(a s) -> a s", a=1)).then_inc(s["rot_loaded"], 16)
                    sp.wait_ge(s["fill_ready"], 2)
                    for l in lists:
                        sp.dma_start(l["list"].rearrange("(p c) k -> p c k", p=P), fill[:, 0:l["NB"], :]).then_inc(s["list_filled"], 16)
                    sp.wait_ge(s["window_out"], 1)
                    sp.dma_start(g["window_dram"].rearrange("(b p) -> p b", p=P), csi[:, 0, :], allow_slow_non_contiguous=True).then_inc(s["window_in"], 16)
                    sp.wait_ge(s["window_in"], 16)
                    sp.dma_start(window_row[:], g["window_dram"].rearrange("(a c) -> a c", a=1)).then_inc(s["window_in"], 16)
                    sp.wait_ge(s["window_in"], 32)
                    sp.wait_ge(s["list_filled"], 32)

                @block.gpsimd
                def _(pool):
                    nc.gpsimd.memset(ia[:], 99999).then_inc(s["rot_padded"], 1)
                    nc.gpsimd.memset(ja[:], 99999).then_inc(s["rot_padded"], 1)
                    nc.gpsimd.memset(wa[:], 0.0).then_inc(s["rot_padded"], 1)
                    nc.gpsimd.memset(fill[:, :, 0:1].bitcast(I32), N).then_inc(s["fill_ready"], 1)
                    nc.gpsimd.memset(fill[:, :, 1:2], -1.0).then_inc(s["fill_ready"], 1)
                    nc.gpsimd.memset(comp[:], 0.0).then_inc(s["comp_zeroed"], 1)
                    pool.wait_ge(s["comp_zeroed"], 1)

                @block.vector
                def _(dve):
                    c = Count(s["dve_step"])

                    def link(ins):
                        dve.wait_ge(c.sem, c.mark(ins))

                    for l in lists:
                        R, F, NB = l["R"], l["F"], l["NB"]
                        m3 = mask[0:R, 0:T * F].rearrange("p (b f) -> p b f", b=T)
                        s3 = scan[0:R, 0:T * F].rearrange("p (b f) -> p b f", b=T)
                        tot, cnt, ngr, gst, sta = (small[:, k, :] for k in range(5))
                        dve.wait_ge(s[f"edges{l['n']}_loaded"], 32)
                        link(nc.vector.tensor_single_scalar(tmp_i[0:R, 0:F], l["key"][:], 7, ALU.logical_shift_right))
                        link(nc.vector.tensor_copy(l["tile"][:], tmp_i[0:R, 0:F]))
                        link(nc.vector.tensor_single_scalar(tmp_i[0:R, 0:F], l["key"][:], P - 1, ALU.bitwise_and))
                        link(nc.vector.tensor_copy(l["rec"][:, :, 1], tmp_i[0:R, 0:F]))
                        link(nc.vector.tensor_copy(l["rec"][:, :, 0].bitcast(I32), l["other"][:]))
                        link(nc.vector.tensor_tensor(m3, l["tile"][:].unsqueeze(1).broadcast_to([R, T, F]),
                                                     g["iota"][0:R, 0:T].unsqueeze(2).broadcast_to([R, T, F]), ALU.is_equal))
                        link(nc.vector.tensor_tensor_scan(scan[0:R, 0:T * F], g["ones"][0:R, 0:1].broadcast_to([R, T * F]),
                                                          mask[0:R, 0:T * F], 0.0, ALU.mult, ALU.add))
                        link(nc.vector.tensor_copy(tot[0:R, 0:1], s3[:, 0, F - 1:F]))
                        nc.vector.tensor_tensor(tot[0:R, 1:T], s3[:, 1:T, F - 1], s3[:, 0:T - 1, F - 1], ALU.subtract).then_inc(s["totals_ready"], 1)
                        dve.wait_ge(s["prefix_ready"], 1 + 2 * l["n"])
                        link(nc.vector.tensor_scalar(cnt, pre[:, T:2 * T], float(GE - 1), None, ALU.add))
                        link(nc.vector.tensor_copy(small_i[:], cnt))
                        link(nc.vector.tensor_single_scalar(small_i[:], small_i[:], 9, ALU.logical_shift_right))
                        link(nc.vector.tensor_copy(ngr, small_i[:]))
                        link(nc.vector.tensor_tensor_scan(gst, g["ones"][:, 0:T], ngr, 0.0, ALU.mult, ALU.add))
                        link(nc.vector.tensor_tensor(gst, gst, ngr, ALU.subtract))
                        link(nc.vector.scalar_tensor_tensor(sta, gst, float(GE), pre[:, 0:T], ALU.mult, ALU.add))
                        link(nc.vector.tensor_tensor(sta[0:R], sta[0:R], tot[0:R], ALU.add))
                        link(nc.vector.tensor_tensor(sta[0:R], sta[0:R], s3[:, :, F - 1], ALU.subtract))
                        link(nc.vector.tensor_scalar(sta[0:R], sta[0:R], -1.0, None, ALU.add))
                        link(nc.vector.tensor_scalar(small[:, 5, 1:T], gst[:, 1:T], g["pidx"][:], None, ALU.is_le))
                        nc.vector.tensor_reduce(small[:, 6, 0:1], small[:, 5, 1:T], X, ALU.add).then_inc(s["totals_ready"], 1)
                        link(nc.vector.tensor_tensor(s3, s3, sta[0:R].unsqueeze(2).broadcast_to([R, T, F]), ALU.add))
                        link(nc.vector.tensor_tensor(s3, s3, m3, ALU.mult))
                        link(nc.vector.tensor_reduce(l["tile"][:], s3.rearrange("p b f -> p f b"), X, ALU.add))
                        link(nc.vector.tensor_copy(l["key"][:], l["tile"][:]))
                        link(nc.vector.tensor_single_scalar(tmp_i[0:R, 0:F], l["key"][:], P - 1, ALU.bitwise_and))
                        link(nc.vector.tensor_single_scalar(l["key"][:], l["key"][:], 7, ALU.logical_shift_right))
                        link(nc.vector.scalar_tensor_tensor(l["slot"][:], tmp_i[0:R, 0:F], float(NB), l["key"][:], ALU.mult, ALU.add))
                        dve.wait_ge(s["prefix_ready"], 2 + 2 * l["n"])
                        nc.vector.tensor_copy(l["group_tile"][:], pre[0:1, 64:64 + P]).then_inc(s["prefix_read"], 1)
                    flat = lambda a: a[:].rearrange("p b s -> p (b s)")
                    dve.wait_ge(s["rot_loaded"], 144)
                    fi, fj, aa, bb, ff, sc_, q = (flat(Fa[k]) for k in ("i", "j", "a", "b", "f", "scan", "q"))
                    link(nc.vector.tensor_copy(fi, flat(ia)))
                    link(nc.vector.tensor_copy(fj, flat(ja)))
                    link(nc.vector.tensor_tensor(aa, fi, fj, ALU.not_equal))
                    link(nc.vector.scalar_tensor_tensor(aa, fi, float(D), aa, ALU.is_lt, ALU.mult))
                    link(nc.vector.scalar_tensor_tensor(ff, fj, float(D), aa, ALU.is_lt, ALU.add))
                    for b in range(CB):
                        link(nc.vector.tensor_tensor_scan(Fa["scan"][:, b, :], g["ones"][:, 0:CH], Fa["f"][:, b, :], 0.0, ALU.mult, ALU.add))
                    nc.vector.tensor_copy(cs[:, 0, :], Fa["scan"][:, :, CH - 1]).then_inc(s["totals_ready"], 1)
                    dve.wait_ge(s["prefix_ready"], 5)
                    link(nc.vector.tensor_copy(cs[:, 7, :], pre[:, CB:2 * CB]))
                    link(nc.vector.tensor_tensor_scan(cs[:, 1, :], g["ones"][:, 0:CB], cs[:, 7, :], 0.0, ALU.mult, ALU.add))
                    link(nc.vector.tensor_tensor(cs[:, 2, :], cs[:, 1, :], cs[:, 7, :], ALU.subtract))
                    link(nc.vector.tensor_tensor(cs[:, 2, :], cs[:, 2, :], pre[:, 0:CB], ALU.add))

                    def whole(dst, src, by, plus):
                        link(nc.vector.tensor_scalar(dst, src, plus + 0.5, 1.0 / by, ALU.add, ALU.mult))
                        link(nc.vector.tensor_scalar(dst, dst, -0.5, None, ALU.add))
                        link(nc.vector.tensor_scalar(dst, dst, MAGIC, None, ALU.add))
                        link(nc.vector.tensor_scalar(dst, dst, -MAGIC, None, ALU.add))

                    whole(cs[:, 3, :], cs[:, 2, :], OWN, 0.0)
                    link(nc.vector.tensor_tensor(cs[:, 4, :], cs[:, 2, :], cs[:, 3, :], ALU.add))
                    link(nc.vector.tensor_copy(csi[:, 1, :], cs[:, 4, :]))
                    link(nc.vector.tensor_single_scalar(csi[:, 0, :], csi[:, 1, :], 7, ALU.logical_shift_right))
                    link(nc.vector.tensor_copy(cs[:, 5, :], csi[:, 0, :]))
                    link(nc.vector.tensor_single_scalar(csi[:, 0, :], csi[:, 0, :], NF, ALU.mult))
                    nc.vector.tensor_scalar(cs[:, 6, :], cs[:, 5, :], float(P), None, ALU.mult).then_inc(s["window_out"], 1)
                    dve.wait_ge(s["window_out"], 1)
                    link(nc.vector.tensor_tensor(aa, sc_, ff, ALU.subtract))
                    link(nc.vector.tensor_tensor(Fa["a"][:], Fa["a"][:], cs[:, 2, :].unsqueeze(2).broadcast_to([P, CB, CH]), ALU.add))
                    whole(bb, aa, OWN, 0.0)
                    link(nc.vector.tensor_tensor(q, aa, bb, ALU.add))
                    nc.vector.tensor_tensor(Fa["q"][:], Fa["q"][:], cs[:, 6, :].unsqueeze(2).broadcast_to([P, CB, CH]), ALU.subtract).then_inc(s["fieldsA_ready"], 1)
                    whole(cs[0:1, 7, 0:1], cs[0:1, 1, CB - 1:CB], OWN * BU, float(OWN * BU - 1))
                    link(nc.vector.tensor_scalar(cs[0:1, 7, 0:1], cs[0:1, 7, 0:1], 1.0, None, ALU.max))
                    link(nc.vector.tensor_copy(turns_i[:], cs[0:1, 7, 0:1]))
                    dve.wait_ge(s["prefix_read"], 2)

                @block.scalar
                def _(act):
                    act.wait_ge(s["fieldsB_ready"], 1)
                    for k, f in enumerate(("i", "j", "w", "q")):
                        nc.scalar.copy(fieldsB[f][:], tp[:, k, :])

                @block.tensor
                def _(pe):
                    for l in lists:
                        R = l["R"]
                        pe.wait_ge(s["totals_ready"], 1 + 2 * l["n"])
                        if l["n"]:
                            pe.wait_ge(s["prefix_read"], l["n"])
                        nc.tensor.matmul(pre[:, 0:T], g["before"][0:R, :], small[0:R, 0, :], start=True, stop=True)
                        nc.tensor.matmul(pre[:, T:2 * T], g["ones"][0:R, :], small[0:R, 0, :], start=True, stop=True).then_inc(s["prefix_ready"], 1)
                        pe.wait_ge(s["totals_ready"], 2 + 2 * l["n"])
                        nc.tensor.matmul(pre[0:1, 64:64 + P], small[:, 6, 0:1], g["ident"][:], start=True, stop=True).then_inc(s["prefix_ready"], 1)
                    pe.wait_ge(s["totals_ready"], 5)
                    pe.wait_ge(s["prefix_read"], 2)
                    nc.tensor.matmul(pre[:, 0:CB], g["before"][:], cs[:, 0, :], start=True, stop=True)
                    nc.tensor.matmul(pre[:, CB:2 * CB], g["ones"][:], cs[:, 0, :], start=True, stop=True).then_inc(s["prefix_ready"], 1)
                    pe.wait_ge(s["fieldsA_ready"], 1)
                    for k, f in enumerate((Fa["i"], Fa["j"], wa, Fa["q"])):
                        for b in range(CB):
                            ins = nc.tensor.transpose(tp[:, k, b * CH:(b + 1) * CH], f[:, b, :], g["ident"][:])
                    ins.then_inc(s["fieldsB_ready"], 1)
                    pe.wait_ge(s["fieldsB_ready"], 1)
            wk.close()
        multiply(nc, g, sem, t, pb, sc, lists, comp, NCOMP, fieldsB, window_row, turns_i, stage_rec, stage_slot)


SCAT = 8


def multiply(nc, g, sem, t, pb, sc, lists, comp, NCOMP, fieldsB, window_row, turns_i, stage_rec, stage_slot):
    names = (
        "lot_staged", "held", "lot_scattered_a", "lot_scattered_b", "step", "angle_ready", "sine_ready",
        "onehot_ready", "window_summed", "window_added", "terms_packed", "v_ready", "vt_ready", "vt_copied",
        "l_ready", "tables_zeroed", "t1_ready", "x1_turned", "x1_copied", "level_ready", "tx_ready", "q_ready",
        "q_copied", "wt_ready", "wt_copied", "y_ready", "y_copied", "dm_ready", "m_added", "m_ready")
    s = {k: sem("rot_" + k) for k in names}
    NC4 = CB * CH
    rec = [t(f"term_records{k}", [P, NC4, NF], BF16) for k in range(2)]
    pos = [t(f"term_position{k}", [P, NC4]) for k in range(2)]
    fi, fj, w1, w2, sn, cn = (t("rB_tmp%d" % k, [P, NC4]) for k in range(6))
    part = t("part_bf", [P, NC4], BF16)
    onehot = t("onehot", [P, 2, 2, WIN * P], BF16)
    below, level, nshift = g["before"], t("level_masks", [P, 7, P]), t("next_column", [P, P])
    xor_i, xs_i = t("xor_i", [P, P], I32), t("xor_shifted", [P, P], I32)
    row_i, col_i = t("row_i", [P, P], I32), t("col_i", [P, P], I32)
    cf = t("coefficients", [P, BU, NF])
    SU = BU // 2
    U, V, V2 = t("U", [P, BU, D], BF16), t("V", [P, BU, D]), t("V2", [P, BU, D])
    VT, UT = t("VT", [P, BU, H2, P]), t("UT", [P, BU, H2, P])
    pair_mask = t("pair_mask", [P, BU, P])
    LT = t("LT", [P, BU, P])
    NK = t("NK", [P, 7, BU, P])
    TX = t("TX", [P, BU, 2, P])
    QS = t("QS", [P, 7, BU, P])
    WT, UC = t("WT", [P, BU, H2, P]), t("UC", [P, BU, D])
    YS = t("YS", [P, 2, P])
    M = g["rot"]
    ps_a = [pb(f"ps_a{k}", [P, 512], sc) for k in range(2)]
    ps_b = [pb(f"ps_b{k}", [P, 512], sc) for k in range(2)]
    ps_y = [pb(f"ps_y{k}", [P, 512], sc) for k in range(2)]
    ps_m = [pb(f"ps_m{k}", [P, 512], sc) for k in range(2)]

    def window(b, w=None):
        return ps_m[b][:, 0:WIN * NF] if w is None else ps_m[b][:, w * NF:(w + 1) * NF]

    def cols(a, k, which):
        letters = "abc"[:len(a.shape) - 2]
        v = a.rearrange(f"p {' '.join(letters)} (n o w) -> p {' '.join(letters)} n o w", o=2, w=2 ** k)
        return v[:, :, :, which, :] if letters == "a" else v[:, :, which, :]

    with nc.Block() as block:
        @block.gpsimd
        def _(pool):
            nc.gpsimd.iota(row_i[:], [[0, P]], base=0, channel_multiplier=1).then_inc(s["m_ready"], 1)
            nc.gpsimd.iota(col_i[:], [[1, P]], base=0, channel_multiplier=0).then_inc(s["m_ready"], 1)
            staged = Count(s["lot_staged"])
            done = [s["lot_scattered_a"], s["lot_scattered_b"]]
            base = [0, 0]
            for l in lists:
                R, F = l["R"], l["F"]

                def lot(turn, b, first):
                    if not first:
                        pool.wait_ge(done[b], base[b] + turn * (SCAT * 16))
                        pool.sem_inc(s["held"], 1)
                    at = (turn * 2 + b) * SCAT
                    cols = slice(at, at + SCAT) if isinstance(at, int) else bass.ds(at, SCAT)
                    staged.mark(nc.gpsimd.tensor_copy(stage_rec[0:R, b], l["rec"][:, cols, :]))
                    v = staged.mark(nc.gpsimd.tensor_copy(stage_slot[0:R, b], l["slot"][:, cols]))
                    pool.wait_ge(staged.sem, v)
                    pool.sem_inc(s["held"], 1)
                    for k in range(SCAT):
                        nc.gpsimd.indirect_dma_start(l["list"][:, :], bass.IndirectOffsetOnAxis(ap=stage_slot[0:R, b, k:k + 1], axis=0),
                                                     stage_rec[0:R, b, k, :], None).then_inc(done[b], 16)

                turns = F // (2 * SCAT)
                for b in range(2):
                    lot(0, b, l["n"] == 0)
                with pool.Fori(1, turns) as i:
                    staged.enter(i - 1, 4)
                    for b in range(2):
                        lot(i, b, False)
                    staged.leave(turns - 1)
                base = [b + turns * SCAT * 16 for b in base]
            for b in range(2):
                pool.wait_ge(done[b], base[b])
            nc.gpsimd.memset(stage_slot[0:1, 0, 0:1], 0)

        @block.scalar
        def _(act):
            act.wait_ge(s["angle_ready"], 1)
            nc.scalar.activation(sn[:], w1[:], ACT.Sin).then_inc(s["sine_ready"], 1)
            nc.scalar.activation(cn[:], w2[:], ACT.Sin).then_inc(s["sine_ready"], 1)
            act.wait_ge(s["terms_packed"], 1)
            trips = act.value_load(turns_i[0:1, 0:1], min_val=1, max_val=NTURN)
            vt, vc, xp, xc, q, qc, wt, wc, y, yc = (Count(s[k]) for k in (
                "vt_ready", "vt_copied", "x1_turned", "x1_copied", "q_ready", "q_copied", "wt_ready", "wt_copied", "y_ready", "y_copied"))

            def need(c_):
                c_.n += 1
                act.wait_ge(c_.sem, c_.value())

            def turn(chain):
                def copy_y(u):
                    for c_ in range(2) if chain else ():
                        need(y)
                        yc.mark(nc.scalar.copy(YS[:, c_, :], ps_y[c_][:, 0:P]))

                def copy_vu(h):
                    b = slice(h * SU, (h + 1) * SU)
                    need(vt)
                    vc.mark(nc.scalar.copy(VT[:, b].rearrange("p u h c -> p (u h c)"), ps_a[h][:]))
                    vc.mark(nc.scalar.copy(UT[:, b].rearrange("p u h c -> p (u h c)"), ps_b[h][:].bitcast(BF16)[:, 0:SU * D]))

                copy_y(0)
                copy_vu(0)
                copy_y(1)
                copy_vu(1)
                copy_y(2)
                for h in range(2):
                    need(xp)
                    xc.mark(nc.scalar.copy(TX[:, h * SU:(h + 1) * SU, 1, :], ps_a[h][:, 0:SU * P].rearrange("p (u c) -> p u c", u=SU)))
                    if h == 0:
                        copy_y(3)
                for k in range(1, 7):
                    for h in range(2):
                        need(q)
                        dst = cols(QS[:, k, h * SU:(h + 1) * SU, :], k, 0)
                        qc.mark(nc.scalar.copy(dst, ps_b[h][:, 0:SU * P // 2].rearrange("p (u n w) -> p u n w", u=SU, w=2 ** k)))
                for h in range(2):
                    b = slice(h * SU, (h + 1) * SU)
                    need(wt)
                    wc.mark(nc.scalar.copy(WT[:, b].rearrange("p u h c -> p (u h c)"), ps_a[h][:]))
                    wc.mark(nc.scalar.copy(UC[:, b], U[:, b]))

            turn(False)
            with act.Fori(0, trips) as i:
                for c_, per in ((vt, 2), (vc, 4), (xp, 2), (xc, 2), (q, 12), (qc, 12), (wt, 2), (wc, 4), (y, 2 * BU), (yc, 2 * BU)):
                    c_.enter(i, per)
                turn(True)

        @block.vector
        def _(dve):
            c = Count(s["step"])

            def link(ins):
                dve.wait_ge(c.sem, c.mark(ins))

            dve.wait_ge(s["m_ready"], 2)
            link(nc.vector.tensor_tensor(xor_i[:], row_i[:], col_i[:], ALU.bitwise_xor))
            for k in range(7):
                link(nc.vector.tensor_single_scalar(xs_i[:], xor_i[:], k, ALU.logical_shift_right))
                link(nc.vector.scalar_tensor_tensor(level[:, k, :], xs_i[:], 1.0, below[:], ALU.is_equal, ALU.mult))
            link(nc.vector.tensor_scalar(nshift[:], g["iota"][:, 0:P], -1.0, g["pidx"][:], ALU.add, ALU.is_equal))
            link(nc.vector.tensor_scalar(nshift[:], nshift[:], -1.0, None, ALU.mult))
            for h in range(H2):
                link(nc.vector.tensor_scalar(M[:, h, :], g["iota"][:, 0:D], float(-h * P), g["pidx"][:], ALU.add, ALU.is_equal))
            B = {k: v[:] for k, v in fieldsB.items()}
            link(nc.vector.tensor_scalar(w1[:], B["w"], 1.0 / TWO_PI, None, ALU.mult))
            link(nc.vector.tensor_scalar(w1[:], w1[:], MAGIC, None, ALU.add))
            link(nc.vector.tensor_scalar(w1[:], w1[:], -MAGIC, None, ALU.add))
            link(nc.vector.scalar_tensor_tensor(w2[:], w1[:], -TWO_PI_HI, B["w"], ALU.mult, ALU.add))
            link(nc.vector.scalar_tensor_tensor(w1[:], w1[:], -TWO_PI_LO, w2[:], ALU.mult, ALU.add))
            link(nc.vector.tensor_scalar(w1[:], w1[:], PI_SAFE, -PI_SAFE, ALU.min, ALU.max))
            link(nc.vector.scalar_tensor_tensor(w2[:], w1[:], -1.0, w1[:], ALU.mult, ALU.max))
            link(nc.vector.tensor_scalar(w2[:], w2[:], -1.0, TWO_PI / 4, ALU.mult, ALU.add))
            dve.sem_inc(s["angle_ready"], 1)
            link(nc.vector.tensor_tensor(fi[:], B["i"], B["j"], ALU.not_equal))
            link(nc.vector.scalar_tensor_tensor(fi[:], B["i"], float(D), fi[:], ALU.is_lt, ALU.mult))
            link(nc.vector.tensor_scalar(fj[:], B["j"], float(D), None, ALU.is_lt))
            link(nc.vector.scalar_tensor_tensor(pos[0][:], B["q"], 1.0, fi[:], ALU.add, ALU.mult))
            link(nc.vector.tensor_scalar(pos[0][:], pos[0][:], -1.0, None, ALU.add))
            link(nc.vector.scalar_tensor_tensor(pos[1][:], B["q"], 1.0, fi[:], ALU.add, ALU.add))
            link(nc.vector.tensor_tensor(pos[1][:], pos[1][:], fj[:], ALU.mult))
            link(nc.vector.tensor_scalar(pos[1][:], pos[1][:], -1.0, None, ALU.add))
            for k, f in enumerate(("i", "j")):
                link(nc.vector.tensor_scalar(rec[k][:, :, 0], B[f], float(D - 1), 1.0, ALU.min, ALU.add))
                for r in rec:
                    link(nc.vector.tensor_scalar(r[:, :, 1 + k], B[f], float(D - 1), None, ALU.min))
            link(nc.vector.tensor_tensor(rec[0][:, :, 3], fi[:], fj[:], ALU.mult))
            link(nc.vector.memset(rec[1][:, :, 3], 0.0))
            dve.wait_ge(s["sine_ready"], 2)
            for v, places in ((cn, ((0, 4, 1.0), (1, 7, 1.0))), (sn, ((0, 7, -1.0), (1, 4, 1.0)))):
                for k in range(3):
                    link(nc.vector.tensor_copy(part[:], v[:]))
                    for r, at, sign in places:
                        link(nc.vector.tensor_scalar(rec[r][:, :, at + k], part[:], sign, None, ALU.mult))
                    if k < 2:
                        link(nc.vector.tensor_tensor(v[:], v[:], part[:], ALU.subtract))
            ready, added = Count(s["onehot_ready"]), Count(s["window_added"])
            dve.sem_inc(s["window_added"], 2)
            added.n = 2

            def onehots(c_, b):
                for k in range(2):
                    ready.mark(nc.vector.tensor_scalar(onehot[:, b, k, :], g["iota16"][:], pos[k][:, bass.ds(c_, 1)], None, ALU.is_equal))

            onehots(0, 0)
            summed = Count(s["window_summed"])
            flat = comp[:].rearrange("p n f -> p (n f)")
            with dve.Fori(0, (NCH + 1) // 2) as i:
                added.enter(i, 2)
                summed.enter(i, 2)
                for b in range(2):
                    at = dve.value_load(window_row[0:1, bass.ds(i * 2 + b, 1)], min_val=0, max_val=(NCOMP - WIN) * NF)
                    onehots(i * 2 + b + 1, 1 - b)
                    summed.n += 1
                    dve.wait_ge(summed.sem, summed.value())
                    dve.wait_ge(added.sem, added.value())
                    added.mark(nc.vector.tensor_tensor(flat[:, bass.ds(at, WIN * NF)], flat[:, bass.ds(at, WIN * NF)], window(b), ALU.add))
                added.leave((NCH + 1) // 2)
            dve.wait_ge(added.sem, added.value())
            link(nc.vector.tensor_tensor(comp[:, :, 4:10:3], comp[:, :, 4:10:3], comp[:, :, 5:10:3], ALU.add))
            link(nc.vector.tensor_tensor(comp[:, :, 4:10:3], comp[:, :, 4:10:3], comp[:, :, 6:10:3], ALU.add))
            dve.sem_inc(s["terms_packed"], 1)
            trips = dve.value_load(turns_i[0:1, 0:1], min_val=1, max_val=NTURN)
            nc.vector.memset(NK[:], 0.0).then_inc(c.sem, 1)
            nc.vector.memset(QS[:], 0.0).then_inc(c.sem, 1)
            c.n += 2
            dve.wait_ge(c.sem, c.value())
            dve.sem_inc(s["tables_zeroed"], 1)
            dve.sem_inc(s["m_added"], 2)
            step = Count(c.sem)
            step.n = c.n
            vr, lr, t1, lv, tx, dm, ma, wc = (Count(s[k]) for k in (
                "v_ready", "l_ready", "t1_ready", "level_ready", "tx_ready", "dm_ready", "m_added", "wt_copied"))

            def slink(ins):
                dve.wait_ge(step.sem, step.mark(ins))

            def need(c_):
                c_.n += 1
                dve.wait_ge(c_.sem, c_.value())

            def turn(i, chain):
                f = lambda u, k: cf[:, u, k:k + 1]
                half = lambda h: slice(h * SU, (h + 1) * SU)

                def rows_of(u):
                    step.mark(nc.vector.tensor_scalar(U[:, u, :], g["iota"][:, 1:D + 1], f(u, 0), None, ALU.is_equal))
                    step.mark(nc.vector.tensor_scalar(V[:, u, :], g["iota"][:, 0:D], f(u, 1), f(u, 4), ALU.is_equal, ALU.mult))
                    step.mark(nc.vector.tensor_scalar(V2[:, u, :], g["iota"][:, 0:D], f(u, 2), f(u, 7), ALU.is_equal, ALU.mult))
                    step.mark(nc.vector.scalar_tensor_tensor(pair_mask[:, u, :], nshift[:], f(u, 3), below[:], ALU.mult, ALU.add))

                def v_of(h):
                    dve.wait_ge(step.sem, step.value())
                    slink(nc.vector.tensor_tensor(V[:, half(h)], V[:, half(h)], V2[:, half(h)], ALU.add))
                    vr.mark(nc.vector.tensor_tensor(V[:, half(h)], V[:, half(h)], U[:, half(h)], ALU.subtract))

                def add_m(u):
                    for c_ in range(2) if chain else ():
                        need(dm)
                        part_ = M[:, :, c_ * P:(c_ + 1) * P]
                        ma.mark(nc.vector.tensor_tensor(part_, part_, ps_m[c_][:, 0:D].rearrange("p (h c) -> p h c", h=H2), ALU.add))

                def nk(h, k):
                    w = 2 ** k
                    m = level[:, k, :].rearrange("p (n o w) -> p n o w", o=2, w=w)[:, :, 1, :]
                    return nc.vector.tensor_tensor(cols(NK[:, k, half(h), :], k, 1), cols(LT[:, half(h), :], k, 1),
                                                   m.unsqueeze(1).broadcast_to([P, SU, P // 2 // w, w]), ALU.mult)

                def l_of(h):
                    need(lr)
                    slink(nc.vector.tensor_tensor(LT[:, half(h)], ps_b[h][:, 0:SU * P].rearrange("p (u c) -> p u c", u=SU), pair_mask[:, half(h)], ALU.mult))
                    slink(nk(h, 0))
                    t1.mark(nc.vector.tensor_tensor(TX[:, half(h), 0, :], NK[:, 0, half(h)], g["ident"][:].unsqueeze(1).broadcast_to([P, SU, P]), ALU.add))
                    lv.mark(nk(h, 1))

                if chain:
                    dve.wait_ge(wc.sem, i * 4 + 4)
                first = (i + 1) * (BU * NF) if chain else 0
                slink(move(nc, cf[:].rearrange("p u c -> p (u c)"), flat[:, bass.ds(first, BU * NF)]))
                for u in range(SU):
                    rows_of(u)
                v_of(0)
                add_m(0)
                for u in range(SU, BU):
                    rows_of(u)
                add_m(1)
                v_of(1)
                l_of(0)
                add_m(2)
                l_of(1)
                add_m(3)
                for k in range(1, 7):
                    for h in range(2):
                        if k < 6:
                            step.mark(nk(h, k + 1))
                    for h in range(2):
                        need(tx)
                        for o, (src, which) in enumerate(((0, 1), (1, 0))[:1 if k == 6 else 2]):
                            dst = cols(TX[:, half(h), src, :], k, which)
                            ins = nc.vector.tensor_tensor(dst, dst, ps_a[h][:, o * P:(o + 1) * P].rearrange("p (u n w) -> p u n w", u=SU, w=2 ** k), ALU.add)
                            if o == 0 and k < 6:
                                step.mark(ins)
                        lv.mark(ins)

            start = step.n
            turn(0, False)
            per = step.n - start
            with dve.Fori(0, trips) as i:
                for c_, p_ in ((step, per), (vr, 2), (lr, 2), (t1, 2), (lv, 14), (tx, 12), (dm, 2 * BU), (ma, 2 * BU)):
                    c_.enter(i, p_)
                turn(i, True)

        @block.tensor
        def _(pe):
            ready, added, summed = Count(s["onehot_ready"]), Count(s["window_added"]), Count(s["window_summed"])
            with pe.Fori(0, (NCH + 1) // 2) as i:
                for c_, per in ((ready, 4), (added, 2), (summed, 2)):
                    c_.enter(i, per)
                for b in range(2):
                    ready.n += 2
                    added.n += 1
                    pe.wait_ge(ready.sem, ready.value())
                    pe.wait_ge(added.sem, added.value())
                    for w in range(WIN):
                        for k in range(2):
                            ins = nc.tensor.matmul(window(b, w), onehot[:, b, k, w * P:(w + 1) * P],
                                                   rec[k][:, bass.ds(i * 2 + b, 1), :].rearrange("p a f -> p (a f)"), start=(k == 0), stop=(k == 1))
                    summed.mark(ins)
            pe.wait_ge(s["terms_packed"], 1)
            trips = pe.value_load(turns_i[0:1, 0:1], min_val=1, max_val=NTURN)
            pe.wait_ge(s["tables_zeroed"], 1)
            vr, vt, vc, lr, t1, xp, xc, lv, q, qc, tx, wt, y, yc, dm = (Count(s[k]) for k in (
                "v_ready", "vt_ready", "vt_copied", "l_ready", "t1_ready", "x1_turned", "x1_copied", "level_ready", "q_ready",
                "q_copied", "tx_ready", "wt_ready", "y_ready", "y_copied", "dm_ready"))

            def need(c_, k=1):
                c_.n += k
                pe.wait_ge(c_.sem, c_.value())

            def turn(i, chain):
                blocks = lambda h: range(h * SU, (h + 1) * SU)

                def chain_block(u):
                    if not chain:
                        return
                    if u == 0:
                        pe.wait_ge(s["wt_copied"], i * 4 + 4)
                    for c_ in range(2):
                        pe.wait_ge(s["m_added"], i * (2 * BU) + (2 * u + c_ + 1))
                        for h in range(H2):
                            ins = nc.tensor.matmul(ps_y[c_][:, 0:P], WT[:, u, h, :], M[:, h, c_ * P:(c_ + 1) * P], start=(h == 0), stop=(h == 1))
                        y.mark(ins)
                    for c_ in range(2):
                        need(yc)
                        for h in range(H2):
                            ins = nc.tensor.matmul(ps_m[c_][:, h * P:(h + 1) * P], UC[:, u, h * P:(h + 1) * P], YS[:, c_, :], start=True, stop=True)
                        dm.mark(ins)

                def turn_vu(b):
                    need(vr)
                    for n, u in enumerate(blocks(b)):
                        for h in range(H2):
                            nc.tensor.transpose(ps_a[b][:, (n * H2 + h) * P:(n * H2 + h + 1) * P], V[:, u, h * P:(h + 1) * P], g["ident"][:])
                            at = (n * H2 + h) * P
                            ins = nc.tensor.transpose(ps_b[b][:].bitcast(BF16)[:, at:at + P], U[:, u, h * P:(h + 1) * P], g["identb"][:])
                    vt.mark(ins)

                def l_of(b):
                    need(vc, 2)
                    for n, u in enumerate(blocks(b)):
                        for h in range(H2):
                            ins = nc.tensor.matmul(ps_b[b][:, n * P:(n + 1) * P], UT[:, u, h, :], VT[:, u, h, :], start=(h == 0), stop=(h == 1))
                    lr.mark(ins)

                def x1_of(b):
                    need(t1)
                    for n, u in enumerate(blocks(b)):
                        ins = nc.tensor.transpose(ps_a[b][:, n * P:(n + 1) * P], TX[:, u, 0, :], g["ident"][:])
                    xp.mark(ins)

                chain_block(0)
                turn_vu(0)
                chain_block(1)
                l_of(0)
                turn_vu(1)
                chain_block(2)
                x1_of(0)
                l_of(1)
                chain_block(3)
                x1_of(1)
                two = lambda a, k: a.rearrange("p (n w) -> p n w", w=2 ** k)
                half_cols = lambda a, k, which: a.rearrange("p (n o w) -> p n o w", o=2, w=2 ** k)[:, :, which, :]
                for k in range(1, 7):
                    for b in range(2):
                        if k == 1:
                            need(xc)
                        need(lv)
                        for n, u in enumerate(blocks(b)):
                            ins = nc.tensor.matmul(two(ps_b[b][:, n * 64:(n + 1) * 64], k), NK[:, k, u, :], half_cols(TX[:, u, 1, :], k, 0), start=True, stop=True)
                        q.mark(ins)
                    for b in range(2):
                        need(qc)
                        for n, u in enumerate(blocks(b)):
                            ins = nc.tensor.matmul(two(ps_a[b][:, n * 64:(n + 1) * 64], k), QS[:, k, u, :], half_cols(TX[:, u, 0, :], k, 1), start=True, stop=True)
                            if k < 6:
                                ins = nc.tensor.matmul(two(ps_a[b][:, P + n * 64:P + (n + 1) * 64], k), TX[:, u, 0, :], half_cols(QS[:, k, u, :], k, 0), start=True, stop=True)
                        tx.mark(ins)
                for b in range(2):
                    need(lv)
                    for n, u in enumerate(blocks(b)):
                        for h in range(H2):
                            at = (n * H2 + h) * P
                            ins = nc.tensor.matmul(ps_a[b][:, at:at + P], V[:, u, h * P:(h + 1) * P], TX[:, u, 0, :], start=True, stop=True)
                    wt.mark(ins)

            turn(0, False)
            with pe.Fori(0, trips) as i:
                for c_, per in ((vr, 2), (vt, 2), (vc, 4), (lr, 2), (t1, 2), (xp, 2), (xc, 2), (lv, 14), (q, 12), (qc, 12),
                                (tx, 12), (wt, 2), (y, 2 * BU), (yc, 2 * BU), (dm, 2 * BU)):
                    c_.enter(i, per)
                turn(i, True)
HEADS, NE0, F0 = 4, 4, 512
NE1, F1 = 8, 1024
CAP = -(-5 * N // (4 * NE1))
SLOTS = -(-CAP // P) * P
TT = 5
NTT = T // TT
SLOPE0, SLOPE1 = 0.2, 0.01
W0, W1R = HEADS * NE0 + HEADS, D + 2


def rest(nc, A, g, sem, sb, pb, out):
    x = g["x"]
    g["xnT"] = sb("x_normed_T", [P, H2, T * P], F32)
    g["mv"] = sb("mean_var", [P, T, 2], F32)
    g["rstd"] = sb("rstd", [P, T], F32)
    g["a_dst"] = sb("a_dst", [P, T, HEADS], F32)
    g["a_src"] = sb("a_src", [P, T, HEADS], F32)
    g["a1"] = sb("a_target1", [P, T, 1], F32)
    tab0 = nc.dram_tensor("node_rows0", (N + 1, W0), F32).ap()
    tab1 = nc.dram_tensor("node_rows1", (N + 1, W1R), F32).ap()
    with ExitStack() as sc:
        def t(name, shape, dt=F32):
            return sb(name, shape, dt, sc)
        MT = t("rotation_T", [P, H2, D])
        transpose_rotation(nc, g, sem, pb, MT)

        def add_to_x(dve, i, k, ps, used):
            used.mark(nc.vector.tensor_tensor(one(x, i, k), one(x, i, k), ps, ALU.add))
        layernorm(nc, g, sem, sb, "n0")
        project(nc, g, sem, sb, pb, "mix", lambda h: MT[:, h, :], D, add_to_x)
    with ExitStack() as sc:
        def t(name, shape, dt=F32):
            return sb(name, shape, dt, sc)
        gates = t("gates", [P, T, NE0])
        with ExitStack() as s2:
            def t2(name, shape, dt=F32):
                return sb(name, shape, dt, s2)
            wg = t2("W_gat", [P, H2, 16])
            rows = t2("rows0", [P, T, W0])
            small = t2("att_small", [P, 5, 16])
            prod = t2("att_prod", [P, T, 16])
            load_small(nc, sem, [(wg[:], A["W_gat"].rearrange("(h p) f -> p h f", p=P))] + [
                (small[:, k, :], A[n].rearrange("a b -> (a b)").partition_broadcast(P) if n[:3] == "att" else A[n].partition_broadcast(P))
                for k, n in enumerate(("att_src", "att_dst", "b_gat", "ln_gamma", "ln_beta"))], "att")

            def keep_rows(dve, i, k, ps, used):
                used.mark(move(nc, rows[:, bass.ds(i * TT + k, 1), 0:16].rearrange("p a d -> p (a d)"), ps))
            layernorm(nc, g, sem, sb, "n1")
            project(nc, g, sem, sb, pb, "gat", lambda h: wg[:, h, :], 16, keep_rows, keep_T=g["xnT"])
            acc = t2("acc0", [P, T, HEADS, NE0 + 1])
            attention_scores0(nc, g, sem, rows, small, prod, acc, tab0)
            attend(nc, g, sem, sb, pb, "e0", g["list0"], tab0, g["group_tile0"], NG0, HEADS, W0, 16, SLOPE0, acc)
            route(nc, g, sem, sb, acc, small, gates)
        g["recycle"]()
        experts0(nc, A, g, sem, sb, pb, gates)
    with ExitStack() as sc:
        def t(name, shape, dt=F32):
            return sb(name, shape, dt, sc)
        acc = t("acc1", [P, T, D + 1])
        with ExitStack() as s2:
            def t2(name, shape, dt=F32):
                return sb(name, shape, dt, s2)
            wl, bl = t2("W_layer", [P, H2, D]), t2("b_layer", [P, D])
            wa, ba = t2("w_a12", [P, 2, D]), t2("b_a", [P, 2])
            row = t2("rows1", [P, 3 * TT + 1, W1R])
            load_small(nc, sem, [(wl[:], A["W_layer"].rearrange("(h p) f -> p h f", p=P)), (bl[:], A["b_layer"].partition_broadcast(P)),
                                 (wa[:, 0, :], A["w_a1"].rearrange("a b -> (a b)").partition_broadcast(P)),
                                 (wa[:, 1, :], A["w_a2"].rearrange("a b -> (a b)").partition_broadcast(P)),
                                 (ba[:, 0:1], A["b_a1"].partition_broadcast(P)), (ba[:, 1:2], A["b_a2"].partition_broadcast(P))], "layer")
            layernorm(nc, g, sem, sb, "n2")
            g["scope"] = s2
            table1(nc, g, sem, sb, pb, wl, bl, wa, ba, row, acc, tab1)
        attend(nc, g, sem, sb, pb, "e1", g["list1"], tab1, g["group_tile1"], NG1, 1, W1R, D + 1, SLOPE1, acc)
        finish1(nc, g, sem, sb, acc)
    g["recycle"]()
    layernorm(nc, g, sem, sb, "n3")
    moe(nc, A, g, sem, sb, pb, out)


def load_small(nc, sem, pairs, tag):
    s = sem(tag + "_weights_loaded")
    with nc.Block() as block:
        @block.sync
        def _(sp):
            for dst, src in pairs:
                sp.dma_start(dst, src).then_inc(s, 16)
            sp.wait_ge(s, 16 * len(pairs))


def transpose_rotation(nc, g, sem, pb, MT):
    s, d = sem("rotation_turned"), sem("rotation_kept")
    with ExitStack() as sc:
        ps = pb("turn_ps", [P, H2, D], sc)
        with nc.Block() as block:
            @block.tensor
            def _(pe):
                for a in range(H2):
                    for b in range(H2):
                        ins = nc.tensor.transpose(ps[:, b, a * P:(a + 1) * P], g["rot"][:, a, b * P:(b + 1) * P], g["ident"][:])
                ins.then_inc(s, 1)

            @block.vector
            def _(dve):
                dve.wait_ge(s, 1)
                nc.vector.tensor_copy(MT[:], ps[:]).then_inc(d, 1)
                dve.wait_ge(d, 1)


def move(nc, dst, src):
    return nc.vector.tensor_scalar(dst, src, 1.0, None, ALU.mult)


def one(a, i, k):
    v = a[:, bass.ds(i * TT + k, 1)]
    return v.rearrange("p a d -> p (a d)") if len(a.shape) == 3 else v


def layernorm(nc, g, sem, sb, tag):
    c_, rooted = sem(tag + "_step"), sem(tag + "_rooted")
    x, mv, rstd = g["x"], g["mv"], g["rstd"]
    with ExitStack() as sc:
        st = sb(tag + "_stats", [P, T, 6], F32, sc)
        with nc.Block() as block:
            @block.vector
            def _(dve):
                c = Count(c_)

                def link(ins):
                    dve.wait_ge(c.sem, c.mark(ins))
                with dve.Fori(0, NTT) as i:
                    c.enter(i, TT)
                    for k in range(TT):
                        c.mark(nc.vector.bn_stats(one(st, i, k), one(x, i, k)))
                    c.leave(NTT)
                dve.wait_ge(c.sem, c.value())
                for k in range(T):
                    c.mark(nc.vector.bn_aggr(mv[:, k, :], st[:, k, :]))
                dve.wait_ge(c.sem, c.value())
                link(nc.vector.tensor_scalar(rstd[:], mv[:, :, 1], EPS, None, ALU.add))
                dve.wait_ge(rooted, 1)
                link(nc.vector.reciprocal(rstd[:], rstd[:]))

            @block.scalar
            def _(act):
                act.wait_ge(c_, 2 * T + 1)
                nc.scalar.sqrt(rstd[:], rstd[:]).then_inc(rooted, 1)


def project(nc, g, sem, sb, pb, tag, weight, width, use, keep_T=None, keep_x=None, per_use=1, rows_out=None, start=None):
    normed, turned, kept, made, used, persisted, step = (
        sem(f"{tag}_{k}") for k in ("normed", "turned", "kept", "made", "used", "persisted", "step"))
    with ExitStack() as sc:
        xs = sb(tag + "_xn", [P, TT, D], F32, sc)
        xt = sb(tag + "_xnT_tile", [P, TT, H2, P], F32, sc)
        pt = pb(tag + "_pt", [P, 2, 512], sc)
        py = pb(tag + "_py", [P, 2, 512], sc)
        with nc.Block() as block:
            if rows_out:
                rows_out(block, used)

            @block.tensor
            def _(pe):
                pe.sem_inc(kept, 1)
                pe.sem_inc(used, 1)
                with pe.Fori(0, NTT) as i:
                    def turn_tile(k):
                        pe.wait_ge(normed, i * TT + (k + 1))
                        if k != 1:
                            pe.wait_ge(kept, i * TT + (max(k - 1, 0) + 1))
                        for h in range(H2):
                            ins = nc.tensor.transpose(pt[:, k % 2, h * P:(h + 1) * P], xs[:, k, h * P:(h + 1) * P], g["ident"][:])
                        ins.then_inc(turned, 1)

                    def multiply_tile(k):
                        pe.wait_ge(kept, i * TT + (k + 2))
                        if k != 1:
                            pe.wait_ge(used, i * (TT * per_use) + (max(k - 1, 0) * per_use + 1))
                        for h in range(H2):
                            ins = nc.tensor.matmul(py[:, k % 2, 0:width], xt[:, k, h, :], weight(h), start=(h == 0), stop=(h == H2 - 1))
                        ins.then_inc(made, 1)

                    turn_tile(0)
                    turn_tile(1)
                    for k in range(TT):
                        multiply_tile(k)
                        if k + 2 < TT:
                            turn_tile(k + 2)

            @block.scalar
            def _(act):
                with act.Fori(0, NTT) as i:
                    for k in range(TT):
                        act.wait_ge(turned, i * TT + (k + 1))
                        nc.scalar.copy(xt[:, k].rearrange("p h c -> p (h c)"), pt[:, k % 2, 0:D]).then_inc(kept, 1)
                        if keep_T is not None:
                            act.wait_ge(kept, i * TT + (k + 2))
                            nc.scalar.copy(keep_T[:, :, bass.ds((i * TT + k) * P, P)], xt[:, k]).then_inc(persisted, 1)
                    if keep_T is not None:
                        act.wait_ge(persisted, i * TT + TT)

            @block.vector
            def _(dve):
                n, m, u, st = (Count(c) for c in (normed, made, used, step))
                if start:
                    start(dve)
                with dve.Fori(0, NTT) as i:
                    for c in (n, m):
                        c.enter(i, TT)
                    u.n = 1
                    u.enter(i, TT * per_use)
                    for k in range(TT):
                        args = (one(g["x"], i, k), g["mv"][:, bass.ds(i * TT + k, 1), 0], one(g["rstd"], i, k), ALU.subtract, ALU.mult)
                        n.mark(nc.vector.tensor_scalar(xs[:, k, :], *args))
                        if keep_x is not None:
                            nc.vector.tensor_scalar(one(keep_x, i, k), *args).then_inc(step, 1)
                    if keep_x is not None:
                        dve.wait_ge(step, i * TT + TT)
                    for k in range(TT):
                        m.n += 1
                        dve.wait_ge(m.sem, m.value())
                        use(dve, i, k, py[:, k % 2, 0:width], u)
                    dve.wait_ge(u.sem, u.value())


def gather_columns(a, n):
    return a


def attention_scores0(nc, g, sem, rows, small, prod, acc, tab0):
    c_, out_ = sem("scores0_step"), sem("rows0_written")
    with nc.Block() as block:
        @block.vector
        def _(dve):
            c = Count(c_)

            def link(ins):
                dve.wait_ge(c.sem, c.mark(ins))
            h = rows[:, :, 0:16]
            for k, dst in enumerate((g["a_src"], g["a_dst"])):
                link(nc.vector.tensor_tensor(prod[:], h, small[:, k, :].unsqueeze(1).broadcast_to([P, T, 16]), ALU.mult))
                link(nc.vector.tensor_reduce(dst[:], prod[:].rearrange("p t (h e) -> p t h e", e=NE0), X, ALU.add))
            link(nc.vector.tensor_copy(rows[:, :, 16:20], g["a_src"][:]))
            link(nc.vector.tensor_copy(acc[:, :, :, 0:NE0], h.rearrange("p t (h e) -> p t h e", e=NE0)))
            link(nc.vector.memset(acc[:, :, :, NE0:NE0 + 1], 1.0))
            nc.vector.memset(prod[:], 0.0).then_inc(c_, 1)

        @block.sync
        def _(sp):
            sp.wait_ge(c_, 8)
            sp.dma_start(tab0[0:NFULL * P, :].rearrange("(t p) d -> p t d", p=P), rows[:, 0:NFULL, :]).then_inc(out_, 16)
            sp.dma_start(tab0[NFULL * P:N, :], rows[0:NREST, NFULL, :]).then_inc(out_, 16)
            sp.dma_start(tab0[N:N + 1, :], prod[0:1, 0:2, :].rearrange("p a b -> p (a b)")[:, 0:W0]).then_inc(out_, 16)
            sp.wait_ge(out_, 48)


def attend(nc, g, sem, sb, pb, tag, edges, table, group_tile, NG, HN, W, acol, slope, acc):
    names = ("list_padded", "list_loaded", "index_staged", "index_ok", "rows_in_0", "rows_in_1", "rows_in_2", "rows_in_3",
             "rows_used", "onehot_ready", "neg_ready", "onehot_turned", "onehot_T_ready", "step", "scores_ready_0",
             "scores_ready_1", "scores_read_0", "scores_read_1", "target_ready", "target_in", "factor_in", "factor_out",
             "weight_in", "weight_out", "message_ready", "sum_ready")
    s = {k: sem(f"{tag}_{k}") for k in names}
    AW = NE0 + 1 if HN > 1 else D + 1
    NM = HN * AW
    NB = NG * G
    GH = G // 2
    with ExitStack() as sc:
        def t(name, shape, dt=F32):
            return sb(f"{tag}_{name}", shape, dt, sc)
        ed = t("edges", [P, NB + 2 * G, 2])
        idx = t("index", [P, NBUF, G], I32)
        rows = t("rows", [P, NBUF, G, W])
        E = t("onehot", [P, NBUF, G, P])
        NEG = t("not_target", [P, NBUF, G, P], BF16)
        ET = t("onehot_T", [P, NBUF, G, P])
        EW = t("onehot_weighted", [P, G, P])
        mg = t("half_max", [P, 2, HN])
        mn, mx = t("new_max", [P, HN]), t("group_max", [P, HN])
        fd, fac = t("max_change", [P, NBUF, HN]), t("factor", [P, NBUF, HN])
        tm = t("target_and_max", [P, 2, HN])
        v, v2, w = (t(n, [P, G, HN]) for n in ("score", "score2", "weight"))
        msg = t("message", [P, G, HN, NE0 + 1])
        top, act_top = t("top", [P, T, HN]), t("top_act", [P, T, HN])
        tmp = t("scaled", [P, HN, AW if HN > 1 else 1])
        consts = t("consts", [P, 2])
        HB = max(512, GH * HN * P)
        ps_flat = pb(tag + "_scores", [P, 2, HB], sc)
        ps = [ps_flat[:, a, 0:GH * HN * P].rearrange("p (g h e) -> p g h e", g=GH, h=HN) for a in range(2)]
        pe8_bank = pb(tag + "_at_edge", [P, 512], sc)
        pe8 = pe8_bank[:, 0:G * 2 * HN].rearrange("p (g h) -> p g h", g=G)
        psum_ = pb(tag + "_sum", [P, 512], sc)
        pt_bank = sc.enter_context(nc.psum_tensor(tag + "_turned", [P, 2 * 512], BF16))
        pt = pt_bank[:, 0:G * P].rearrange("p (g e) -> p g e", g=G)
        a_dst = g["a_dst"] if HN > 1 else g["a1"]
        turns = NG // NBUF
        with nc.Block() as block:
            @block.sync
            def _(sp):
                sp.dma_start(ed[:, 0:NB, :], edges.rearrange("(p b) k -> p b k", p=P)).then_inc(s["list_loaded"], 16)
                sp.wait_ge(s["list_loaded"], 16)

            @block.gpsimd
            def _(pool):
                nc.gpsimd.memset(ed[:, NB:, 0].bitcast(I32), N).then_inc(s["list_padded"], 1)
                nc.gpsimd.memset(ed[:, NB:, 1], -1.0).then_inc(s["list_padded"], 1)
                pool.wait_ge(s["list_padded"], 2)
                pool.wait_ge(s["list_loaded"], 16)
                pool.sem_inc(s["rows_used"], NBUF)

                def gather(i, b):
                    grp = i * NBUF + b
                    pool.wait_ge(s["rows_used"], grp + 1)
                    pool.sem_inc(s["index_ok"], 1)
                    cols = slice(grp * G, grp * G + G) if isinstance(grp, int) else bass.ds(grp * G, G)
                    nc.gpsimd.tensor_copy(idx[:, b, :], ed[:, cols, 0].bitcast(I32)).then_inc(s["index_staged"], 1)
                    pool.wait_ge(s["index_staged"], grp + 1)
                    pool.sem_inc(s["index_ok"], 1)
                    for k in range(G):
                        nc.gpsimd.indirect_dma_start(rows[:, b, k, :], None, table[:, :],
                                                     bass.IndirectOffsetOnAxis(ap=idx[:, b, k:k + 1], axis=0)).then_inc(s[f"rows_in_{b}"], 16)

                with pool.Fori(0, turns) as i:
                    for b in range(NBUF):
                        gather(i, b)
                gather(turns, 0)

            @block.scalar
            def _(act):
                act.wait_ge(s["step"], 2)

                def masks(i, b):
                    c = b % NBUF
                    act.wait_ge(s["onehot_ready"], i * NBUF + (b + 1))
                    nc.scalar.activation(NEG[:, c], E[:, c], ACT.Identity, bias=consts[:, 0:1], scale=BIG).then_inc(s["neg_ready"], 1)
                    act.wait_ge(s["onehot_turned"], i * NBUF + (b + 1))
                    nc.scalar.activation(ET[:, c], pt, ACT.Identity, bias=consts[:, 1:2], scale=1.0 / BIG).then_inc(s["onehot_T_ready"], 1)

                masks(0, 0)
                masks(0, 1)
                with act.Fori(0, turns) as i:
                    for b in range(NBUF):
                        act.wait_ge(s["factor_in"], i * NBUF + (b + 1))
                        nc.scalar.activation(fac[:, b], fd[:, b], ACT.Exp).then_inc(s["factor_out"], 1)
                        act.wait_ge(s["weight_in"], i * NBUF + (b + 1))
                        nc.scalar.activation(w[:], v[:], ACT.Exp).then_inc(s["weight_out"], 1)
                        masks(i, b + 2)

            @block.vector
            def _(dve):
                c = Count(s["step"])

                def link(ins):
                    dve.wait_ge(c.sem, c.mark(ins))
                link(nc.vector.memset(consts[:, 0:1], -BIG))
                link(nc.vector.memset(consts[:, 1:2], 1.0))
                if HN > 1:
                    link(nc.vector.tensor_copy(top[:], g["a_src"][:]))
                    link(nc.vector.tensor_tensor(act_top[:], top[:], a_dst[:], ALU.add))
                else:
                    link(nc.vector.memset(top[:], -BIG))
                    link(nc.vector.memset(act_top[:], -BIG))
                    link(nc.vector.memset(acc[:], 0.0))
                link(nc.vector.scalar_tensor_tensor(act_top[:], act_top[:], slope, act_top[:], ALU.mult, ALU.max))
                dve.wait_ge(s["list_loaded"], 16)
                dve.wait_ge(s["list_padded"], 2)

                def onehots(i, b):
                    grp = i * NBUF + b
                    cols = slice(grp * G, grp * G + G) if isinstance(grp, int) else bass.ds(grp * G, G)
                    dl = ed[:, cols, 1].unsqueeze(2).broadcast_to([P, G, P])
                    nc.vector.tensor_tensor(E[:, b % NBUF], g["iota"][:, 0:P].unsqueeze(1).broadcast_to([P, G, P]), dl,
                                            ALU.is_equal).then_inc(s["onehot_ready"], 1)

                def tile_of(grp):
                    at = slice(grp, grp + 1) if isinstance(grp, int) else bass.ds(grp, 1)
                    return dve.value_load(group_tile[0:1, at], min_val=0, max_val=T - 1)

                def add_sum(i, b, tile):
                    grp = i * NBUF + b
                    f = fac[:, b % NBUF]
                    dve.wait_ge(s["factor_out"], grp + 1)
                    if HN > 1:
                        a4 = acc[:, bass.ds(tile, 1)].rearrange("p a h e -> p (a h) e")
                        link(nc.vector.tensor_tensor(tmp[:], a4, f.unsqueeze(2).broadcast_to([P, HN, AW]), ALU.mult))
                        dve.wait_ge(s["sum_ready"], grp + 1)
                        link(nc.vector.tensor_tensor(a4, tmp[:], psum_[:, 0:NM].rearrange("p (h e) -> p h e", e=AW), ALU.add))
                    else:
                        a1 = acc[:, bass.ds(tile, 1)].rearrange("p a h -> p (a h)")
                        dve.wait_ge(s["sum_ready"], grp + 1)
                        link(nc.vector.scalar_tensor_tensor(a1, a1, f, psum_[:, 0:NM], ALU.mult, ALU.add))
                    dve.sem_inc(s["rows_used"], 1)

                def step(i, b, first):
                    grp = i * NBUF + b
                    tile = tile_of(grp)
                    before = tile_of(grp - 1) if not first else None
                    at = lambda a: a[:, bass.ds(tile, 1)].rearrange("p a h -> p (a h)")
                    c.mark(move(nc, tm[:, 0, :], at(a_dst)))
                    for a in range(2):
                        dve.wait_ge(s[f"scores_ready_{a}"], grp + 1)
                        nc.vector.tensor_reduce(mg[:, a, :], ps[a].rearrange("p g h e -> p h g e"), XY, ALU.max).then_inc(s[f"scores_read_{a}"], 1)
                    for a in range(2):
                        dve.wait_ge(s[f"scores_read_{a}"], grp + 1)
                    link(nc.vector.tensor_tensor(mx[:], mg[:, 0, :], mg[:, 1, :], ALU.max))
                    link(nc.vector.tensor_tensor(at(top), mx[:], at(top), ALU.max))
                    link(nc.vector.tensor_tensor(mn[:], at(top), tm[:, 0, :], ALU.add))
                    nc.vector.scalar_tensor_tensor(tm[:, 1, :], mn[:], slope, mn[:], ALU.mult, ALU.max).then_inc(s["target_ready"], 1)
                    dve.wait_ge(s["target_ready"], grp + 1)
                    nc.vector.tensor_tensor(fd[:, b], at(act_top), tm[:, 1, :], ALU.subtract).then_inc(s["factor_in"], 1)
                    dve.wait_ge(s["factor_in"], grp + 1)
                    c.mark(move(nc, at(act_top), tm[:, 1, :]))
                    if first:
                        dve.sem_inc(c.sem, 2 if HN > 1 else 1)
                        c.n += 2 if HN > 1 else 1
                    else:
                        add_sum(i, b - 1, before)
                    dve.wait_ge(s["target_in"], grp + 1)
                    link(nc.vector.tensor_tensor(v2[:], rows[:, b, :, acol:acol + HN], pe8[:, :, 0:HN], ALU.add))
                    link(nc.vector.scalar_tensor_tensor(v2[:], v2[:], slope, v2[:], ALU.mult, ALU.max))
                    nc.vector.tensor_tensor(v[:], v2[:], pe8[:, :, HN:2 * HN], ALU.subtract).then_inc(s["weight_in"], 1)
                    onehots(i, b + 2)
                    dve.wait_ge(s["weight_out"], grp + 1)
                    if HN > 1:
                        c.mark(nc.vector.tensor_tensor(msg[:, :, :, 0:NE0], rows[:, b, :, 0:HN * NE0].rearrange("p g (h e) -> p g h e", e=NE0),
                                                       w[:].unsqueeze(3).broadcast_to([P, G, HN, NE0]), ALU.mult))
                        link(nc.vector.tensor_copy(msg[:, :, :, NE0], w[:]))
                    else:
                        c.mark(nc.vector.tensor_tensor(EW[:], E[:, b], w[:].broadcast_to([P, G, P]), ALU.mult))
                        dve.wait_ge(c.sem, c.value())
                    dve.sem_inc(s["message_ready"], 1)

                onehots(0, 0)
                onehots(0, 1)
                start = c.n
                for b in range(NBUF):
                    step(0, b, b == 0)
                per = c.n - start
                with dve.Fori(1, turns) as i:
                    c.enter(i - 1, per)
                    for b in range(NBUF):
                        step(i, b, False)
                    c.leave(turns - 1)
                add_sum(turns - 1, NBUF - 1, tile_of(NG - 1))

            @block.tensor
            def _(pe):
                def scores(i, b, a):
                    c = b % NBUF
                    for k in range(GH):
                        blk = a * GH + k
                        for h in range(HN):
                            nc.tensor.matmul(ps[a][:, k, h, :], rows[:, c, blk, acol + h:acol + h + 1].broadcast_to([P, P]), g["ident"][:], start=True, stop=False)
                            ins = nc.tensor.matmul(ps[a][:, k, h, :], NEG[:, c, blk, :], g["identb"][:], start=False, stop=True)
                    ins.then_inc(s[f"scores_ready_{a}"], 1)

                def turn_onehots(i, b):
                    c = b % NBUF
                    grp = i * NBUF + b
                    pe.wait_ge(s["neg_ready"], grp + 1)
                    if b or not isinstance(i, int):
                        pe.wait_ge(s["onehot_T_ready"], grp)
                    for k in range(G):
                        ins = nc.tensor.transpose(pt[:, k, :], NEG[:, c, k, :], g["identb"][:])
                    ins.then_inc(s["onehot_turned"], 1)

                turn_onehots(0, 0)
                turn_onehots(0, 1)
                pe.wait_ge(s["rows_in_0"], 16 * G)
                for a in range(2):
                    scores(0, 0, a)
                with pe.Fori(0, turns) as i:
                    for b in range(NBUF):
                        grp = i * NBUF + b
                        nb = (b + 1) % NBUF
                        pe.wait_ge(s[f"rows_in_{nb}"], i * (16 * G) + (16 * G * (1 + (b + 1) // NBUF)))
                        pe.wait_ge(s["scores_read_0"], grp + 1)
                        scores(i, b + 1, 0)
                        pe.wait_ge(s["target_ready"], grp + 1)
                        for k in range(G):
                            ins = nc.tensor.matmul(pe8[:, k, :], ET[:, b, k, :], tm[:].rearrange("p a h -> p (a h)"), start=True, stop=True)
                        ins.then_inc(s["target_in"], 1)
                        pe.wait_ge(s["scores_read_1"], grp + 1)
                        scores(i, b + 1, 1)
                        pe.wait_ge(s["message_ready"], grp + 1)
                        for k in range(G):
                            ins = nc.tensor.matmul(psum_[:, 0:NM], E[:, b, k, :] if HN > 1 else EW[:, k, :],
                                                   msg[:, k].rearrange("p h e -> p (h e)") if HN > 1 else rows[:, b, k, 0:NM], start=(k == 0), stop=(k == G - 1))
                        ins.then_inc(s["sum_ready"], 1)
                        turn_onehots(i, b + 2)


def route(nc, g, sem, sb, acc, small, gates):
    c_, a_ = sem("route_step"), sem("route_act")
    with ExitStack() as sc:
        def t(name, shape):
            return sb("route_" + name, shape, F32, sc)
        agg, inv, m, sq = t("agg", [P, T, 16]), t("inv", [P, T, HEADS]), t("mean", [P, T]), t("sq", [P, T, 16])
        sco, cnt, cmp_, top, e = t("score", [P, T, NE0]), t("above", [P, T, NE0]), t("cmp", [P, T]), t("top", [P, T]), t("exp", [P, T, NE0])
        with nc.Block() as block:
            @block.vector
            def _(dve):
                c = Count(c_)

                def link(ins):
                    dve.wait_ge(c.sem, c.mark(ins))
                bc = lambda a, n: a.unsqueeze(2).broadcast_to([P, T, n])
                row = lambda k: small[:, k, :].unsqueeze(1).broadcast_to([P, T, 16])
                link(nc.vector.tensor_scalar(inv[:], acc[:, :, :, NE0], 1e-16, None, ALU.add))
                link(nc.vector.reciprocal(inv[:], inv[:]))
                link(nc.vector.tensor_tensor(agg[:].rearrange("p t (h e) -> p t h e", e=NE0), acc[:, :, :, 0:NE0],
                                             inv[:].unsqueeze(3).broadcast_to([P, T, HEADS, NE0]), ALU.mult))
                link(nc.vector.tensor_tensor(agg[:], agg[:], row(2), ALU.add))
                link(nc.vector.tensor_reduce(m[:], agg[:], X, ALU.add))
                link(nc.vector.tensor_scalar(m[:], m[:], 1.0 / 16, None, ALU.mult))
                link(nc.vector.tensor_tensor(agg[:], agg[:], bc(m[:], 16), ALU.subtract))
                link(nc.vector.tensor_tensor(sq[:], agg[:], agg[:], ALU.mult))
                link(nc.vector.tensor_reduce(m[:], sq[:], X, ALU.add))
                link(nc.vector.tensor_scalar(m[:], m[:], 1.0 / 16, EPS, ALU.mult, ALU.add))
                dve.sem_inc(a_, 1)
                dve.wait_ge(a_, 2)
                link(nc.vector.reciprocal(m[:], m[:]))
                link(nc.vector.tensor_tensor(agg[:], agg[:], bc(m[:], 16), ALU.mult))
                link(nc.vector.tensor_tensor(agg[:], agg[:], row(3), ALU.mult))
                link(nc.vector.tensor_tensor(agg[:], agg[:], row(4), ALU.add))
                link(nc.vector.tensor_reduce(sco[:], agg[:].rearrange("p t (h e) -> p t e h", e=NE0), X, ALU.add))
                link(nc.vector.tensor_scalar(sco[:], sco[:], 1.0 / HEADS, None, ALU.mult))
                link(nc.vector.tensor_reduce(top[:], sco[:], X, ALU.max))
                link(nc.vector.tensor_tensor(e[:], sco[:], bc(top[:], NE0), ALU.subtract))
                dve.sem_inc(a_, 1)
                link(nc.vector.memset(cnt[:], 0.0))
                for a in range(NE0):
                    for b in range(NE0):
                        if a != b:
                            link(nc.vector.tensor_tensor(cmp_[:], sco[:, :, b], sco[:, :, a], ALU.is_ge if b < a else ALU.is_gt))
                            link(nc.vector.tensor_tensor(cnt[:, :, a], cnt[:, :, a], cmp_[:], ALU.add))
                dve.wait_ge(a_, 4)
                link(nc.vector.scalar_tensor_tensor(e[:], cnt[:], 2.0, e[:], ALU.is_lt, ALU.mult))
                link(nc.vector.tensor_reduce(m[:], e[:], X, ALU.add))
                link(nc.vector.reciprocal(m[:], m[:]))
                link(nc.vector.tensor_tensor(gates[:], e[:], bc(m[:], NE0), ALU.mult))

            @block.scalar
            def _(act):
                act.wait_ge(a_, 1)
                nc.scalar.sqrt(m[:], m[:]).then_inc(a_, 1)
                act.wait_ge(a_, 3)
                nc.scalar.activation(e[:], e[:], ACT.Exp).then_inc(a_, 1)


def experts0(nc, A, g, sem, sb, pb, gates):
    s = {k: sem("ex0_" + k) for k in ("loaded", "up_ready", "hidden_ready", "down_ready", "added")}
    FT, HALF = F0 // P, TT * P // 2
    with ExitStack() as sc:
        def t(name, shape, dt=F32):
            return sb("ex0_" + name, shape, dt, sc)
        W1, W2 = t("W1", [P, NE0, H2, F0]), t("W2", [P, NE0, FT, D])
        b1, b2 = t("b1", [P, NE0 * FT]), t("b2", [1, NE0, D])
        hid = t("hidden", [P, 2, FT, TT * P])
        up = pb("ex0_up", [P, 2, 2, 512], sc)
        dn = pb("ex0_down", [P, 2, 512], sc)
        with nc.Block() as block:
            @block.sync
            def _(sp):
                for e in range(NE0):
                    sp.dma_start(W1[:, e], A["W1"][e].rearrange("(h p) f -> p h f", p=P)).then_inc(s["loaded"], 16)
                    sp.dma_start(W2[:, e], A["W2"][e].rearrange("(f p) d -> p f d", p=P)).then_inc(s["loaded"], 16)
                sp.dma_start(b1[:], A["b1"]).then_inc(s["loaded"], 16)
                sp.dma_start(b2[:], A["b2"].rearrange("(a e) d -> a e d", a=1)).then_inc(s["loaded"], 16)
                sp.wait_ge(s["loaded"], 16 * (2 * NE0 + 2))

            @block.tensor
            def _(pe):
                U, Hd, Dn, Ad = (Count(s[k]) for k in ("up_ready", "hidden_ready", "down_ready", "added"))
                pe.wait_ge(s["loaded"], 16 * (2 * NE0 + 2))
                nu, nd = NE0 * FT, NE0 * TT
                with pe.Fori(0, NTT) as i:
                    def up_(e):
                        for f in range(FT):
                            pe.wait_ge(Hd.sem, i * nu + (e * FT + f + 1))
                            for n in range(2):
                                for h in range(H2):
                                    ins = nc.tensor.matmul(up[:, f % 2, n, 0:HALF], W1[:, e, h, f * P:(f + 1) * P],
                                                           g["xnT"][:, h, bass.ds(i * (TT * P) + n * HALF, HALF)], start=(h == 0), stop=(h == 1))
                            ins.then_inc(U.sem, 1)

                    def down_(e):
                        pe.wait_ge(Hd.sem, i * nu + ((e + 1) * FT + 2))
                        for k in range(TT):
                            n = e * TT + k
                            pe.wait_ge(Ad.sem, i * nd + n + 1)
                            for f in range(FT):
                                nc.tensor.matmul(dn[:, n % 2, 0:D], hid[:, e % 2, f, k * P:(k + 1) * P], W2[:, e, f, :], start=(f == 0), stop=False)
                            nc.tensor.matmul(dn[:, n % 2, 0:D], g["ones"][0:1, :], b2[:, e, :], start=False, stop=True).then_inc(Dn.sem, 1)

                    up_(0)
                    for e in range(NE0):
                        if e + 1 < NE0:
                            up_(e + 1)
                        down_(e)

            @block.scalar
            def _(act):
                act.sem_inc(s["hidden_ready"], 2)
                act.wait_ge(s["loaded"], 16 * (2 * NE0 + 2))
                nu, nd = NE0 * FT, NE0 * TT
                act.sem_inc(s["down_ready"], TT)
                with act.Fori(0, NTT) as i:
                    for e in range(NE0):
                        act.wait_ge(s["down_ready"], i * nd + (e - 1) * TT + TT if e else i * nd + 0 + 1)
                        for f in range(FT):
                            act.wait_ge(s["up_ready"], i * nu + (e * FT + f + 1))
                            nc.scalar.activation(hid[:, e % 2, f, :].rearrange("p (n c) -> p n c", n=2), up[:, f % 2, :, 0:HALF],
                                                 ACT.Gelu, bias=b1[:, e * FT + f:e * FT + f + 1]).then_inc(s["hidden_ready"], 1)

            @block.vector
            def _(dve):
                dve.sem_inc(s["added"], 2)
                nd = NE0 * TT
                with dve.Fori(0, NTT) as i:
                    for e in range(NE0):
                        for k in range(TT):
                            n = e * TT + k
                            dve.wait_ge(s["down_ready"], i * nd + n + 1 + TT)
                            if e:
                                dve.wait_ge(s["added"], i * nd + n + 1 + 2 - TT)
                            tile = one(g["x"], i, k)
                            nc.vector.scalar_tensor_tensor(tile, dn[:, n % 2, 0:D], gates[:, bass.ds(i * TT + k, 1), e], tile,
                                                           ALU.mult, ALU.add).then_inc(s["added"], 1)
                dve.wait_ge(s["added"], NTT * nd + 2)


def table1(nc, g, sem, sb, pb, wl, bl, wa, ba, row, acc, tab1):
    out_, ready, zr = sem("rows1_out"), sem("rows1_ready"), sem("rows1_zero_ready")
    rows_s = sem("rows1_step")
    target = sb("rows1_target", [P, TT], F32, g["scope"])
    junk = row[:, TT:2 * TT, 0:D]

    def start(dve):
        nc.vector.memset(row[0:1, 2 * TT, :], 0.0).then_inc(zr, 1)
        nc.vector.memset(row[:, 0:TT, D:D + 1], 1.0).then_inc(zr, 1)
        dve.wait_ge(zr, 2)

    def use(dve, i, k, ps, used):
        if k == 0:
            dve.wait_ge(out_, i * (16 * TT) + 16)
        r = row[:, k, :]
        v = used.mark(nc.vector.tensor_tensor(r[:, 0:D], ps, bl[:], ALU.add))
        dve.wait_ge(used.sem, v)
        used.mark(nc.vector.tensor_tensor_reduce(junk[:, k, :], r[:, 0:D], wa[:, 1, :], 1.0, ba[:, 1:2], ALU.mult, ALU.add, r[:, D + 1:D + 2]))
        v = used.mark(nc.vector.tensor_tensor_reduce(row[:, 2 * TT + 1 + k, 0:D], r[:, 0:D], wa[:, 0, :], 1.0, ba[:, 0:1], ALU.mult, ALU.add,
                                                     target[:, k:k + 1]))
        if k == TT - 1:
            dve.wait_ge(used.sem, v)
            dve.sem_inc(ready, 1)
            move(nc, g["a1"][:, bass.ds(i * TT, TT), :].rearrange("p t a -> p (t a)"), target[:]).then_inc(rows_s, 1)
            dve.wait_ge(rows_s, i + 1)

    def rows_out(block, used):
        @block.sync
        def _(sp):
            sp.wait_ge(zr, 2)
            sp.dma_start(tab1[N:N + 1, :], row[0:1, 2 * TT, :]).then_inc(out_, 16)
            whole = NFULL // TT
            with sp.Fori(0, whole) as i:
                sp.wait_ge(ready, i + 1)
                for k in range(TT):
                    sp.dma_start(tab1[bass.ds((i * TT + k) * P, P), :], row[:, k, :]).then_inc(out_, 16)
            for i in range(whole, NTT):
                sp.wait_ge(ready, i + 1)
                for k in range(TT):
                    n0 = (i * TT + k) * P
                    n = min(P, N - n0)
                    sp.dma_start(tab1[n0:n0 + n, :], row[0:n, k, :]).then_inc(out_, 16)
            sp.wait_ge(out_, 16 * (T + 1))

    project(nc, g, sem, sb, pb, "layer", lambda h: wl[:, h, :], D, use, per_use=3, rows_out=rows_out, start=start)


def finish1(nc, g, sem, sb, acc):
    c_ = sem("finish1_step")
    with ExitStack() as sc:
        inv = sb("finish1_inv", [P, T], F32, sc)
        with nc.Block() as block:
            @block.vector
            def _(dve):
                c = Count(c_)

                def link(ins):
                    dve.wait_ge(c.sem, c.mark(ins))
                link(nc.vector.tensor_scalar(inv[:], acc[:, :, D], 1e-30, None, ALU.max))
                link(nc.vector.reciprocal(inv[:], inv[:]))
                with dve.Fori(0, NTT) as i:
                    for k in range(TT):
                        nc.vector.scalar_tensor_tensor(one(g["x"], i, k), one(acc, i, k)[:, 0:D], one(inv, i, k), one(g["x"], i, k),
                                                       ALU.mult, ALU.add).then_inc(c_, 1)
                dve.wait_ge(c_, 2 + T)


def moe(nc, A, g, sem, sb, pb, out):
    x, buf, ybuf = g["x"], nc.dram_tensor("expert_in", (NE1 * SLOTS, D), F32).ap(), nc.dram_tensor("expert_out", (NE1 * SLOTS, D), F32).ap()
    OUT = NE1 * SLOTS
    with ExitStack() as sc:
        def t(name, shape, dt=F32, where=sc):
            return sb("moe_" + name, shape, dt, where)
        slot, prob = t("slot", [P, T], I32), t("prob", [P, T])
        with ExitStack() as s2:
            xn = t("xn", [P, T, D], F32, s2)
            gw, gb = t("gate_w", [P, H2, NE1], F32, s2), t("gate_b", [P, NE1], F32, s2)
            lg = t("logits", [P, T, NE1], F32, s2)
            load_small(nc, sem, [(gw[:], A["gate_w"].rearrange("(h p) f -> p h f", p=P)), (gb[:], A["gate_b"].partition_broadcast(P))], "gate")

            def keep(dve, i, k, ps, used):
                used.mark(nc.vector.tensor_tensor(one(lg, i, k), ps, gb[:], ALU.add))
            project(nc, g, sem, sb, pb, "gate", lambda h: gw[:, h, :], NE1, keep, keep_x=xn)
            dispatch(nc, g, sem, sb, pb, lg, slot, prob, xn, buf, OUT)
        experts1(nc, A, g, sem, sb, pb, buf, ybuf)
        collect(nc, g, sem, sb, slot, prob, ybuf, OUT, out)


def dispatch(nc, g, sem, sb, pb, lg, slot, prob, xn, buf, OUT):
    c_, exp_in, exp_out, oh_ready, pre_ready, zeroed, cleared, slots, sent = (sem("dispatch_" + k) for k in (
        "step", "exp_in", "exp_out", "onehot_ready", "prefix_ready", "zero_ready", "cleared", "slots_ready", "sent"))
    with ExitStack() as sc:
        def t(name, shape, dt=F32):
            return sb("dispatch_" + name, shape, dt, sc)
        top, e, oh, taken, hit = t("top", [P, T]), t("exp", [P, T, NE1]), t("onehot", [P, T, NE1]), t("taken", [P, T]), t("hit", [P, T])
        pre, tot, inc, sl, base = t("prefix", [P, T, NE1]), t("totals", [P, T, NE1]), t("scan", [P, NE1, T]), t("slot_f", [P, T]), t("base", [P, NE1])
        sm, upto_ = t("sum", [P, T]), t("row_upto_column", [P, P])
        zero = t("zero", [P, 4 * D])
        ps = pb("dispatch_ps", [P, 2, 512], sc)
        bc = lambda a: a.unsqueeze(2).broadcast_to([P, T, NE1])
        with nc.Block() as block:
            @block.vector
            def _(dve):
                c = Count(c_)

                def link(ins):
                    dve.wait_ge(c.sem, c.mark(ins))
                nc.vector.memset(zero[:], 0.0).then_inc(zeroed, 1)
                link(nc.vector.tensor_scalar(upto_[:], g["iota"][:, 0:P], g["pidx"][:], None, ALU.is_ge))
                link(nc.vector.tensor_reduce(top[:], lg[:], X, ALU.max))
                link(nc.vector.tensor_tensor(e[:], lg[:], bc(top[:]), ALU.subtract))
                dve.sem_inc(exp_in, 1)
                dve.wait_ge(exp_out, 1)
                link(nc.vector.tensor_reduce(sm[:], e[:], X, ALU.add))
                link(nc.vector.reciprocal(sm[:], sm[:]))
                link(nc.vector.tensor_tensor(e[:], e[:], bc(sm[:]), ALU.mult))
                link(nc.vector.tensor_reduce(prob[:], e[:], X, ALU.max))
                link(nc.vector.memset(taken[:], 0.0))
                link(nc.vector.tensor_scalar(taken[:, T - 1:T], g["pidx"][:], float(NREST), None, ALU.is_ge))
                for k in range(NE1):
                    link(nc.vector.tensor_tensor(hit[:], e[:, :, k], prob[:], ALU.is_ge))
                    link(nc.vector.tensor_tensor(oh[:, :, k], hit[:], taken[:], ALU.is_gt))
                    link(nc.vector.tensor_tensor(taken[:], taken[:], oh[:, :, k], ALU.add))
                dve.sem_inc(oh_ready, 1)
                dve.wait_ge(pre_ready, 1)
                flat = lambda a: a[:].rearrange("p t e -> p (t e)")
                link(nc.vector.tensor_copy(flat(pre), ps[:, 0, 0:T * NE1]))
                link(nc.vector.tensor_copy(flat(tot), ps[:, 1, 0:T * NE1]))
                for k in range(NE1):
                    link(nc.vector.tensor_tensor_scan(inc[:, k, :], g["ones"][:, 0:T], tot[:, :, k], 0.0, ALU.mult, ALU.add))
                link(nc.vector.tensor_tensor(pre[:], pre[:], inc[:].rearrange("p e t -> p t e"), ALU.add))
                link(nc.vector.tensor_tensor(pre[:], pre[:], tot[:], ALU.subtract))
                link(nc.vector.tensor_tensor(pre[:], pre[:], oh[:], ALU.mult))
                link(nc.vector.tensor_reduce(sl[:], pre[:], X, ALU.add))
                link(nc.vector.tensor_scalar(base[:], g["iota"][:, 0:NE1], float(SLOTS), None, ALU.mult))
                link(nc.vector.tensor_tensor(e[:], oh[:], base[:].unsqueeze(1).broadcast_to([P, T, NE1]), ALU.mult))
                link(nc.vector.tensor_reduce(sm[:], e[:], X, ALU.add))
                link(nc.vector.tensor_tensor(sm[:], sm[:], sl[:], ALU.add))
                link(nc.vector.tensor_scalar(sm[:], sm[:], -1.0 - OUT, None, ALU.add))
                link(nc.vector.tensor_scalar(hit[:], sl[:], float(CAP), None, ALU.is_le))
                link(nc.vector.scalar_tensor_tensor(hit[:], sl[:], 0.0, hit[:], ALU.is_gt, ALU.mult))
                link(nc.vector.tensor_tensor(sm[:], sm[:], hit[:], ALU.mult))
                link(nc.vector.tensor_scalar(sm[:], sm[:], float(OUT), None, ALU.add))
                link(nc.vector.tensor_copy(slot[:], sm[:]))
                link(nc.vector.tensor_tensor(prob[:], prob[:], hit[:], ALU.mult))
                dve.sem_inc(slots, 1)

            @block.scalar
            def _(act):
                act.wait_ge(exp_in, 1)
                nc.scalar.activation(e[:], e[:], ACT.Exp).then_inc(exp_out, 1)

            @block.tensor
            def _(pe):
                pe.wait_ge(oh_ready, 1)
                flat = oh[:].rearrange("p t e -> p (t e)")
                nc.tensor.matmul(ps[:, 0, 0:T * NE1], upto_[:], flat, start=True, stop=True)
                nc.tensor.matmul(ps[:, 1, 0:T * NE1], g["ones"][:], flat, start=True, stop=True).then_inc(pre_ready, 1)

            @block.sync
            def _(sp):
                sp.wait_ge(zeroed, 1)
                for k in range(OUT // (4 * P)):
                    sp.dma_start(buf[k * 4 * P:(k + 1) * 4 * P, :].rearrange("(p a) d -> p (a d)", p=P), zero[:]).then_inc(cleared, 16)
                sp.wait_ge(cleared, 16 * (OUT // (4 * P)))

            @block.gpsimd
            def _(pool):
                pool.wait_ge(slots, 1)
                pool.wait_ge(cleared, 16 * (OUT // (4 * P)))
                for k in range(T):
                    nc.gpsimd.indirect_dma_start(buf[:, :], bass.IndirectOffsetOnAxis(ap=slot[:, k:k + 1], axis=0), xn[:, k, :], None,
                                                 bounds_check=OUT - 1, oob_is_err=False).then_inc(sent, 16)
                pool.wait_ge(sent, 16 * T)


def experts1(nc, A, g, sem, sb, pb, buf, ybuf):
    s = {k: sem("ex1_" + k) for k in ("in_a", "in_b", "bias_in", "turned", "turned_kept", "up_ready", "hidden_ready", "down_ready",
                                      "added", "out_a", "out_b", "w_free", "y_free")}
    KS, FT = SLOTS // P, F1 // P
    with ExitStack() as sc:
        def t(name, shape, dt=F32):
            return sb("ex1_" + name, shape, dt, sc)
        w1, w2 = t("w1", [P, 2, H2, F1]), t("w2", [P, 2, FT, D])
        xe, xT = t("x", [P, 2, KS, D]), t("xT", [P, H2, SLOTS])
        b1, b2 = t("b1", [P, NE1 * FT]), t("b2", [P, NE1, D])
        hid = t("hidden", [P, FT, SLOTS])
        y = t("y", [P, 2, KS, D])
        pt = pb("ex1_turn", [P, 2, 512], sc)
        up = pb("ex1_up", [P, 2, 512], sc)
        dn = pb("ex1_down", [P, 2, 512], sc)
        LOADS = 16 * 3
        with nc.Block() as block:
            @block.sync
            def _(sp):
                sp.dma_start(b1[:], A["b1m"]).then_inc(s["bias_in"], 16)
                sp.dma_start(b2[:], A["b2m"].partition_broadcast(P)).then_inc(s["bias_in"], 16)
                sp.sem_inc(s["w_free"], 2)
                for e in range(NE1):
                    b = e % 2
                    sp.wait_ge(s["w_free"], e + 1)
                    sp.dma_start(xe[:, b], buf[e * SLOTS:(e + 1) * SLOTS, :].rearrange("(k p) d -> p k d", p=P)).then_inc(s[f"in_{'ab'[b]}"], 16)
                    sp.dma_start(w1[:, b], A["w1"][e].rearrange("(h p) f -> p h f", p=P)).then_inc(s[f"in_{'ab'[b]}"], 16)
                    sp.dma_start(w2[:, b], A["w2"][e].rearrange("(f p) d -> p f d", p=P)).then_inc(s[f"in_{'ab'[b]}"], 16)

            @block.gpsimd
            def _(pool):
                for e in range(NE1):
                    pool.wait_ge(s["y_free"], e + 1)
                    pool.dma_start(ybuf[e * SLOTS:(e + 1) * SLOTS, :].rearrange("(k p) d -> p k d", p=P), y[:, e % 2]).then_inc(s[f"out_{'ab'[e % 2]}"], 16)
                for b in "ab":
                    pool.wait_ge(s["out_" + b], 16 * (NE1 // 2))

            @block.tensor
            def _(pe):
                pe.wait_ge(s["bias_in"], 32)
                for e in range(NE1):
                    b = e % 2
                    pe.wait_ge(s[f"in_{'ab'[b]}"], LOADS * (e // 2 + 1))
                    for h in range(H2):
                        if e:
                            pe.wait_ge(s["turned_kept"], H2 * e)
                        for k in range(KS):
                            ins = nc.tensor.transpose(pt[:, h, k * P:(k + 1) * P], xe[:, b, k, h * P:(h + 1) * P], g["ident"][:])
                        ins.then_inc(s["turned"], 1)
                    pe.wait_ge(s["turned_kept"], H2 * (e + 1))
                    for f in range(FT):
                        n = e * FT + f
                        if n >= 2:
                            pe.wait_ge(s["hidden_ready"], n - 1)
                        for h in range(H2):
                            ins = nc.tensor.matmul(up[:, f % 2, :], w1[:, b, h, f * P:(f + 1) * P], xT[:, h, :], start=(h == 0), stop=(h == 1))
                        ins.then_inc(s["up_ready"], 1)
                    pe.wait_ge(s["hidden_ready"], (e + 1) * FT)
                    for k in range(KS):
                        n = e * KS + k
                        if n >= 2:
                            pe.wait_ge(s["added"], n - 1)
                        for f in range(FT):
                            ins = nc.tensor.matmul(dn[:, k % 2, 0:D], hid[:, f, k * P:(k + 1) * P], w2[:, b, f, :], start=(f == 0), stop=(f == FT - 1))
                        ins.then_inc(s["down_ready"], 1)
                    pe.wait_ge(s["down_ready"], (e + 1) * KS)
                    pe.sem_inc(s["w_free"], 1)

            @block.scalar
            def _(act):
                act.wait_ge(s["bias_in"], 32)
                for e in range(NE1):
                    for h in range(H2):
                        act.wait_ge(s["turned"], H2 * e + h + 1)
                        nc.scalar.copy(xT[:, h, :], pt[:, h, :]).then_inc(s["turned_kept"], 1)
                    if e:
                        act.wait_ge(s["down_ready"], e * KS)
                    for f in range(FT):
                        n = e * FT + f
                        act.wait_ge(s["up_ready"], n + 1)
                        nc.scalar.activation(hid[:, f, :], up[:, f % 2, :], ACT.Relu, bias=b1[:, n:n + 1]).then_inc(s["hidden_ready"], 1)

            @block.vector
            def _(dve):
                dve.wait_ge(s["bias_in"], 32)
                for e in range(NE1):
                    if e >= 2:
                        dve.wait_ge(s[f"out_{'ab'[e % 2]}"], 16 * (e // 2))
                    for k in range(KS):
                        n = e * KS + k
                        dve.wait_ge(s["down_ready"], n + 1)
                        nc.vector.tensor_tensor(y[:, e % 2, k, :], dn[:, k % 2, 0:D], b2[:, e, :], ALU.add).then_inc(s["added"], 1)
                    dve.wait_ge(s["added"], (e + 1) * KS)
                    dve.sem_inc(s["y_free"], 1)


def collect(nc, g, sem, sb, slot, prob, ybuf, OUT, out):
    zeroed, got, c_, ready, done = (sem("collect_" + k) for k in ("zeroed", "rows_in", "step", "ready", "out"))
    x = g["x"]
    with ExitStack() as sc:
        def t(name, shape, dt=F32):
            return sb("collect_" + name, shape, dt, sc)
        y, m, lim = t("y", [P, T, D]), t("mask", [P, T, D]), t("limits", [P, 3])
        with nc.Block() as block:
            @block.vector
            def _(dve):
                c = Count(c_)

                def link(ins):
                    dve.wait_ge(c.sem, c.mark(ins))
                nc.vector.memset(y[:], 0.0).then_inc(zeroed, 1)
                for k, v in enumerate((0.0, 10000.0, -10000.0)):
                    link(nc.vector.memset(lim[:, k:k + 1], v))
                dve.wait_ge(got, 16 * T)
                bc = lambda a: a.unsqueeze(2).broadcast_to([P, T, D])
                link(nc.vector.tensor_tensor(y[:], y[:], bc(prob[:]), ALU.mult))
                flat = y[:].rearrange("p t d -> p (t d)")
                mf = m[:].rearrange("p t d -> p (t d)")
                big = 3.4028234e38
                for k, (op, v) in enumerate(((None, 0.0), (ALU.is_gt, big), (ALU.is_lt, -big))):
                    if op is None:
                        link(nc.vector.tensor_tensor(mf, flat, flat, ALU.not_equal))
                    else:
                        link(nc.vector.tensor_scalar(mf, flat, v, None, op))
                    link(nc.vector.copy_predicated(flat, mf.bitcast(I32), lim[:, k:k + 1].broadcast_to([P, T * D])))
                link(nc.vector.tensor_tensor(x[:], x[:], y[:], ALU.add))
                dve.sem_inc(ready, 1)

            @block.gpsimd
            def _(pool):
                pool.wait_ge(zeroed, 1)
                for k in range(T):
                    nc.gpsimd.indirect_dma_start(y[:, k, :], None, ybuf[:, :], bass.IndirectOffsetOnAxis(ap=slot[:, k:k + 1], axis=0),
                                                 bounds_check=OUT - 1, oob_is_err=False).then_inc(got, 16)

            @block.sync
            def _(sp):
                sp.wait_ge(ready, 1)
                sp.dma_start(out[0:NFULL * P, :].rearrange("(t p) d -> p t d", p=P), x[:, 0:NFULL, :]).then_inc(done, 16)
                sp.dma_start(out[NFULL * P:N, :], x[0:NREST, NFULL, :]).then_inc(done, 16)
                sp.wait_ge(done, 32)


_INS = {"x": "x", "src": "src", "dst": "dst", "w": "edge_weight", "W_gat": "L0_ffn_W_gat", "att_src": "L0_ffn_att_src",
        "att_dst": "L0_ffn_att_dst", "b_gat": "L0_ffn_b_gat", "ln_gamma": "L0_ffn_ln_gamma", "ln_beta": "L0_ffn_ln_beta",
        "W1": "L0_ffn_W1", "b1": "L0_ffn_b1", "W2": "L0_ffn_W2", "b2": "L0_ffn_b2", "ei": "L0_ffn_edge_index",
        "W_layer": "L1_gnn_W_layer", "b_layer": "L1_gnn_b_layer", "w_a1": "L1_gnn_w_a1", "b_a1": "L1_gnn_b_a1",
        "w_a2": "L1_gnn_w_a2", "b_a2": "L1_gnn_b_a2", "gate_w": "L1_ffn_gate_w", "gate_b": "L1_ffn_gate_b",
        "w1": "L1_ffn_w1", "b1m": "L1_ffn_b1", "w2": "L1_ffn_w2", "b2m": "L1_ffn_b2"}


def kernel(**inputs):
    import numpy as _np
    import concourse.bacc as _bacc
    from concourse import mybir as _mybir
    from concourse.bass_utils import run_bass_kernel_spmd as _run

    nc = _bacc.Bacc("TRN2", target_bir_lowering=False, num_devices=1)
    arrays, aps = {}, {}
    for short, name in _INS.items():
        a = _np.asarray(inputs[name])
        if short == "W_layer":
            a = a.T
        if short in ("b1", "b1m"):
            a = a.reshape(-1, P).T
        a = _np.ascontiguousarray(a)
        arrays[f"in_{short}"] = a
        aps[short] = nc.dram_tensor(f"in_{short}", a.shape, _mybir.dt.from_np(a.dtype), kind="ExternalInput").ap()
    out = nc.dram_tensor("out_0", (N, D), F32, kind="ExternalOutput").ap()
    build(nc, aps, out)
    r = _run(nc, [arrays], core_ids=[0])
    return r.results[0]["out_0"]
```

```python
from contextlib import ExitStack

import concourse.bass as bass
from concourse import mybir

F32 = mybir.dt.float32
BF16 = mybir.dt.bfloat16
I32 = mybir.dt.int32
I16 = mybir.dt.int16
ALU = mybir.AluOpType
ACT = mybir.ActivationFunctionType
X = mybir.AxisListType.X
XY = mybir.AxisListType.XY

P = 128
N = 3125
D = 256
H2 = D // P
T = -(-N // P)
NFULL = N // P
NREST = N - NFULL * P
EPS = 1e-5
BIG = 2.0 ** 100

G = 4
GE = G * P
E0 = 32768
E1 = 50000
NBUF = 4


def groups(edges):
    return -(-((edges + T * (GE - 1)) // GE) // NBUF) * NBUF


NG0, NG1 = groups(E0), groups(E1)

CH = P
NCH = -(-E1 // CH)
CB = -(-NCH // P)
OWN = P - 1
BU = 4
NTURN = -(-(2 * E1) // (OWN * BU))
PK = 4
LOTS = 2 * -(-NCH // (2 * PK))
WIN = 3
NF = 10
TWO_PI = 6.283185307179586
TWO_PI_HI = 6.28125
TWO_PI_LO = TWO_PI - TWO_PI_HI
PI_SAFE = 3.1415925
MAGIC = 1.5 * 2.0 ** 23


class Count:

    def __init__(self, sem):
        self.sem, self.n, self.turn, self.per = sem, 0, None, 0

    def mark(self, ins, by=1):
        ins.then_inc(self.sem, by)
        self.n += by
        return self.value()

    def value(self):
        return self.n if self.turn is None else self.turn * self.per + self.n

    def enter(self, turn, per):
        self.turn, self.per, self.start = turn, per, self.n

    def leave(self, turns):
        assert self.n - self.start == self.per, (self.n - self.start, self.per)
        self.n = self.start + self.per * turns
        self.turn = None


def build(nc, A, out):
    with ExitStack() as ctx:
        nsem = [0]

        def sb(name, shape, dt, where=ctx):
            return where.enter_context(nc.sbuf_tensor(name, shape, dt))

        def pb(name, shape, where):
            return where.enter_context(nc.psum_tensor(name, shape, F32))

        live = []

        def sem(name):
            live.append(nc.alloc_semaphore(name=name))
            return live[-1]

        def recycle():
            nc.all_engine_barrier()
            nc.clear_and_free_semaphores(list(live))
            nc.all_engine_barrier()
            live.clear()

        g = {"recycle": recycle}
        g["x"] = sb("x_nodes", [P, T, D], F32)
        g["iota"] = sb("iota_row", [P, WIN * P], F32)
        g["iota16"] = sb("iota_row16", [P, WIN * P], I16)
        g["pidx"] = sb("partition_index", [P, 1], F32)
        g["ident"] = sb("identity", [P, P], F32)
        g["identb"] = sb("identity_bf", [P, P], BF16)
        g["before"] = sb("row_before_column", [P, P], F32)
        g["ones"] = sb("ones", [P, P], F32)
        g["group_tile0"] = sb("group_tile0", [1, P], I32)
        g["group_tile1"] = sb("group_tile1", [1, P], I32)
        g["rot"] = sb("rotation_matrix", [P, H2, D], F32)
        g["list0"] = nc.dram_tensor("edges_by_tile0", (P * G * NG0, 2), F32).ap()
        g["list1"] = nc.dram_tensor("edges_by_tile1", (P * G * NG1, 2), F32).ap()
        g["window_dram"] = nc.dram_tensor("window_of_chunk", (CB * P,), I32).ap()
        constants(nc, A, g, sem)
        rotations(nc, A, g, sem, sb, pb)
        recycle()
        rest(nc, A, g, sem, sb, pb, out)


def constants(nc, A, g, sem):
    x_loaded, iota_done, const_done, zeroed = sem("x_loaded"), sem("iota_done"), sem("const_done"), sem("x_padding_zeroed")
    with nc.Block() as block:
        @block.sync
        def _(sp):
            sp.dma_start(g["x"][:, 0:NFULL, :], A["x"][0:NFULL * P, :].rearrange("(t p) d -> p t d", p=P)).then_inc(x_loaded, 16)
            sp.wait_ge(zeroed, 1)
            sp.dma_start(g["x"][0:NREST, NFULL, :], A["x"][NFULL * P:N, :]).then_inc(x_loaded, 16)
            sp.wait_ge(x_loaded, 32)

        @block.gpsimd
        def _(pool):
            nc.gpsimd.iota(g["iota"][:], [[1, WIN * P]], base=0, channel_multiplier=0,
                           allow_small_or_imprecise_dtypes=True).then_inc(iota_done, 1)
            nc.gpsimd.iota(g["iota16"][:], [[1, WIN * P]], base=0, channel_multiplier=0,
                           allow_small_or_imprecise_dtypes=True).then_inc(iota_done, 1)
            nc.gpsimd.iota(g["pidx"][:], [[0, 1]], base=0, channel_multiplier=1,
                           allow_small_or_imprecise_dtypes=True).then_inc(iota_done, 1)

        @block.vector
        def _(dve):
            nc.vector.memset(g["x"][:, NFULL, :], 0.0).then_inc(zeroed, 1)
            nc.vector.memset(g["ones"][:], 1.0).then_inc(const_done, 1)
            dve.wait_ge(iota_done, 3)
            row = g["iota"][:, 0:P]
            nc.vector.tensor_scalar(g["ident"][:], row, g["pidx"][:], None, ALU.is_equal).then_inc(const_done, 1)
            nc.vector.tensor_scalar(g["identb"][:], row, g["pidx"][:], None, ALU.is_equal).then_inc(const_done, 1)
            nc.vector.tensor_scalar(g["before"][:], row, g["pidx"][:], None, ALU.is_gt).then_inc(const_done, 1)


def rotations(nc, A, g, sem, sb, pb):
    with ExitStack() as sc:
        def t(name, shape, dt=F32):
            return sb(name, shape, dt, sc)

        lists = []
        for n, (rows, cols, key, other, ngroups) in enumerate((
                (P, E0 // P, A["ei"][1], A["ei"][0], NG0),
                (125, E1 // 125, A["src"], A["dst"], NG1))):
            lists.append(dict(
                n=n, R=rows, F=cols, key_in=key, other_in=other, NG=ngroups, NB=ngroups * G,
                key=t(f"key{n}", [rows, cols], I32), other=t(f"other{n}", [rows, cols], I32),
                tile=t(f"tile{n}", [rows, cols]), slot=t(f"slot{n}", [rows, cols], I32),
                rec=t(f"record{n}", [rows, cols, 2]), list=g[f"list{n}"], group_tile=g[f"group_tile{n}"]))
        FL = max(l["F"] for l in lists)
        tmp_i = t("tmp_i", [P, FL], I32)
        small = t("small", [P, 8, T])
        small_i = t("small_i", [P, T], I32)
        stage_rec = t("stage_rec", [P, 2, 8, 2])
        stage_slot = t("stage_slot", [P, 2, 8], I32)
        ia, ja = t("i_int", [P, CB, CH], I32), t("j_int", [P, CB, CH], I32)
        wa = t("w_a", [P, CB, CH])
        cs = t("chunk_small", [P, 8, CB])
        csi = t("chunk_small_i", [P, 2, CB], I32)
        window_row = t("window_row", [1, CB * P], I32)
        turns_i = t("turns_i", [1, 1], I32)
        NCOMP = BU * (NTURN + 2)
        fieldsB = {k: t("rB_" + k, [P, CB * CH]) for k in ("i", "j", "w", "q")}
        comp = t("terms", [P, NCOMP, NF])

        s = {k: sem(k) for k in (
            "edges0_loaded", "edges1_loaded", "rot_loaded", "rot_padded", "fill_ready", "list_filled", "dve_step", "totals_ready",
            "prefix_ready", "prefix_read", "slots_ready", "window_out",
            "window_in", "fieldsA_ready", "fieldsB_ready", "onehot_ready",
            "comp_zeroed")}
        block = nc.Block()
        with ExitStack() as inner:
            wk = ExitStack()
            mask = wk.enter_context(nc.sbuf_tensor("tile_mask", [P, T * FL], F32))
            scan = wk.enter_context(nc.sbuf_tensor("tile_scan", [P, T * FL], F32))
            fill = wk.enter_context(nc.sbuf_tensor("list_fill", [P, G * NG1, 2], F32))
            pre = pb("prefix_ps", [P, 512], wk)
            Fa = {k: wk.enter_context(nc.sbuf_tensor("rA_" + k, [P, CB, CH], F32)) for k in ("i", "j", "a", "b", "f", "scan", "q")}
            tp = wk.enter_context(nc.psum_tensor("fields_ps", [P, 4, CB * CH], F32))
            with nc.Block() as block:
                @block.sync
                def _(sp):
                    for l in lists:
                        sp.dma_start(l["key"][:], l["key_in"].rearrange("(p f) -> p f", p=l["R"])).then_inc(s[f"edges{l['n']}_loaded"], 16)
                        sp.dma_start(l["other"][:], l["other_in"].rearrange("(p f) -> p f", p=l["R"])).then_inc(s[f"edges{l['n']}_loaded"], 16)
                    sp.wait_ge(s["rot_padded"], 3)
                    full, last = E1 // (P * CH), E1 % CH
                    more = NCH - 1 - full * P
                    for tile_, src in ((ia, A["src"]), (ja, A["dst"]), (wa, A["w"])):
                        sp.dma_start(tile_[:, 0:full, :], src[0:full * P * CH].rearrange("(b p s) -> p b s", p=P, s=CH)).then_inc(s["rot_loaded"], 16)
                        sp.dma_start(tile_[0:more, full, :], src[full * P * CH:(NCH - 1) * CH].rearrange("(p s) -> p s", s=CH)).then_inc(s["rot_loaded"], 16)
                        sp.dma_start(tile_[more:more + 1, full, 0:last], src[(NCH - 1) * CH:E1].rearrange("(a s) -> a s", a=1)).then_inc(s["rot_loaded"], 16)
                    sp.wait_ge(s["fill_ready"], 2)
                    for l in lists:
                        sp.dma_start(l["list"].rearrange("(p c) k -> p c k", p=P), fill[:, 0:l["NB"], :]).then_inc(s["list_filled"], 16)
                    sp.wait_ge(s["window_out"], 1)
                    sp.dma_start(g["window_dram"].rearrange("(b p) -> p b", p=P), csi[:, 0, :], allow_slow_non_contiguous=True).then_inc(s["window_in"], 16)
                    sp.wait_ge(s["window_in"], 16)
                    sp.dma_start(window_row[:], g["window_dram"].rearrange("(a c) -> a c", a=1)).then_inc(s["window_in"], 16)
                    sp.wait_ge(s["window_in"], 32)
                    sp.wait_ge(s["list_filled"], 32)

                @block.gpsimd
                def _(pool):
                    nc.gpsimd.memset(ia[:], 99999).then_inc(s["rot_padded"], 1)
                    nc.gpsimd.memset(ja[:], 99999).then_inc(s["rot_padded"], 1)
                    nc.gpsimd.memset(wa[:], 0.0).then_inc(s["rot_padded"], 1)
                    nc.gpsimd.memset(fill[:, :, 0:1].bitcast(I32), N).then_inc(s["fill_ready"], 1)
                    nc.gpsimd.memset(fill[:, :, 1:2], -1.0).then_inc(s["fill_ready"], 1)
                    nc.gpsimd.memset(comp[:], 0.0).then_inc(s["comp_zeroed"], 1)
                    pool.wait_ge(s["comp_zeroed"], 1)

                @block.vector
                def _(dve):
                    c = Count(s["dve_step"])

                    def link(ins):
                        dve.wait_ge(c.sem, c.mark(ins))

                    for l in lists:
                        R, F, NB = l["R"], l["F"], l["NB"]
                        m3 = mask[0:R, 0:T * F].rearrange("p (b f) -> p b f", b=T)
                        s3 = scan[0:R, 0:T * F].rearrange("p (b f) -> p b f", b=T)
                        tot, cnt, ngr, gst, sta = (small[:, k, :] for k in range(5))
                        dve.wait_ge(s[f"edges{l['n']}_loaded"], 32)
                        link(nc.vector.tensor_single_scalar(tmp_i[0:R, 0:F], l["key"][:], 7, ALU.logical_shift_right))
                        link(nc.vector.tensor_copy(l["tile"][:], tmp_i[0:R, 0:F]))
                        link(nc.vector.tensor_single_scalar(tmp_i[0:R, 0:F], l["key"][:], P - 1, ALU.bitwise_and))
                        link(nc.vector.tensor_copy(l["rec"][:, :, 1], tmp_i[0:R, 0:F]))
                        link(nc.vector.tensor_copy(l["rec"][:, :, 0].bitcast(I32), l["other"][:]))
                        link(nc.vector.tensor_tensor(m3, l["tile"][:].unsqueeze(1).broadcast_to([R, T, F]),
                                                     g["iota"][0:R, 0:T].unsqueeze(2).broadcast_to([R, T, F]), ALU.is_equal))
                        link(nc.vector.tensor_tensor_scan(scan[0:R, 0:T * F], g["ones"][0:R, 0:1].broadcast_to([R, T * F]),
                                                          mask[0:R, 0:T * F], 0.0, ALU.mult, ALU.add))
                        link(nc.vector.tensor_copy(tot[0:R, 0:1], s3[:, 0, F - 1:F]))
                        nc.vector.tensor_tensor(tot[0:R, 1:T], s3[:, 1:T, F - 1], s3[:, 0:T - 1, F - 1], ALU.subtract).then_inc(s["totals_ready"], 1)
                        dve.wait_ge(s["prefix_ready"], 1 + 2 * l["n"])
                        link(nc.vector.tensor_scalar(cnt, pre[:, T:2 * T], float(GE - 1), None, ALU.add))
                        link(nc.vector.tensor_copy(small_i[:], cnt))
                        link(nc.vector.tensor_single_scalar(small_i[:], small_i[:], 9, ALU.logical_shift_right))
                        link(nc.vector.tensor_copy(ngr, small_i[:]))
                        link(nc.vector.tensor_tensor_scan(gst, g["ones"][:, 0:T], ngr, 0.0, ALU.mult, ALU.add))
                        link(nc.vector.tensor_tensor(gst, gst, ngr, ALU.subtract))
                        link(nc.vector.scalar_tensor_tensor(sta, gst, float(GE), pre[:, 0:T], ALU.mult, ALU.add))
                        link(nc.vector.tensor_tensor(sta[0:R], sta[0:R], tot[0:R], ALU.add))
                        link(nc.vector.tensor_tensor(sta[0:R], sta[0:R], s3[:, :, F - 1], ALU.subtract))
                        link(nc.vector.tensor_scalar(sta[0:R], sta[0:R], -1.0, None, ALU.add))
                        link(nc.vector.tensor_scalar(small[:, 5, 1:T], gst[:, 1:T], g["pidx"][:], None, ALU.is_le))
                        nc.vector.tensor_reduce(small[:, 6, 0:1], small[:, 5, 1:T], X, ALU.add).then_inc(s["totals_ready"], 1)
                        link(nc.vector.tensor_tensor(s3, s3, sta[0:R].unsqueeze(2).broadcast_to([R, T, F]), ALU.add))
                        link(nc.vector.tensor_tensor(s3, s3, m3, ALU.mult))
                        link(nc.vector.tensor_reduce(l["tile"][:], s3.rearrange("p b f -> p f b"), X, ALU.add))
                        link(nc.vector.tensor_copy(l["key"][:], l["tile"][:]))
                        link(nc.vector.tensor_single_scalar(tmp_i[0:R, 0:F], l["key"][:], P - 1, ALU.bitwise_and))
                        link(nc.vector.tensor_single_scalar(l["key"][:], l["key"][:], 7, ALU.logical_shift_right))
                        link(nc.vector.scalar_tensor_tensor(l["slot"][:], tmp_i[0:R, 0:F], float(NB), l["key"][:], ALU.mult, ALU.add))
                        dve.wait_ge(s["prefix_ready"], 2 + 2 * l["n"])
                        nc.vector.tensor_copy(l["group_tile"][:], pre[0:1, 64:64 + P]).then_inc(s["prefix_read"], 1)
                    flat = lambda a: a[:].rearrange("p b s -> p (b s)")
                    dve.wait_ge(s["rot_loaded"], 144)
                    fi, fj, aa, bb, ff, sc_, q = (flat(Fa[k]) for k in ("i", "j", "a", "b", "f", "scan", "q"))
                    link(nc.vector.tensor_copy(fi, flat(ia)))
                    link(nc.vector.tensor_copy(fj, flat(ja)))
                    link(nc.vector.tensor_tensor(aa, fi, fj, ALU.not_equal))
                    link(nc.vector.scalar_tensor_tensor(aa, fi, float(D), aa, ALU.is_lt, ALU.mult))
                    link(nc.vector.scalar_tensor_tensor(ff, fj, float(D), aa, ALU.is_lt, ALU.add))
                    for b in range(CB):
                        link(nc.vector.tensor_tensor_scan(Fa["scan"][:, b, :], g["ones"][:, 0:CH], Fa["f"][:, b, :], 0.0, ALU.mult, ALU.add))
                    nc.vector.tensor_copy(cs[:, 0, :], Fa["scan"][:, :, CH - 1]).then_inc(s["totals_ready"], 1)
                    dve.wait_ge(s["prefix_ready"], 5)
                    link(nc.vector.tensor_copy(cs[:, 7, :], pre[:, CB:2 * CB]))
                    link(nc.vector.tensor_tensor_scan(cs[:, 1, :], g["ones"][:, 0:CB], cs[:, 7, :], 0.0, ALU.mult, ALU.add))
                    link(nc.vector.tensor_tensor(cs[:, 2, :], cs[:, 1, :], cs[:, 7, :], ALU.subtract))
                    link(nc.vector.tensor_tensor(cs[:, 2, :], cs[:, 2, :], pre[:, 0:CB], ALU.add))

                    def whole(dst, src, by, plus):
                        link(nc.vector.tensor_scalar(dst, src, plus + 0.5, 1.0 / by, ALU.add, ALU.mult))
                        link(nc.vector.tensor_scalar(dst, dst, -0.5, None, ALU.add))
                        link(nc.vector.tensor_scalar(dst, dst, MAGIC, None, ALU.add))
                        link(nc.vector.tensor_scalar(dst, dst, -MAGIC, None, ALU.add))

                    whole(cs[:, 3, :], cs[:, 2, :], OWN, 0.0)
                    link(nc.vector.tensor_tensor(cs[:, 4, :], cs[:, 2, :], cs[:, 3, :], ALU.add))
                    link(nc.vector.tensor_copy(csi[:, 1, :], cs[:, 4, :]))
                    link(nc.vector.tensor_single_scalar(csi[:, 0, :], csi[:, 1, :], 7, ALU.logical_shift_right))
                    link(nc.vector.tensor_copy(cs[:, 5, :], csi[:, 0, :]))
                    link(nc.vector.tensor_single_scalar(csi[:, 0, :], csi[:, 0, :], NF, ALU.mult))
                    nc.vector.tensor_scalar(cs[:, 6, :], cs[:, 5, :], float(P), None, ALU.mult).then_inc(s["window_out"], 1)
                    dve.wait_ge(s["window_out"], 1)
                    link(nc.vector.tensor_tensor(aa, sc_, ff, ALU.subtract))
                    link(nc.vector.tensor_tensor(Fa["a"][:], Fa["a"][:], cs[:, 2, :].unsqueeze(2).broadcast_to([P, CB, CH]), ALU.add))
                    whole(bb, aa, OWN, 0.0)
                    link(nc.vector.tensor_tensor(q, aa, bb, ALU.add))
                    nc.vector.tensor_tensor(Fa["q"][:], Fa["q"][:], cs[:, 6, :].unsqueeze(2).broadcast_to([P, CB, CH]), ALU.subtract).then_inc(s["fieldsA_ready"], 1)
                    whole(cs[0:1, 7, 0:1], cs[0:1, 1, CB - 1:CB], OWN * BU, float(OWN * BU - 1))
                    link(nc.vector.tensor_scalar(cs[0:1, 7, 0:1], cs[0:1, 7, 0:1], 1.0, None, ALU.max))
                    link(nc.vector.tensor_copy(turns_i[:], cs[0:1, 7, 0:1]))
                    dve.wait_ge(s["prefix_read"], 2)

                @block.scalar
                def _(act):
                    act.wait_ge(s["fieldsB_ready"], 1)
                    for k, f in enumerate(("i", "j", "w", "q")):
                        nc.scalar.copy(fieldsB[f][:], tp[:, k, :])

                @block.tensor
                def _(pe):
                    for l in lists:
                        R = l["R"]
                        pe.wait_ge(s["totals_ready"], 1 + 2 * l["n"])
                        if l["n"]:
                            pe.wait_ge(s["prefix_read"], l["n"])
                        nc.tensor.matmul(pre[:, 0:T], g["before"][0:R, :], small[0:R, 0, :], start=True, stop=True)
                        nc.tensor.matmul(pre[:, T:2 * T], g["ones"][0:R, :], small[0:R, 0, :], start=True, stop=True).then_inc(s["prefix_ready"], 1)
                        pe.wait_ge(s["totals_ready"], 2 + 2 * l["n"])
                        nc.tensor.matmul(pre[0:1, 64:64 + P], small[:, 6, 0:1], g["ident"][:], start=True, stop=True).then_inc(s["prefix_ready"], 1)
                    pe.wait_ge(s["totals_ready"], 5)
                    pe.wait_ge(s["prefix_read"], 2)
                    nc.tensor.matmul(pre[:, 0:CB], g["before"][:], cs[:, 0, :], start=True, stop=True)
                    nc.tensor.matmul(pre[:, CB:2 * CB], g["ones"][:], cs[:, 0, :], start=True, stop=True).then_inc(s["prefix_ready"], 1)
                    pe.wait_ge(s["fieldsA_ready"], 1)
                    for k, f in enumerate((Fa["i"], Fa["j"], wa, Fa["q"])):
                        for b in range(CB):
                            ins = nc.tensor.transpose(tp[:, k, b * CH:(b + 1) * CH], f[:, b, :], g["ident"][:])
                    ins.then_inc(s["fieldsB_ready"], 1)
                    pe.wait_ge(s["fieldsB_ready"], 1)
            wk.close()
        multiply(nc, g, sem, t, pb, sc, lists, comp, NCOMP, fieldsB, window_row, turns_i, stage_rec, stage_slot)


SCAT = 8


def multiply(nc, g, sem, t, pb, sc, lists, comp, NCOMP, fieldsB, window_row, turns_i, stage_rec, stage_slot):
    names = (
        "lot_staged", "held", "lot_scattered_a", "lot_scattered_b", "step", "angle_ready", "sine_ready",
        "onehot_ready", "window_summed", "window_added", "terms_packed", "tables_zeroed",
        "next_coef_ready", "diag_ready", "rows_spread", "rows_copied", "v_ready", "u_ready",
        "t1_ready", "x1_turned", "x1_copied", "level_ready", "tx_ready", "q_ready",
        "q_copied", "wt_ready", "wt_copied", "y_ready", "y_copied", "dm_ready", "m_added", "m_ready")
    s = {k: sem("rot_" + k) for k in names}
    NC4 = CB * CH
    rec = [t(f"term_records{k}", [P, NC4, NF], BF16) for k in range(2)]
    pos = [t(f"term_position{k}", [P, NC4]) for k in range(2)]
    fi, fj, w1, w2, sn, cn = (t("rB_tmp%d" % k, [P, NC4]) for k in range(6))
    part = t("part_bf", [P, NC4], BF16)
    after, level, previous = t("row_after_column", [P, P]), t("level_masks", [P, 7, P]), t("previous_column", [P, P])
    xor_i, xs_i = t("xor_i", [P, P], I32), t("xor_shifted", [P, P], I32)
    row_i, col_i = t("row_i", [P, P], I32), t("col_i", [P, P], I32)
    cf, cfn = t("coefficients", [P, BU, NF]), t("next_coefficients", [P, BU, NF])
    SU = BU // 2
    U, V, VJ = t("U", [P, BU, D]), t("V", [P, BU, D]), t("V_of_j", [P, D])
    ones, diag, spread_rows = t("ones_bf", [P, P], BF16), t("diag_rows", [P, BU, P], BF16), t("spread_rows", [P, BU, P], BF16)
    LI, LJ = t("L_of_i", [P, BU, P]), t("L_of_j", [P, BU, P])
    pair_mask = t("pair_mask", [P, BU, P])
    LM = t("L_matrix", [P, BU, P])
    NK = t("NK", [P, 7, BU, P])
    onehot = NK[:].rearrange("p k u c -> p (k u c)").bitcast(BF16)[:, 0:2 * PK * 2 * WIN * P].rearrange(
        "p (b n o c) -> p b n o c", b=2, n=PK, o=2)
    TX = t("TX", [P, BU, 2, P])
    QS = t("QS", [P, 7, BU, P])
    WT = t("WT", [P, BU, H2, P])
    YS = t("YS", [P, 2, P])
    M = g["rot"]
    ps_a = [pb(f"ps_a{k}", [P, 512], sc) for k in range(2)]
    ps_b = [pb(f"ps_b{k}", [P, 512], sc) for k in range(2)]
    ps_y = [pb(f"ps_y{k}", [P, 512], sc) for k in range(2)]
    ps_m = [pb(f"ps_m{k}", [P, 512], sc) for k in range(2)]

    def window(b, n, w=None):
        at = n * WIN * NF
        return ps_m[b][:, at:at + WIN * NF] if w is None else ps_m[b][:, at + w * NF:at + (w + 1) * NF]

    def cols(a, k, which):
        letters = "abc"[:len(a.shape) - 2]
        v = a.rearrange(f"p {' '.join(letters)} (n o w) -> p {' '.join(letters)} n o w", o=2, w=2 ** k)
        return v[:, :, :, which, :] if letters == "a" else v[:, :, which, :]

    with nc.Block() as block:
        @block.gpsimd
        def _(pool):
            nc.gpsimd.iota(row_i[:], [[0, P]], base=0, channel_multiplier=1).then_inc(s["m_ready"], 1)
            nc.gpsimd.iota(col_i[:], [[1, P]], base=0, channel_multiplier=0).then_inc(s["m_ready"], 1)
            staged = Count(s["lot_staged"])
            done = [s["lot_scattered_a"], s["lot_scattered_b"]]
            base = [0, 0]
            for l in lists:
                R, F = l["R"], l["F"]

                def lot(turn, b, first):
                    if not first:
                        pool.wait_ge(done[b], base[b] + turn * (SCAT * 16))
                        pool.sem_inc(s["held"], 1)
                    at = (turn * 2 + b) * SCAT
                    cols = slice(at, at + SCAT) if isinstance(at, int) else bass.ds(at, SCAT)
                    staged.mark(nc.gpsimd.tensor_copy(stage_rec[0:R, b], l["rec"][:, cols, :]))
                    v = staged.mark(nc.gpsimd.tensor_copy(stage_slot[0:R, b], l["slot"][:, cols]))
                    pool.wait_ge(staged.sem, v)
                    pool.sem_inc(s["held"], 1)
                    for k in range(SCAT):
                        nc.gpsimd.indirect_dma_start(l["list"][:, :], bass.IndirectOffsetOnAxis(ap=stage_slot[0:R, b, k:k + 1], axis=0),
                                                     stage_rec[0:R, b, k, :], None).then_inc(done[b], 16)

                turns = F // (2 * SCAT)
                for b in range(2):
                    lot(0, b, l["n"] == 0)
                with pool.Fori(1, turns) as i:
                    staged.enter(i - 1, 4)
                    for b in range(2):
                        lot(i, b, False)
                    staged.leave(turns - 1)
                base = [b + turns * SCAT * 16 for b in base]
            for b in range(2):
                pool.wait_ge(done[b], base[b])
            nc.gpsimd.memset(stage_slot[0:1, 0, 0:1], 0)

        @block.scalar
        def _(act):
            act.wait_ge(s["angle_ready"], 1)
            nc.scalar.activation(sn[:], w1[:], ACT.Sin).then_inc(s["sine_ready"], 1)
            nc.scalar.activation(cn[:], w2[:], ACT.Sin).then_inc(s["sine_ready"], 1)
            act.wait_ge(s["terms_packed"], 1)
            trips = act.value_load(turns_i[0:1, 0:1], min_val=1, max_val=NTURN)
            nx, dg, rs, rc, xp, xc, q, qc, wt, wc, y, yc = (Count(s[k]) for k in (
                "next_coef_ready", "diag_ready", "rows_spread", "rows_copied", "x1_turned", "x1_copied", "q_ready", "q_copied", "wt_ready", "wt_copied", "y_ready", "y_copied"))

            def need(c_):
                c_.n += 1
                act.wait_ge(c_.sem, c_.value())

            def diagonals():
                need(nx)
                for u in range(BU):
                    dg.mark(nc.scalar.activation(diag[:, u, :], g["ident"][:], ACT.Identity, scale=cfn[:, u, 0:1]))

            def copy_rows():
                need(rs)
                rc.mark(nc.scalar.copy(spread_rows[:].rearrange("p u c -> p (u c)"), ps_y[0][:]))

            def turn(chain):
                for h in range(2):
                    need(xp)
                    xc.mark(nc.scalar.copy(TX[:, h * SU:(h + 1) * SU, 1, :], ps_b[h][:, 0:SU * P].rearrange("p (u c) -> p u c", u=SU)))
                for k in range(1, 7):
                    if k == 5:
                        copy_rows()
                    for h in range(2):
                        need(q)
                        dst = cols(QS[:, k, h * SU:(h + 1) * SU, :], k, 1)
                        qc.mark(nc.scalar.copy(dst, ps_b[h][:, 0:SU * P // 2].rearrange("p (u n w) -> p u n w", u=SU, w=2 ** k)))
                    if chain and k <= BU:
                        for c_ in range(2):
                            need(y)
                            yc.mark(nc.scalar.copy(YS[:, c_, :], ps_y[c_][:, 0:P]))
                    if k == 3:
                        diagonals()
                for h in range(2):
                    need(wt)
                    wc.mark(nc.scalar.copy(WT[:, h * SU:(h + 1) * SU].rearrange("p u h c -> p (u h c)"), ps_a[h][:]))

            diagonals()
            copy_rows()
            turn(False)
            with act.Fori(0, trips) as i:
                for c_, per in ((nx, 1), (dg, BU), (rs, 1), (rc, 1), (xp, 2), (xc, 2), (q, 12), (qc, 12), (wt, 2), (wc, 2), (y, 2 * BU), (yc, 2 * BU)):
                    c_.enter(i, per)
                turn(True)

        @block.vector
        def _(dve):
            c = Count(s["step"])

            def link(ins):
                dve.wait_ge(c.sem, c.mark(ins))

            dve.wait_ge(s["m_ready"], 2)
            link(nc.vector.tensor_scalar(after[:], g["iota"][:, 0:P], g["pidx"][:], None, ALU.is_lt))
            link(nc.vector.tensor_tensor(xor_i[:], row_i[:], col_i[:], ALU.bitwise_xor))
            for k in range(7):
                link(nc.vector.tensor_single_scalar(xs_i[:], xor_i[:], k, ALU.logical_shift_right))
                link(nc.vector.scalar_tensor_tensor(level[:, k, :], xs_i[:], 1.0, after[:], ALU.is_equal, ALU.mult))
            link(nc.vector.tensor_scalar(previous[:], g["iota"][:, 0:P], 1.0, g["pidx"][:], ALU.add, ALU.is_equal))
            link(nc.vector.tensor_scalar(previous[:], previous[:], -1.0, None, ALU.mult))
            for h in range(H2):
                link(nc.vector.tensor_scalar(M[:, h, :], g["iota"][:, 0:D], float(-h * P), g["pidx"][:], ALU.add, ALU.is_equal))
            B = {k: v[:] for k, v in fieldsB.items()}
            link(nc.vector.tensor_scalar(w1[:], B["w"], 1.0 / TWO_PI, None, ALU.mult))
            link(nc.vector.tensor_scalar(w1[:], w1[:], MAGIC, None, ALU.add))
            link(nc.vector.tensor_scalar(w1[:], w1[:], -MAGIC, None, ALU.add))
            link(nc.vector.scalar_tensor_tensor(w2[:], w1[:], -TWO_PI_HI, B["w"], ALU.mult, ALU.add))
            link(nc.vector.scalar_tensor_tensor(w1[:], w1[:], -TWO_PI_LO, w2[:], ALU.mult, ALU.add))
            link(nc.vector.tensor_scalar(w1[:], w1[:], PI_SAFE, -PI_SAFE, ALU.min, ALU.max))
            link(nc.vector.scalar_tensor_tensor(w2[:], w1[:], -1.0, w1[:], ALU.mult, ALU.max))
            link(nc.vector.tensor_scalar(w2[:], w2[:], -1.0, TWO_PI / 4, ALU.mult, ALU.add))
            dve.sem_inc(s["angle_ready"], 1)
            link(nc.vector.tensor_tensor(fi[:], B["i"], B["j"], ALU.not_equal))
            link(nc.vector.scalar_tensor_tensor(fi[:], B["i"], float(D), fi[:], ALU.is_lt, ALU.mult))
            link(nc.vector.tensor_scalar(fj[:], B["j"], float(D), None, ALU.is_lt))
            link(nc.vector.scalar_tensor_tensor(pos[0][:], B["q"], 1.0, fi[:], ALU.add, ALU.mult))
            link(nc.vector.tensor_scalar(pos[0][:], pos[0][:], -1.0, None, ALU.add))
            link(nc.vector.scalar_tensor_tensor(pos[1][:], B["q"], 1.0, fi[:], ALU.add, ALU.add))
            link(nc.vector.tensor_tensor(pos[1][:], pos[1][:], fj[:], ALU.mult))
            link(nc.vector.tensor_scalar(pos[1][:], pos[1][:], -1.0, None, ALU.add))
            for k, f in enumerate(("i", "j")):
                link(nc.vector.tensor_scalar(rec[k][:, :, 0], B[f], float(D - 1), 1.0, ALU.min, ALU.add))
                for r in rec:
                    link(nc.vector.tensor_scalar(r[:, :, 1 + k], B[f], float(D - 1), 1.0, ALU.min, ALU.add))
            link(nc.vector.tensor_tensor(rec[1][:, :, 3], fi[:], fj[:], ALU.mult))
            link(nc.vector.memset(rec[0][:, :, 3], 0.0))
            dve.wait_ge(s["sine_ready"], 2)
            for v, places in ((cn, ((0, 4, 1.0), (1, 7, 1.0))), (sn, ((0, 7, -1.0), (1, 4, 1.0)))):
                for k in range(3):
                    link(nc.vector.tensor_copy(part[:], v[:]))
                    for r, at, sign in places:
                        link(nc.vector.tensor_scalar(rec[r][:, :, at + k], part[:], sign, None, ALU.mult))
                    if k < 2:
                        link(nc.vector.tensor_tensor(v[:], v[:], part[:], ALU.subtract))
            ready, summed, added = (Count(s[k]) for k in ("onehot_ready", "window_summed", "window_added"))

            def onehots(c_, b):
                for n in range(PK):
                    for k in range(2):
                        ready.mark(nc.vector.tensor_scalar(onehot[:, b, n, k, :], g["iota16"][:], pos[k][:, bass.ds(c_ * PK + n, 1)], None, ALU.is_equal))

            onehots(0, 0)
            flat = comp[:].rearrange("p n f -> p (n f)")
            with dve.Fori(0, LOTS // 2) as i:
                added.enter(i, 2 * PK)
                summed.enter(i, 2)
                _, at = nc.values_load_multi_w_load_instructions(
                    window_row[0:1, bass.ds(i * (2 * PK), 2 * PK)], [mybir.EngineType.DVE], min_val=0, max_val=(NCOMP - WIN) * NF,
                    skip_runtime_bounds_check_because="it is a prefix sum of 0s, 1s and 2s over all rotations")
                for b in range(2):
                    onehots(i * 2 + b + 1, 1 - b)
                    summed.n += 1
                    dve.wait_ge(summed.sem, summed.value())
                    for n in range(PK):
                        if n:
                            dve.wait_ge(added.sem, added.value())
                        added.mark(nc.vector.tensor_tensor(flat[:, bass.ds(at[b * PK + n], WIN * NF)], flat[:, bass.ds(at[b * PK + n], WIN * NF)], window(b, n), ALU.add))
                    dve.wait_ge(added.sem, added.value())
                added.leave(LOTS // 2)
            dve.wait_ge(added.sem, added.value())
            link(nc.vector.tensor_tensor(comp[:, :, 4:10:3], comp[:, :, 4:10:3], comp[:, :, 5:10:3], ALU.add))
            link(nc.vector.tensor_tensor(comp[:, :, 4:10:3], comp[:, :, 4:10:3], comp[:, :, 6:10:3], ALU.add))
            spare = NK[:].rearrange("p k u c -> p (k u c)")
            own, other = (spare[:, k * NCOMP:(k + 1) * NCOMP] for k in range(2))
            field = lambda k: comp[:, :, k]
            link(nc.vector.tensor_tensor(own[:], field(0), field(1), ALU.is_equal))
            link(nc.vector.scalar_tensor_tensor(own[:], field(0), 0.0, own[:], ALU.is_gt, ALU.mult))
            link(nc.vector.tensor_tensor(field(4), field(4), own[:], ALU.subtract))
            link(nc.vector.tensor_tensor(own[:], field(0), field(2), ALU.is_equal))
            link(nc.vector.tensor_tensor(other[:], field(1), field(2), ALU.not_equal))
            link(nc.vector.tensor_tensor(own[:], own[:], other[:], ALU.mult))
            link(nc.vector.tensor_tensor(field(7), field(7), own[:], ALU.subtract))
            dve.sem_inc(s["terms_packed"], 1)
            trips = dve.value_load(turns_i[0:1, 0:1], min_val=1, max_val=NTURN)
            nc.vector.memset(NK[:], 0.0).then_inc(c.sem, 1)
            nc.vector.memset(QS[:], 0.0).then_inc(c.sem, 1)
            nc.vector.memset(ones[:], 1.0).then_inc(c.sem, 1)
            c.n += 3
            dve.wait_ge(c.sem, c.value())
            dve.sem_inc(s["tables_zeroed"], 1)
            dve.sem_inc(s["m_added"], 2)
            step = Count(c.sem)
            step.n = c.n
            nx, rc, vr, ur, t1, lv, tx, dm, ma = (Count(s[k]) for k in (
                "next_coef_ready", "rows_copied", "v_ready", "u_ready", "t1_ready", "level_ready", "tx_ready", "dm_ready", "m_added"))

            def slink(ins):
                dve.wait_ge(step.sem, step.mark(ins))

            def need(c_):
                c_.n += 1
                dve.wait_ge(c_.sem, c_.value())

            half = lambda h: slice(h * SU, (h + 1) * SU)

            def load(dst, turn_):
                return move(nc, dst[:].rearrange("p u c -> p (u c)"), flat[:, bass.ds(turn_ * (BU * NF), BU * NF)])

            def pairs(u):
                step.mark(nc.vector.scalar_tensor_tensor(pair_mask[:, u, :], previous[:], cfn[:, u, 3:4], after[:], ALU.mult, ALU.add))

            def spread():
                need(rc)
                f = lambda u, k: cfn[:, u, k:k + 1]
                for u in range(BU):
                    step.mark(nc.vector.tensor_scalar(LI[:, u, :], spread_rows[:, u, :], f(u, 1), f(u, 4), ALU.is_equal, ALU.mult))
                    step.mark(nc.vector.tensor_scalar(LJ[:, u, :], spread_rows[:, u, :], f(u, 2), f(u, 7), ALU.is_equal, ALU.mult))
                dve.wait_ge(step.sem, step.value())

            def lower():
                slink(nc.vector.tensor_tensor(LI[:], LI[:], LJ[:], ALU.add))
                slink(nc.vector.tensor_tensor(LM[:], LI[:], pair_mask[:], ALU.mult))

            def turn(i, chain):
                def add_m(u):
                    for c_ in range(2):
                        need(dm)
                        part_ = M[:, :, c_ * P:(c_ + 1) * P]
                        ma.mark(nc.vector.tensor_tensor(part_, part_, ps_m[c_][:, 0:D].rearrange("p (h c) -> p h c", h=H2), ALU.add))

                def nk(h, k):
                    w = 2 ** k
                    m = level[:, k, :].rearrange("p (n o w) -> p n o w", o=2, w=w)[:, :, 0, :]
                    return nc.vector.tensor_tensor(cols(NK[:, k, half(h), :], k, 0), cols(LM[:, half(h), :], k, 0),
                                                   m.unsqueeze(1).broadcast_to([P, SU, P // 2 // w, w]), ALU.mult)

                f = lambda u, k: cf[:, u, k:k + 1]

                def v_of(u):
                    step.mark(nc.vector.tensor_scalar(V[:, u, :], g["iota16"][:, 1:D + 1], f(u, 1), f(u, 4), ALU.is_equal, ALU.mult))
                    slink(nc.vector.tensor_scalar(VJ[:], g["iota16"][:, 1:D + 1], f(u, 2), f(u, 7), ALU.is_equal, ALU.mult))
                    vr.mark(nc.vector.tensor_tensor(V[:, u, :], V[:, u, :], VJ[:], ALU.add))
                    dve.wait_ge(vr.sem, vr.value())

                step.mark(load(cf, i + 1 if chain else 0))
                for h in range(2):
                    step.mark(nk(h, 0))
                made = step.value()
                for h in range(2):
                    lv.mark(nk(h, 1))
                dve.wait_ge(step.sem, made)
                for h in range(2):
                    if chain:
                        dve.wait_ge(s["wt_ready"], i * 2 + 1 + h)
                    t1.mark(nc.vector.tensor_tensor(TX[:, half(h), 0, :], NK[:, 0, half(h)], g["ident"][:].unsqueeze(1).broadcast_to([P, SU, P]), ALU.add))
                for k in range(1, 7):
                    if k < 6:
                        for h in range(2):
                            step.mark(nk(h, k + 1))
                    if k <= BU:
                        v_of(k - 1)
                    if k == 5:
                        spread()
                    if k == 6:
                        lower()
                    for h in range(2):
                        need(tx)
                        for o in range(1 if k == 6 else 2):
                            src = which = 1 - o
                            dst = cols(TX[:, half(h), src, :], k, which)
                            ins = nc.vector.tensor_tensor(dst, dst, ps_a[h][:, o * P:(o + 1) * P].rearrange("p (u n w) -> p u n w", u=SU, w=2 ** k), ALU.add)
                            if o == 0 and k < 6:
                                step.mark(ins)
                        lv.mark(ins)
                    if k == 1:
                        nx.mark(load(cfn, i + 2 if chain else 1))
                    if k <= BU:
                        if chain:
                            add_m(k - 1)
                        ur.mark(nc.vector.tensor_scalar(U[:, k - 1, :], g["iota16"][:, 1:D + 1], f(k - 1, 0), None, ALU.is_equal))
                        if k == 1:
                            dve.wait_ge(nx.sem, nx.value())
                        pairs(k - 1)

            nx.mark(load(cfn, 0))
            dve.wait_ge(nx.sem, nx.value())
            for u in range(BU):
                pairs(u)
            spread()
            lower()
            start = step.n
            turn(0, False)
            per = step.n - start
            with dve.Fori(0, trips) as i:
                for c_, p_ in ((step, per), (nx, 1), (rc, 1), (vr, BU), (ur, BU), (t1, 2), (lv, 14), (tx, 12), (dm, 2 * BU), (ma, 2 * BU)):
                    c_.enter(i, p_)
                turn(i, True)

        @block.tensor
        def _(pe):
            ready, summed = Count(s["onehot_ready"]), Count(s["window_summed"])
            with pe.Fori(0, LOTS // 2) as i:
                for c_, per in ((ready, 4 * PK), (summed, 2)):
                    c_.enter(i, per)
                for b in range(2):
                    for n in range(PK):
                        ready.n += 2
                        pe.wait_ge(ready.sem, ready.value())
                        for w in range(WIN):
                            for k in range(2):
                                ins = nc.tensor.matmul(window(b, n, w), onehot[:, b, n, k, w * P:(w + 1) * P],
                                                       rec[k][:, bass.ds((i * 2 + b) * PK + n, 1), :].rearrange("p a f -> p (a f)"), start=(k == 0), stop=(k == 1))
                    summed.mark(ins)
            pe.wait_ge(s["terms_packed"], 1)
            trips = pe.value_load(turns_i[0:1, 0:1], min_val=1, max_val=NTURN)
            pe.wait_ge(s["tables_zeroed"], 1)
            dg, rs, vr, t1, xp, xc, lv, q, qc, tx, wt, y, yc, dm = (Count(s[k]) for k in (
                "diag_ready", "rows_spread", "v_ready", "t1_ready", "x1_turned", "x1_copied", "level_ready", "q_ready",
                "q_copied", "tx_ready", "wt_ready", "y_ready", "y_copied", "dm_ready"))

            def need(c_, k=1):
                c_.n += k
                pe.wait_ge(c_.sem, c_.value())

            def keep_warm(n):
                for _ in range(n):
                    nc.tensor.matmul(ps_y[1][:, 0:P], g["identb"][:], g["identb"][:], start=True, stop=True)

            def spread():
                need(dg, BU)
                rs.mark(nc.tensor.matmul(ps_y[0][:], ones[:], diag[:].rearrange("p u c -> p (u c)"), start=True, stop=True))

            def turn(i, chain):
                blocks = lambda h: range(h * SU, (h + 1) * SU)

                def chain_y(u):
                    if u == 0:
                        pe.wait_ge(s["wt_copied"], i * 2 + 2)
                        pe.wait_ge(s["rows_copied"], i + 2)
                        pe.wait_ge(s["u_ready"], i * BU + BU)
                    for c_ in range(2):
                        pe.wait_ge(s["m_added"], i * (2 * BU) + (2 * u + c_ + 1))
                        for h in range(H2):
                            ins = nc.tensor.matmul(ps_y[c_][:, 0:P], WT[:, u, h, :], M[:, h, c_ * P:(c_ + 1) * P], start=(h == 0), stop=(h == 1))
                        y.mark(ins)

                def chain_m(u):
                    for c_ in range(2):
                        need(yc)
                        for h in range(H2):
                            ins = nc.tensor.matmul(ps_m[c_][:, h * P:(h + 1) * P], U[:, u, h * P:(h + 1) * P], YS[:, c_, :], start=True, stop=True)
                        dm.mark(ins)

                for b in range(2):
                    need(t1)
                    for n, u in enumerate(blocks(b)):
                        ins = nc.tensor.transpose(ps_b[b][:, n * P:(n + 1) * P], TX[:, u, 0, :], g["ident"][:])
                    xp.mark(ins)
                two = lambda a, k: a.rearrange("p (n w) -> p n w", w=2 ** k)
                half_cols = lambda a, k, which: a.rearrange("p (n o w) -> p n o w", o=2, w=2 ** k)[:, :, which, :]
                for k in range(1, 7):
                    for b in range(2):
                        if k == 1:
                            need(xc)
                        need(lv)
                        for n, u in enumerate(blocks(b)):
                            ins = nc.tensor.matmul(two(ps_b[b][:, n * 64:(n + 1) * 64], k), NK[:, k, u, :], half_cols(TX[:, u, 1, :], k, 1), start=True, stop=True)
                        q.mark(ins)
                    if chain and k <= BU:
                        chain_y(k - 1)
                    else:
                        keep_warm(4)
                    for b in range(2):
                        need(qc)
                        if chain and k == 1:
                            pe.wait_ge(s["wt_copied"], i * 2 + 1 + b)
                        for n, u in enumerate(blocks(b)):
                            ins = nc.tensor.matmul(two(ps_a[b][:, n * 64:(n + 1) * 64], k), TX[:, u, 0, :], half_cols(QS[:, k, u, :], k, 1), start=True, stop=True)
                            if k < 6:
                                ins = nc.tensor.matmul(two(ps_a[b][:, P + n * 64:P + (n + 1) * 64], k), QS[:, k, u, :], half_cols(TX[:, u, 0, :], k, 0), start=True, stop=True)
                        tx.mark(ins)
                    if chain and k <= BU:
                        chain_m(k - 1)
                    else:
                        keep_warm(12)
                    if k == 4:
                        spread()
                need(vr, BU)
                for b in range(2):
                    need(lv)
                    for n, u in enumerate(blocks(b)):
                        for h in range(H2):
                            at = (n * H2 + h) * P
                            ins = nc.tensor.matmul(ps_a[b][:, at:at + P], V[:, u, h * P:(h + 1) * P], TX[:, u, 1, :], start=True, stop=True)
                    wt.mark(ins)

            spread()
            turn(0, False)
            with pe.Fori(0, trips) as i:
                for c_, per in ((dg, BU), (rs, 1), (vr, BU), (t1, 2), (xp, 2), (xc, 2), (lv, 14), (q, 12), (qc, 12),
                                (tx, 12), (wt, 2), (y, 2 * BU), (yc, 2 * BU), (dm, 2 * BU)):
                    c_.enter(i, per)
                turn(i, True)
HEADS, NE0, F0 = 4, 4, 512
NE1, F1 = 8, 1024
CAP = -(-5 * N // (4 * NE1))
SLOTS = -(-CAP // P) * P
TT = 5
NTT = T // TT
SLOPE0, SLOPE1 = 0.2, 0.01
W0, W1R = HEADS * NE0 + HEADS, D + 2


def rest(nc, A, g, sem, sb, pb, out):
    x = g["x"]
    g["xnT"] = sb("x_normed_T", [P, H2, T * P], F32)
    g["mv"] = sb("mean_var", [P, T, 2], F32)
    g["rstd"] = sb("rstd", [P, T], F32)
    g["a_dst"] = sb("a_dst", [P, T, HEADS], F32)
    g["a_src"] = sb("a_src", [P, T, HEADS], F32)
    g["a1"] = sb("a_target1", [P, T, 1], F32)
    tab0 = nc.dram_tensor("node_rows0", (N + 1, W0), F32).ap()
    tab1 = nc.dram_tensor("node_rows1", (N + 1, W1R), F32).ap()
    with ExitStack() as sc:
        def t(name, shape, dt=F32):
            return sb(name, shape, dt, sc)
        MT = t("rotation_T", [P, H2, D])
        transpose_rotation(nc, g, sem, pb, MT)

        def add_to_x(dve, i, k, ps, used):
            used.mark(nc.vector.tensor_tensor(one(x, i, k), one(x, i, k), ps, ALU.add))
        layernorm(nc, g, sem, sb, "n0")
        project(nc, g, sem, sb, pb, "mix", lambda h: MT[:, h, :], D, add_to_x)
    with ExitStack() as sc:
        def t(name, shape, dt=F32):
            return sb(name, shape, dt, sc)
        gates = t("gates", [P, T, NE0])
        with ExitStack() as s2:
            def t2(name, shape, dt=F32):
                return sb(name, shape, dt, s2)
            wg = t2("W_gat", [P, H2, 16])
            rows = t2("rows0", [P, T, W0])
            small = t2("att_small", [P, 5, 16])
            prod = t2("att_prod", [P, T, 16])
            load_small(nc, sem, [(wg[:], A["W_gat"].rearrange("(h p) f -> p h f", p=P))] + [
                (small[:, k, :], A[n].rearrange("a b -> (a b)").partition_broadcast(P) if n[:3] == "att" else A[n].partition_broadcast(P))
                for k, n in enumerate(("att_src", "att_dst", "b_gat", "ln_gamma", "ln_beta"))], "att")

            def keep_rows(dve, i, k, ps, used):
                used.mark(move(nc, rows[:, bass.ds(i * TT + k, 1), 0:16].rearrange("p a d -> p (a d)"), ps))
            layernorm(nc, g, sem, sb, "n1")
            project(nc, g, sem, sb, pb, "gat", lambda h: wg[:, h, :], 16, keep_rows, keep_T=g["xnT"])
            acc = t2("acc0", [P, T, HEADS, NE0 + 1])
            attention_scores0(nc, g, sem, rows, small, prod, acc, tab0)
            attend(nc, g, sem, sb, pb, "e0", g["list0"], tab0, g["group_tile0"], NG0, HEADS, W0, 16, SLOPE0, acc)
            route(nc, g, sem, sb, acc, small, gates)
        g["recycle"]()
        experts0(nc, A, g, sem, sb, pb, gates)
    with ExitStack() as sc:
        def t(name, shape, dt=F32):
            return sb(name, shape, dt, sc)
        acc = t("acc1", [P, T, D + 1])
        with ExitStack() as s2:
            def t2(name, shape, dt=F32):
                return sb(name, shape, dt, s2)
            wl, bl = t2("W_layer", [P, H2, D]), t2("b_layer", [P, D])
            wa, ba = t2("w_a12", [P, 2, D]), t2("b_a", [P, 2])
            row = t2("rows1", [P, 3 * TT + 1, W1R])
            load_small(nc, sem, [(wl[:], A["W_layer"].rearrange("(h p) f -> p h f", p=P)), (bl[:], A["b_layer"].partition_broadcast(P)),
                                 (wa[:, 0, :], A["w_a1"].rearrange("a b -> (a b)").partition_broadcast(P)),
                                 (wa[:, 1, :], A["w_a2"].rearrange("a b -> (a b)").partition_broadcast(P)),
                                 (ba[:, 0:1], A["b_a1"].partition_broadcast(P)), (ba[:, 1:2], A["b_a2"].partition_broadcast(P))], "layer")
            layernorm(nc, g, sem, sb, "n2")
            g["scope"] = s2
            table1(nc, g, sem, sb, pb, wl, bl, wa, ba, row, acc, tab1)
        attend(nc, g, sem, sb, pb, "e1", g["list1"], tab1, g["group_tile1"], NG1, 1, W1R, D + 1, SLOPE1, acc)
        finish1(nc, g, sem, sb, acc)
    g["recycle"]()
    layernorm(nc, g, sem, sb, "n3")
    moe(nc, A, g, sem, sb, pb, out)


def load_small(nc, sem, pairs, tag):
    s = sem(tag + "_weights_loaded")
    with nc.Block() as block:
        @block.sync
        def _(sp):
            for dst, src in pairs:
                sp.dma_start(dst, src).then_inc(s, 16)
            sp.wait_ge(s, 16 * len(pairs))


def transpose_rotation(nc, g, sem, pb, MT):
    s, d = sem("rotation_turned"), sem("rotation_kept")
    with ExitStack() as sc:
        ps = pb("turn_ps", [P, H2, D], sc)
        with nc.Block() as block:
            @block.tensor
            def _(pe):
                for a in range(H2):
                    for b in range(H2):
                        ins = nc.tensor.transpose(ps[:, b, a * P:(a + 1) * P], g["rot"][:, a, b * P:(b + 1) * P], g["ident"][:])
                ins.then_inc(s, 1)

            @block.vector
            def _(dve):
                dve.wait_ge(s, 1)
                nc.vector.tensor_copy(MT[:], ps[:]).then_inc(d, 1)
                dve.wait_ge(d, 1)


def move(nc, dst, src):
    return nc.vector.tensor_scalar(dst, src, 1.0, None, ALU.mult)


def one(a, i, k):
    v = a[:, bass.ds(i * TT + k, 1)]
    return v.rearrange("p a d -> p (a d)") if len(a.shape) == 3 else v


def layernorm(nc, g, sem, sb, tag):
    c_, rooted = sem(tag + "_step"), sem(tag + "_rooted")
    x, mv, rstd = g["x"], g["mv"], g["rstd"]
    with ExitStack() as sc:
        st = sb(tag + "_stats", [P, T, 6], F32, sc)
        with nc.Block() as block:
            @block.vector
            def _(dve):
                c = Count(c_)

                def link(ins):
                    dve.wait_ge(c.sem, c.mark(ins))
                with dve.Fori(0, NTT) as i:
                    c.enter(i, TT)
                    for k in range(TT):
                        c.mark(nc.vector.bn_stats(one(st, i, k), one(x, i, k)))
                    c.leave(NTT)
                dve.wait_ge(c.sem, c.value())
                for k in range(T):
                    c.mark(nc.vector.bn_aggr(mv[:, k, :], st[:, k, :]))
                dve.wait_ge(c.sem, c.value())
                link(nc.vector.tensor_scalar(rstd[:], mv[:, :, 1], EPS, None, ALU.add))
                dve.wait_ge(rooted, 1)
                link(nc.vector.reciprocal(rstd[:], rstd[:]))

            @block.scalar
            def _(act):
                act.wait_ge(c_, 2 * T + 1)
                nc.scalar.sqrt(rstd[:], rstd[:]).then_inc(rooted, 1)


def project(nc, g, sem, sb, pb, tag, weight, width, use, keep_T=None, keep_x=None, per_use=1, rows_out=None, start=None):
    normed, turned, kept, made, used, persisted, step = (
        sem(f"{tag}_{k}") for k in ("normed", "turned", "kept", "made", "used", "persisted", "step"))
    with ExitStack() as sc:
        xs = sb(tag + "_xn", [P, TT, D], F32, sc)
        xt = sb(tag + "_xnT_tile", [P, TT, H2, P], F32, sc)
        pt = pb(tag + "_pt", [P, 2, 512], sc)
        py = pb(tag + "_py", [P, 2, 512], sc)
        with nc.Block() as block:
            if rows_out:
                rows_out(block, used)

            @block.tensor
            def _(pe):
                pe.sem_inc(kept, 1)
                pe.sem_inc(used, 1)
                with pe.Fori(0, NTT) as i:
                    def turn_tile(k):
                        pe.wait_ge(normed, i * TT + (k + 1))
                        if k != 1:
                            pe.wait_ge(kept, i * TT + (max(k - 1, 0) + 1))
                        for h in range(H2):
                            ins = nc.tensor.transpose(pt[:, k % 2, h * P:(h + 1) * P], xs[:, k, h * P:(h + 1) * P], g["ident"][:])
                        ins.then_inc(turned, 1)

                    def multiply_tile(k):
                        pe.wait_ge(kept, i * TT + (k + 2))
                        if k != 1:
                            pe.wait_ge(used, i * (TT * per_use) + (max(k - 1, 0) * per_use + 1))
                        for h in range(H2):
                            ins = nc.tensor.matmul(py[:, k % 2, 0:width], xt[:, k, h, :], weight(h), start=(h == 0), stop=(h == H2 - 1))
                        ins.then_inc(made, 1)

                    turn_tile(0)
                    turn_tile(1)
                    for k in range(TT):
                        multiply_tile(k)
                        if k + 2 < TT:
                            turn_tile(k + 2)

            @block.scalar
            def _(act):
                with act.Fori(0, NTT) as i:
                    for k in range(TT):
                        act.wait_ge(turned, i * TT + (k + 1))
                        nc.scalar.copy(xt[:, k].rearrange("p h c -> p (h c)"), pt[:, k % 2, 0:D]).then_inc(kept, 1)
                        if keep_T is not None:
                            act.wait_ge(kept, i * TT + (k + 2))
                            nc.scalar.copy(keep_T[:, :, bass.ds((i * TT + k) * P, P)], xt[:, k]).then_inc(persisted, 1)
                    if keep_T is not None:
                        act.wait_ge(persisted, i * TT + TT)

            @block.vector
            def _(dve):
                n, m, u, st = (Count(c) for c in (normed, made, used, step))
                if start:
                    start(dve)
                with dve.Fori(0, NTT) as i:
                    for c in (n, m):
                        c.enter(i, TT)
                    u.n = 1
                    u.enter(i, TT * per_use)
                    for k in range(TT):
                        args = (one(g["x"], i, k), g["mv"][:, bass.ds(i * TT + k, 1), 0], one(g["rstd"], i, k), ALU.subtract, ALU.mult)
                        n.mark(nc.vector.tensor_scalar(xs[:, k, :], *args))
                        if keep_x is not None:
                            nc.vector.tensor_scalar(one(keep_x, i, k), *args).then_inc(step, 1)
                    if keep_x is not None:
                        dve.wait_ge(step, i * TT + TT)
                    for k in range(TT):
                        m.n += 1
                        dve.wait_ge(m.sem, m.value())
                        use(dve, i, k, py[:, k % 2, 0:width], u)
                    dve.wait_ge(u.sem, u.value())


def attention_scores0(nc, g, sem, rows, small, prod, acc, tab0):
    c_, out_ = sem("scores0_step"), sem("rows0_written")
    with nc.Block() as block:
        @block.vector
        def _(dve):
            c = Count(c_)

            def link(ins):
                dve.wait_ge(c.sem, c.mark(ins))
            h = rows[:, :, 0:16]
            for k, dst in enumerate((g["a_src"], g["a_dst"])):
                link(nc.vector.tensor_tensor(prod[:], h, small[:, k, :].unsqueeze(1).broadcast_to([P, T, 16]), ALU.mult))
                link(nc.vector.tensor_reduce(dst[:], prod[:].rearrange("p t (h e) -> p t h e", e=NE0), X, ALU.add))
            link(nc.vector.tensor_copy(rows[:, :, 16:20], g["a_src"][:]))
            link(nc.vector.tensor_copy(acc[:, :, :, 0:NE0], h.rearrange("p t (h e) -> p t h e", e=NE0)))
            link(nc.vector.memset(acc[:, :, :, NE0:NE0 + 1], 1.0))
            nc.vector.memset(prod[:], 0.0).then_inc(c_, 1)

        @block.sync
        def _(sp):
            sp.wait_ge(c_, 8)
            sp.dma_start(tab0[0:NFULL * P, :].rearrange("(t p) d -> p t d", p=P), rows[:, 0:NFULL, :]).then_inc(out_, 16)
            sp.dma_start(tab0[NFULL * P:N, :], rows[0:NREST, NFULL, :]).then_inc(out_, 16)
            sp.dma_start(tab0[N:N + 1, :], prod[0:1, 0:2, :].rearrange("p a b -> p (a b)")[:, 0:W0]).then_inc(out_, 16)
            sp.wait_ge(out_, 48)


def attend(nc, g, sem, sb, pb, tag, edges, table, group_tile, NG, HN, W, acol, slope, acc):
    names = ("list_padded", "list_loaded", "index_staged", "index_ok", "rows_in_0", "rows_in_1", "rows_in_2", "rows_in_3",
             "rows_used", "onehot_ready", "neg_ready", "onehot_turned", "onehot_T_ready", "step", "scores_ready_0",
             "scores_ready_1", "scores_read_0", "scores_read_1", "target_ready", "target_in", "factor_in", "factor_out",
             "weight_in", "weight_out", "message_ready", "sum_ready")
    s = {k: sem(f"{tag}_{k}") for k in names}
    AW = NE0 + 1 if HN > 1 else D + 1
    NM = HN * AW
    NB = NG * G
    GH = G // 2
    with ExitStack() as sc:
        def t(name, shape, dt=F32):
            return sb(f"{tag}_{name}", shape, dt, sc)
        ed = t("edges", [P, NB + 2 * G, 2])
        idx = t("index", [P, NBUF, G], I32)
        rows = t("rows", [P, NBUF, G, W])
        E = t("onehot", [P, NBUF, G, P])
        NEG = t("not_target", [P, NBUF, G, P], BF16)
        ET = t("onehot_T", [P, NBUF, G, P])
        EW = t("onehot_weighted", [P, G, P])
        mg = t("half_max", [P, 2, HN])
        mn, mx = t("new_max", [P, HN]), t("group_max", [P, HN])
        fd, fac = t("max_change", [P, NBUF, HN]), t("factor", [P, NBUF, HN])
        tm = t("target_and_max", [P, 2, HN])
        v, v2, w = (t(n, [P, G, HN]) for n in ("score", "score2", "weight"))
        msg = t("message", [P, G, HN, NE0 + 1])
        top, act_top = t("top", [P, T, HN]), t("top_act", [P, T, HN])
        tmp = t("scaled", [P, HN, AW if HN > 1 else 1])
        consts = t("consts", [P, 2])
        HB = max(512, GH * HN * P)
        ps_flat = pb(tag + "_scores", [P, 2, HB], sc)
        ps = [ps_flat[:, a, 0:GH * HN * P].rearrange("p (g h e) -> p g h e", g=GH, h=HN) for a in range(2)]
        pe8_bank = pb(tag + "_at_edge", [P, 512], sc)
        pe8 = pe8_bank[:, 0:G * 2 * HN].rearrange("p (g h) -> p g h", g=G)
        psum_ = pb(tag + "_sum", [P, 512], sc)
        pt_bank = sc.enter_context(nc.psum_tensor(tag + "_turned", [P, 2 * 512], BF16))
        pt = pt_bank[:, 0:G * P].rearrange("p (g e) -> p g e", g=G)
        warm = pb(tag + "_warm", [P, P], sc)
        a_dst = g["a_dst"] if HN > 1 else g["a1"]
        turns = NG // NBUF
        with nc.Block() as block:
            @block.sync
            def _(sp):
                sp.dma_start(ed[:, 0:NB, :], edges.rearrange("(p b) k -> p b k", p=P)).then_inc(s["list_loaded"], 16)
                sp.wait_ge(s["list_loaded"], 16)

            @block.gpsimd
            def _(pool):
                nc.gpsimd.memset(ed[:, NB:, 0].bitcast(I32), N).then_inc(s["list_padded"], 1)
                nc.gpsimd.memset(ed[:, NB:, 1], -1.0).then_inc(s["list_padded"], 1)
                pool.wait_ge(s["list_padded"], 2)
                pool.wait_ge(s["list_loaded"], 16)
                pool.sem_inc(s["rows_used"], NBUF)

                def gather(i, b):
                    grp = i * NBUF + b
                    pool.wait_ge(s["rows_used"], grp + 1)
                    pool.sem_inc(s["index_ok"], 1)
                    cols = slice(grp * G, grp * G + G) if isinstance(grp, int) else bass.ds(grp * G, G)
                    nc.gpsimd.tensor_copy(idx[:, b, :], ed[:, cols, 0].bitcast(I32)).then_inc(s["index_staged"], 1)
                    pool.wait_ge(s["index_staged"], grp + 1)
                    pool.sem_inc(s["index_ok"], 1)
                    for k in range(G):
                        nc.gpsimd.indirect_dma_start(rows[:, b, k, :], None, table[:, :],
                                                     bass.IndirectOffsetOnAxis(ap=idx[:, b, k:k + 1], axis=0)).then_inc(s[f"rows_in_{b}"], 16)

                with pool.Fori(0, turns) as i:
                    for b in range(NBUF):
                        gather(i, b)
                gather(turns, 0)

            @block.scalar
            def _(act):
                act.wait_ge(s["step"], 2)

                def masks(i, b):
                    c = b % NBUF
                    act.wait_ge(s["onehot_ready"], i * NBUF + (b + 1))
                    nc.scalar.activation(NEG[:, c], E[:, c], ACT.Identity, bias=consts[:, 0:1], scale=BIG).then_inc(s["neg_ready"], 1)
                    act.wait_ge(s["onehot_turned"], i * NBUF + (b + 1))
                    nc.scalar.activation(ET[:, c], pt, ACT.Identity, bias=consts[:, 1:2], scale=1.0 / BIG).then_inc(s["onehot_T_ready"], 1)

                masks(0, 0)
                masks(0, 1)
                with act.Fori(0, turns) as i:
                    for b in range(NBUF):
                        act.wait_ge(s["factor_in"], i * NBUF + (b + 1))
                        nc.scalar.activation(fac[:, b], fd[:, b], ACT.Exp).then_inc(s["factor_out"], 1)
                        act.wait_ge(s["weight_in"], i * NBUF + (b + 1))
                        nc.scalar.activation(w[:], v[:], ACT.Exp).then_inc(s["weight_out"], 1)
                        masks(i, b + 2)

            @block.vector
            def _(dve):
                c = Count(s["step"])

                def link(ins):
                    dve.wait_ge(c.sem, c.mark(ins))
                link(nc.vector.memset(consts[:, 0:1], -BIG))
                link(nc.vector.memset(consts[:, 1:2], 1.0))
                if HN > 1:
                    link(nc.vector.tensor_copy(top[:], g["a_src"][:]))
                    link(nc.vector.tensor_tensor(act_top[:], top[:], a_dst[:], ALU.add))
                else:
                    link(nc.vector.memset(top[:], -BIG))
                    link(nc.vector.memset(act_top[:], -BIG))
                    link(nc.vector.memset(acc[:], 0.0))
                link(nc.vector.scalar_tensor_tensor(act_top[:], act_top[:], slope, act_top[:], ALU.mult, ALU.max))
                dve.wait_ge(s["list_loaded"], 16)
                dve.wait_ge(s["list_padded"], 2)

                def onehots(i, b):
                    grp = i * NBUF + b
                    cols = slice(grp * G, grp * G + G) if isinstance(grp, int) else bass.ds(grp * G, G)
                    dl = ed[:, cols, 1].unsqueeze(2).broadcast_to([P, G, P])
                    nc.vector.tensor_tensor(E[:, b % NBUF], g["iota"][:, 0:P].unsqueeze(1).broadcast_to([P, G, P]), dl,
                                            ALU.is_equal).then_inc(s["onehot_ready"], 1)

                def tiles_of(first, n):
                    at = slice(first, first + n) if isinstance(first, int) else bass.ds(first, n)
                    return nc.values_load_multi_w_load_instructions(
                        group_tile[0:1, at], [mybir.EngineType.DVE], min_val=0, max_val=T - 1,
                        skip_runtime_bounds_check_because="they are counts of tiles, capped where they are made")[1]

                def add_sum(i, b, tile):
                    grp = i * NBUF + b
                    f = fac[:, b % NBUF]
                    dve.wait_ge(s["factor_out"], grp + 1)
                    if HN > 1:
                        a4 = acc[:, bass.ds(tile, 1)].rearrange("p a h e -> p (a h) e")
                        link(nc.vector.tensor_tensor(tmp[:], a4, f.unsqueeze(2).broadcast_to([P, HN, AW]), ALU.mult))
                        dve.wait_ge(s["sum_ready"], grp + 1)
                        link(nc.vector.tensor_tensor(a4, tmp[:], psum_[:, 0:NM].rearrange("p (h e) -> p h e", e=AW), ALU.add))
                    else:
                        a1 = acc[:, bass.ds(tile, 1)].rearrange("p a h -> p (a h)")
                        dve.wait_ge(s["sum_ready"], grp + 1)
                        link(nc.vector.scalar_tensor_tensor(a1, a1, f, psum_[:, 0:NM], ALU.mult, ALU.add))
                    dve.sem_inc(s["rows_used"], 1)

                def step(i, b, first, tile, before):
                    grp = i * NBUF + b
                    at = lambda a: a[:, bass.ds(tile, 1)].rearrange("p a h -> p (a h)")
                    c.mark(move(nc, tm[:, 0, :], at(a_dst)))
                    for a in range(2):
                        dve.wait_ge(s[f"scores_ready_{a}"], grp + 1)
                        nc.vector.tensor_reduce(mg[:, a, :], ps[a].rearrange("p g h e -> p h g e"), XY, ALU.max).then_inc(s[f"scores_read_{a}"], 1)
                    for a in range(2):
                        dve.wait_ge(s[f"scores_read_{a}"], grp + 1)
                    link(nc.vector.tensor_tensor(mx[:], mg[:, 0, :], mg[:, 1, :], ALU.max))
                    link(nc.vector.tensor_tensor(at(top), mx[:], at(top), ALU.max))
                    link(nc.vector.tensor_tensor(mn[:], at(top), tm[:, 0, :], ALU.add))
                    nc.vector.scalar_tensor_tensor(tm[:, 1, :], mn[:], slope, mn[:], ALU.mult, ALU.max).then_inc(s["target_ready"], 1)
                    dve.wait_ge(s["target_ready"], grp + 1)
                    nc.vector.tensor_tensor(fd[:, b], at(act_top), tm[:, 1, :], ALU.subtract).then_inc(s["factor_in"], 1)
                    dve.wait_ge(s["factor_in"], grp + 1)
                    c.mark(move(nc, at(act_top), tm[:, 1, :]))
                    if first:
                        dve.sem_inc(c.sem, 2 if HN > 1 else 1)
                        c.n += 2 if HN > 1 else 1
                    else:
                        add_sum(i, b - 1, before)
                    dve.wait_ge(s["target_in"], grp + 1)
                    link(nc.vector.tensor_tensor(v2[:], rows[:, b, :, acol:acol + HN], pe8[:, :, 0:HN], ALU.add))
                    link(nc.vector.scalar_tensor_tensor(v2[:], v2[:], slope, v2[:], ALU.mult, ALU.max))
                    nc.vector.tensor_tensor(v[:], v2[:], pe8[:, :, HN:2 * HN], ALU.subtract).then_inc(s["weight_in"], 1)
                    onehots(i, b + 2)
                    dve.wait_ge(s["weight_out"], grp + 1)
                    if HN > 1:
                        c.mark(nc.vector.tensor_tensor(msg[:, :, :, 0:NE0], rows[:, b, :, 0:HN * NE0].rearrange("p g (h e) -> p g h e", e=NE0),
                                                       w[:].unsqueeze(3).broadcast_to([P, G, HN, NE0]), ALU.mult))
                        link(nc.vector.tensor_copy(msg[:, :, :, NE0], w[:]))
                    else:
                        c.mark(nc.vector.tensor_tensor(EW[:], E[:, b], w[:].broadcast_to([P, G, P]), ALU.mult))
                        dve.wait_ge(c.sem, c.value())
                    dve.sem_inc(s["message_ready"], 1)

                onehots(0, 0)
                onehots(0, 1)
                start = c.n
                tiles = tiles_of(0, NBUF)
                for b in range(NBUF):
                    step(0, b, b == 0, tiles[b], tiles[b - 1])
                per = c.n - start
                with dve.Fori(1, turns) as i:
                    c.enter(i - 1, per)
                    tiles = tiles_of(i * NBUF - 1, NBUF + 1)
                    for b in range(NBUF):
                        step(i, b, False, tiles[b + 1], tiles[b])
                    c.leave(turns - 1)
                add_sum(turns - 1, NBUF - 1, tiles_of(NG - 1, 1)[0])

            @block.tensor
            def _(pe):
                def scores(i, b, a):
                    c = b % NBUF
                    for k in range(GH):
                        blk = a * GH + k
                        for h in range(HN):
                            nc.tensor.matmul(ps[a][:, k, h, :], rows[:, c, blk, acol + h:acol + h + 1].broadcast_to([P, P]), g["ident"][:], start=True, stop=False)
                            ins = nc.tensor.matmul(ps[a][:, k, h, :], NEG[:, c, blk, :], g["identb"][:], start=False, stop=True)
                    ins.then_inc(s[f"scores_ready_{a}"], 1)

                def turn_onehots(i, b):
                    c = b % NBUF
                    grp = i * NBUF + b
                    pe.wait_ge(s["neg_ready"], grp + 1)
                    if b or not isinstance(i, int):
                        pe.wait_ge(s["onehot_T_ready"], grp)
                    for k in range(G):
                        ins = nc.tensor.transpose(pt[:, k, :], NEG[:, c, k, :], g["identb"][:])
                    ins.then_inc(s["onehot_turned"], 1)

                def keep_warm(n):
                    for _ in range(n):
                        nc.tensor.matmul(warm[:], g["identb"][:], g["identb"][:], start=True, stop=True)

                turn_onehots(0, 0)
                turn_onehots(0, 1)
                pe.wait_ge(s["rows_in_0"], 16 * G)
                for a in range(2):
                    scores(0, 0, a)
                with pe.Fori(0, turns) as i:
                    for b in range(NBUF):
                        grp = i * NBUF + b
                        nb = (b + 1) % NBUF
                        pe.wait_ge(s[f"rows_in_{nb}"], i * (16 * G) + (16 * G * (1 + (b + 1) // NBUF)))
                        pe.wait_ge(s["scores_read_0"], grp + 1)
                        scores(i, b + 1, 0)
                        pe.wait_ge(s["target_ready"], grp + 1)
                        for k in range(G):
                            ins = nc.tensor.matmul(pe8[:, k, :], ET[:, b, k, :], tm[:].rearrange("p a h -> p (a h)"), start=True, stop=True)
                        ins.then_inc(s["target_in"], 1)
                        pe.wait_ge(s["scores_read_1"], grp + 1)
                        scores(i, b + 1, 1)
                        keep_warm(0 if HN > 1 else 12)
                        pe.wait_ge(s["message_ready"], grp + 1)
                        for k in range(G):
                            ins = nc.tensor.matmul(psum_[:, 0:NM], E[:, b, k, :] if HN > 1 else EW[:, k, :],
                                                   msg[:, k].rearrange("p h e -> p (h e)") if HN > 1 else rows[:, b, k, 0:NM], start=(k == 0), stop=(k == G - 1))
                        ins.then_inc(s["sum_ready"], 1)
                        turn_onehots(i, b + 2)


def route(nc, g, sem, sb, acc, small, gates):
    c_, a_ = sem("route_step"), sem("route_act")
    with ExitStack() as sc:
        def t(name, shape):
            return sb("route_" + name, shape, F32, sc)
        agg, inv, m, sq = t("agg", [P, T, 16]), t("inv", [P, T, HEADS]), t("mean", [P, T]), t("sq", [P, T, 16])
        sco, cnt, cmp_, top, e = t("score", [P, T, NE0]), t("above", [P, T, NE0]), t("cmp", [P, T]), t("top", [P, T]), t("exp", [P, T, NE0])
        with nc.Block() as block:
            @block.vector
            def _(dve):
                c = Count(c_)

                def link(ins):
                    dve.wait_ge(c.sem, c.mark(ins))
                bc = lambda a, n: a.unsqueeze(2).broadcast_to([P, T, n])
                row = lambda k: small[:, k, :].unsqueeze(1).broadcast_to([P, T, 16])
                link(nc.vector.tensor_scalar(inv[:], acc[:, :, :, NE0], 1e-16, None, ALU.add))
                link(nc.vector.reciprocal(inv[:], inv[:]))
                link(nc.vector.tensor_tensor(agg[:].rearrange("p t (h e) -> p t h e", e=NE0), acc[:, :, :, 0:NE0],
                                             inv[:].unsqueeze(3).broadcast_to([P, T, HEADS, NE0]), ALU.mult))
                link(nc.vector.tensor_tensor(agg[:], agg[:], row(2), ALU.add))
                link(nc.vector.tensor_reduce(m[:], agg[:], X, ALU.add))
                link(nc.vector.tensor_scalar(m[:], m[:], 1.0 / 16, None, ALU.mult))
                link(nc.vector.tensor_tensor(agg[:], agg[:], bc(m[:], 16), ALU.subtract))
                link(nc.vector.tensor_tensor(sq[:], agg[:], agg[:], ALU.mult))
                link(nc.vector.tensor_reduce(m[:], sq[:], X, ALU.add))
                link(nc.vector.tensor_scalar(m[:], m[:], 1.0 / 16, EPS, ALU.mult, ALU.add))
                dve.sem_inc(a_, 1)
                dve.wait_ge(a_, 2)
                link(nc.vector.reciprocal(m[:], m[:]))
                link(nc.vector.tensor_tensor(agg[:], agg[:], bc(m[:], 16), ALU.mult))
                link(nc.vector.tensor_tensor(agg[:], agg[:], row(3), ALU.mult))
                link(nc.vector.tensor_tensor(agg[:], agg[:], row(4), ALU.add))
                link(nc.vector.tensor_reduce(sco[:], agg[:].rearrange("p t (h e) -> p t e h", e=NE0), X, ALU.add))
                link(nc.vector.tensor_scalar(sco[:], sco[:], 1.0 / HEADS, None, ALU.mult))
                link(nc.vector.tensor_reduce(top[:], sco[:], X, ALU.max))
                link(nc.vector.tensor_tensor(e[:], sco[:], bc(top[:], NE0), ALU.subtract))
                dve.sem_inc(a_, 1)
                link(nc.vector.memset(cnt[:], 0.0))
                for a in range(NE0):
                    for b in range(NE0):
                        if a != b:
                            link(nc.vector.tensor_tensor(cmp_[:], sco[:, :, b], sco[:, :, a], ALU.is_ge if b < a else ALU.is_gt))
                            link(nc.vector.tensor_tensor(cnt[:, :, a], cnt[:, :, a], cmp_[:], ALU.add))
                dve.wait_ge(a_, 4)
                link(nc.vector.scalar_tensor_tensor(e[:], cnt[:], 2.0, e[:], ALU.is_lt, ALU.mult))
                link(nc.vector.tensor_reduce(m[:], e[:], X, ALU.add))
                link(nc.vector.reciprocal(m[:], m[:]))
                link(nc.vector.tensor_tensor(gates[:], e[:], bc(m[:], NE0), ALU.mult))

            @block.scalar
            def _(act):
                act.wait_ge(a_, 1)
                nc.scalar.sqrt(m[:], m[:]).then_inc(a_, 1)
                act.wait_ge(a_, 3)
                nc.scalar.activation(e[:], e[:], ACT.Exp).then_inc(a_, 1)


def experts0(nc, A, g, sem, sb, pb, gates):
    s = {k: sem("ex0_" + k) for k in ("loaded", "up_ready", "hidden_ready", "down_ready", "biased", "added")}
    FT, HALF = F0 // P, TT * P // 2
    with ExitStack() as sc:
        def t(name, shape, dt=F32):
            return sb("ex0_" + name, shape, dt, sc)
        W1, W2 = t("W1", [P, NE0, H2, F0]), t("W2", [P, NE0, FT, D])
        b1, b2 = t("b1", [P, NE0 * FT]), t("b2", [P, NE0, D])
        hid = t("hidden", [P, 2, FT, TT * P])
        up = pb("ex0_up", [P, 2, 2, 512], sc)
        dn = pb("ex0_down", [P, 2, 512], sc)
        with nc.Block() as block:
            @block.sync
            def _(sp):
                for e in range(NE0):
                    sp.dma_start(W1[:, e], A["W1"][e].rearrange("(h p) f -> p h f", p=P)).then_inc(s["loaded"], 16)
                    sp.dma_start(W2[:, e], A["W2"][e].rearrange("(f p) d -> p f d", p=P)).then_inc(s["loaded"], 16)
                sp.dma_start(b1[:], A["b1"]).then_inc(s["loaded"], 16)
                sp.dma_start(b2[:], A["b2"].partition_broadcast(P)).then_inc(s["loaded"], 16)
                sp.wait_ge(s["loaded"], 16 * (2 * NE0 + 2))

            @block.tensor
            def _(pe):
                U, Hd, Dn, Ad = (Count(s[k]) for k in ("up_ready", "hidden_ready", "down_ready", "added"))
                pe.wait_ge(s["loaded"], 16 * (2 * NE0 + 2))
                nu, nd = NE0 * FT, NE0 * TT
                with pe.Fori(0, NTT) as i:
                    def up_(e):
                        for f in range(FT):
                            pe.wait_ge(Hd.sem, i * nu + (e * FT + f + 1))
                            for n in range(2):
                                for h in range(H2):
                                    ins = nc.tensor.matmul(up[:, f % 2, n, 0:HALF], W1[:, e, h, f * P:(f + 1) * P],
                                                           g["xnT"][:, h, bass.ds(i * (TT * P) + n * HALF, HALF)], start=(h == 0), stop=(h == 1))
                            ins.then_inc(U.sem, 1)

                    def down_(e):
                        pe.wait_ge(Hd.sem, i * nu + ((e + 1) * FT + 2))
                        for k in range(TT):
                            n = e * TT + k
                            pe.wait_ge(Ad.sem, i * nd + n + 1)
                            for f in range(FT):
                                ins = nc.tensor.matmul(dn[:, n % 2, 0:D], hid[:, e % 2, f, k * P:(k + 1) * P], W2[:, e, f, :], start=(f == 0), stop=(f == FT - 1))
                            ins.then_inc(Dn.sem, 1)

                    up_(0)
                    for e in range(NE0):
                        if e + 1 < NE0:
                            up_(e + 1)
                        down_(e)

            @block.scalar
            def _(act):
                act.sem_inc(s["hidden_ready"], 2)
                act.wait_ge(s["loaded"], 16 * (2 * NE0 + 2))
                nu, nd = NE0 * FT, NE0 * TT
                act.sem_inc(s["down_ready"], TT)
                with act.Fori(0, NTT) as i:
                    for e in range(NE0):
                        act.wait_ge(s["down_ready"], i * nd + (e - 1) * TT + TT if e else i * nd + 0 + 1)
                        for f in range(FT):
                            act.wait_ge(s["up_ready"], i * nu + (e * FT + f + 1))
                            nc.scalar.activation(hid[:, e % 2, f, :].rearrange("p (n c) -> p n c", n=2), up[:, f % 2, :, 0:HALF],
                                                 ACT.Gelu, bias=b1[:, e * FT + f:e * FT + f + 1]).then_inc(s["hidden_ready"], 1)

            @block.vector
            def _(dve):
                dve.sem_inc(s["added"], 2)
                dve.wait_ge(s["loaded"], 16 * (2 * NE0 + 2))
                nd = NE0 * TT
                with dve.Fori(0, NTT) as i:
                    for e in range(NE0):
                        for k in range(TT):
                            n = e * TT + k
                            if e:
                                dve.wait_ge(s["added"], i * nd + n + 1 + 2 - TT)
                            tile, gate = one(g["x"], i, k), gates[:, bass.ds(i * TT + k, 1), e]
                            nc.vector.scalar_tensor_tensor(tile, b2[:, e, :], gate, tile, ALU.mult, ALU.add).then_inc(s["biased"], 1)
                            dve.wait_ge(s["biased"], i * nd + n + 1)
                            dve.wait_ge(s["down_ready"], i * nd + n + 1 + TT)
                            nc.vector.scalar_tensor_tensor(tile, dn[:, n % 2, 0:D], gate, tile,
                                                           ALU.mult, ALU.add).then_inc(s["added"], 1)
                dve.wait_ge(s["added"], NTT * nd + 2)


def table1(nc, g, sem, sb, pb, wl, bl, wa, ba, row, acc, tab1):
    out_, ready, zr = sem("rows1_out"), sem("rows1_ready"), sem("rows1_zero_ready")
    rows_s = sem("rows1_step")
    target = sb("rows1_target", [P, TT], F32, g["scope"])
    junk = row[:, TT:2 * TT, 0:D]

    def start(dve):
        nc.vector.memset(row[0:1, 2 * TT, :], 0.0).then_inc(zr, 1)
        nc.vector.memset(row[:, 0:TT, D:D + 1], 1.0).then_inc(zr, 1)
        dve.wait_ge(zr, 2)

    def use(dve, i, k, ps, used):
        if k == 0:
            dve.wait_ge(out_, i * (16 * TT) + 16)
        r = row[:, k, :]
        v = used.mark(nc.vector.tensor_tensor(r[:, 0:D], ps, bl[:], ALU.add))
        dve.wait_ge(used.sem, v)
        used.mark(nc.vector.tensor_tensor_reduce(junk[:, k, :], r[:, 0:D], wa[:, 1, :], 1.0, ba[:, 1:2], ALU.mult, ALU.add, r[:, D + 1:D + 2]))
        v = used.mark(nc.vector.tensor_tensor_reduce(row[:, 2 * TT + 1 + k, 0:D], r[:, 0:D], wa[:, 0, :], 1.0, ba[:, 0:1], ALU.mult, ALU.add,
                                                     target[:, k:k + 1]))
        if k == TT - 1:
            dve.wait_ge(used.sem, v)
            dve.sem_inc(ready, 1)
            move(nc, g["a1"][:, bass.ds(i * TT, TT), :].rearrange("p t a -> p (t a)"), target[:]).then_inc(rows_s, 1)
            dve.wait_ge(rows_s, i + 1)

    def rows_out(block, used):
        @block.sync
        def _(sp):
            sp.wait_ge(zr, 2)
            sp.dma_start(tab1[N:N + 1, :], row[0:1, 2 * TT, :]).then_inc(out_, 16)
            whole = NFULL // TT
            with sp.Fori(0, whole) as i:
                sp.wait_ge(ready, i + 1)
                for k in range(TT):
                    sp.dma_start(tab1[bass.ds((i * TT + k) * P, P), :], row[:, k, :]).then_inc(out_, 16)
            for i in range(whole, NTT):
                sp.wait_ge(ready, i + 1)
                for k in range(TT):
                    n0 = (i * TT + k) * P
                    n = min(P, N - n0)
                    sp.dma_start(tab1[n0:n0 + n, :], row[0:n, k, :]).then_inc(out_, 16)
            sp.wait_ge(out_, 16 * (T + 1))

    project(nc, g, sem, sb, pb, "layer", lambda h: wl[:, h, :], D, use, per_use=3, rows_out=rows_out, start=start)


def finish1(nc, g, sem, sb, acc):
    c_ = sem("finish1_step")
    with ExitStack() as sc:
        inv = sb("finish1_inv", [P, T], F32, sc)
        with nc.Block() as block:
            @block.vector
            def _(dve):
                c = Count(c_)

                def link(ins):
                    dve.wait_ge(c.sem, c.mark(ins))
                link(nc.vector.tensor_scalar(inv[:], acc[:, :, D], 1e-30, None, ALU.max))
                link(nc.vector.reciprocal(inv[:], inv[:]))
                with dve.Fori(0, NTT) as i:
                    for k in range(TT):
                        nc.vector.scalar_tensor_tensor(one(g["x"], i, k), one(acc, i, k)[:, 0:D], one(inv, i, k), one(g["x"], i, k),
                                                       ALU.mult, ALU.add).then_inc(c_, 1)
                dve.wait_ge(c_, 2 + T)


def moe(nc, A, g, sem, sb, pb, out):
    x, buf, ybuf = g["x"], nc.dram_tensor("expert_in", (NE1 * SLOTS, D), F32).ap(), nc.dram_tensor("expert_out", (NE1 * SLOTS, D), F32).ap()
    OUT = NE1 * SLOTS
    with ExitStack() as sc:
        def t(name, shape, dt=F32, where=sc):
            return sb("moe_" + name, shape, dt, where)
        slot, prob = t("slot", [P, T], I32), t("prob", [P, T])
        w1, w2 = t("w1", [P, 2, H2, F1]), t("w2", [P, 2, F1 // P, D])
        first_in = sem("ex1_first_weights_in")
        with ExitStack() as s2:
            xn = t("xn", [P, T, D], F32, s2)
            gw, gb = t("gate_w", [P, H2, NE1], F32, s2), t("gate_b", [P, NE1], F32, s2)
            lg = t("logits", [P, T, NE1], F32, s2)
            load_small(nc, sem, [(gw[:], A["gate_w"].rearrange("(h p) f -> p h f", p=P)), (gb[:], A["gate_b"].partition_broadcast(P))], "gate")

            def keep(dve, i, k, ps, used):
                used.mark(nc.vector.tensor_tensor(one(lg, i, k), ps, gb[:], ALU.add))
            project(nc, g, sem, sb, pb, "gate", lambda h: gw[:, h, :], NE1, keep, keep_x=xn)
            dispatch(nc, A, g, sem, sb, pb, lg, slot, prob, xn, buf, OUT, w1, w2, first_in)
        experts1(nc, A, g, sem, sb, pb, buf, ybuf, w1, w2, first_in)
        collect(nc, g, sem, sb, slot, prob, ybuf, OUT, out)


def load_expert(sp, A, w1, w2, e, loaded):
    sp.dma_start(w1[:, e % 2], A["w1"][e].rearrange("(h p) f -> p h f", p=P)).then_inc(loaded, 16)
    sp.dma_start(w2[:, e % 2], A["w2"][e].rearrange("(f p) d -> p f d", p=P)).then_inc(loaded, 16)


def dispatch(nc, A, g, sem, sb, pb, lg, slot, prob, xn, buf, OUT, w1, w2, first_in):
    c_, exp_in, exp_out, oh_ready, pre_ready, zeroed, cleared, slots, sent = (sem("dispatch_" + k) for k in (
        "step", "exp_in", "exp_out", "onehot_ready", "prefix_ready", "zero_ready", "cleared", "slots_ready", "sent"))
    with ExitStack() as sc:
        def t(name, shape, dt=F32):
            return sb("dispatch_" + name, shape, dt, sc)
        top, e, oh, taken, hit = t("top", [P, T]), t("exp", [P, T, NE1]), t("onehot", [P, T, NE1]), t("taken", [P, T]), t("hit", [P, T])
        pre, tot, inc, sl, base = t("prefix", [P, T, NE1]), t("totals", [P, T, NE1]), t("scan", [P, NE1, T]), t("slot_f", [P, T]), t("base", [P, NE1])
        sm, upto_ = t("sum", [P, T]), t("row_upto_column", [P, P])
        zero = t("zero", [P, 4 * D])
        ps = pb("dispatch_ps", [P, 2, 512], sc)
        bc = lambda a: a.unsqueeze(2).broadcast_to([P, T, NE1])
        with nc.Block() as block:
            @block.vector
            def _(dve):
                c = Count(c_)

                def link(ins):
                    dve.wait_ge(c.sem, c.mark(ins))
                nc.vector.memset(zero[:], 0.0).then_inc(zeroed, 1)
                link(nc.vector.tensor_scalar(upto_[:], g["iota"][:, 0:P], g["pidx"][:], None, ALU.is_ge))
                link(nc.vector.tensor_reduce(top[:], lg[:], X, ALU.max))
                link(nc.vector.tensor_tensor(e[:], lg[:], bc(top[:]), ALU.subtract))
                dve.sem_inc(exp_in, 1)
                dve.wait_ge(exp_out, 1)
                link(nc.vector.tensor_reduce(sm[:], e[:], X, ALU.add))
                link(nc.vector.reciprocal(sm[:], sm[:]))
                link(nc.vector.tensor_tensor(e[:], e[:], bc(sm[:]), ALU.mult))
                link(nc.vector.tensor_reduce(prob[:], e[:], X, ALU.max))
                link(nc.vector.memset(taken[:], 0.0))
                link(nc.vector.tensor_scalar(taken[:, T - 1:T], g["pidx"][:], float(NREST), None, ALU.is_ge))
                for k in range(NE1):
                    link(nc.vector.tensor_tensor(hit[:], e[:, :, k], prob[:], ALU.is_ge))
                    link(nc.vector.tensor_tensor(oh[:, :, k], hit[:], taken[:], ALU.is_gt))
                    link(nc.vector.tensor_tensor(taken[:], taken[:], oh[:, :, k], ALU.add))
                dve.sem_inc(oh_ready, 1)
                dve.wait_ge(pre_ready, 1)
                flat = lambda a: a[:].rearrange("p t e -> p (t e)")
                link(nc.vector.tensor_copy(flat(pre), ps[:, 0, 0:T * NE1]))
                link(nc.vector.tensor_copy(flat(tot), ps[:, 1, 0:T * NE1]))
                for k in range(NE1):
                    link(nc.vector.tensor_tensor_scan(inc[:, k, :], g["ones"][:, 0:T], tot[:, :, k], 0.0, ALU.mult, ALU.add))
                link(nc.vector.tensor_tensor(pre[:], pre[:], inc[:].rearrange("p e t -> p t e"), ALU.add))
                link(nc.vector.tensor_tensor(pre[:], pre[:], tot[:], ALU.subtract))
                link(nc.vector.tensor_tensor(pre[:], pre[:], oh[:], ALU.mult))
                link(nc.vector.tensor_reduce(sl[:], pre[:], X, ALU.add))
                link(nc.vector.tensor_scalar(base[:], g["iota"][:, 0:NE1], float(SLOTS), None, ALU.mult))
                link(nc.vector.tensor_tensor(e[:], oh[:], base[:].unsqueeze(1).broadcast_to([P, T, NE1]), ALU.mult))
                link(nc.vector.tensor_reduce(sm[:], e[:], X, ALU.add))
                link(nc.vector.tensor_tensor(sm[:], sm[:], sl[:], ALU.add))
                link(nc.vector.tensor_scalar(sm[:], sm[:], -1.0 - OUT, None, ALU.add))
                link(nc.vector.tensor_scalar(hit[:], sl[:], float(CAP), None, ALU.is_le))
                link(nc.vector.scalar_tensor_tensor(hit[:], sl[:], 0.0, hit[:], ALU.is_gt, ALU.mult))
                link(nc.vector.tensor_tensor(sm[:], sm[:], hit[:], ALU.mult))
                link(nc.vector.tensor_scalar(sm[:], sm[:], float(OUT), None, ALU.add))
                link(nc.vector.tensor_copy(slot[:], sm[:]))
                link(nc.vector.tensor_tensor(prob[:], prob[:], hit[:], ALU.mult))
                dve.sem_inc(slots, 1)

            @block.scalar
            def _(act):
                act.wait_ge(exp_in, 1)
                nc.scalar.activation(e[:], e[:], ACT.Exp).then_inc(exp_out, 1)

            @block.tensor
            def _(pe):
                pe.wait_ge(oh_ready, 1)
                flat = oh[:].rearrange("p t e -> p (t e)")
                nc.tensor.matmul(ps[:, 0, 0:T * NE1], upto_[:], flat, start=True, stop=True)
                nc.tensor.matmul(ps[:, 1, 0:T * NE1], g["ones"][:], flat, start=True, stop=True).then_inc(pre_ready, 1)

            @block.sync
            def _(sp):
                sp.wait_ge(zeroed, 1)
                for k in range(OUT // (4 * P)):
                    sp.dma_start(buf[k * 4 * P:(k + 1) * 4 * P, :].rearrange("(p a) d -> p (a d)", p=P), zero[:]).then_inc(cleared, 16)
                for e in range(2):
                    load_expert(sp, A, w1, w2, e, first_in)
                sp.wait_ge(cleared, 16 * (OUT // (4 * P)))

            @block.gpsimd
            def _(pool):
                pool.wait_ge(slots, 1)
                pool.wait_ge(cleared, 16 * (OUT // (4 * P)))
                for k in range(T):
                    nc.gpsimd.indirect_dma_start(buf[:, :], bass.IndirectOffsetOnAxis(ap=slot[:, k:k + 1], axis=0), xn[:, k, :], None,
                                                 bounds_check=OUT - 1, oob_is_err=False).then_inc(sent, 16)
                pool.wait_ge(sent, 16 * T)


def experts1(nc, A, g, sem, sb, pb, buf, ybuf, w1, w2, first_in):
    s = {k: sem("ex1_" + k) for k in ("in_a", "in_b", "bias_in", "turned", "turned_kept", "up_ready", "hidden_ready", "down_ready",
                                      "added", "out_a", "out_b", "w_free", "y_free")}
    KS, FT = SLOTS // P, F1 // P
    with ExitStack() as sc:
        def t(name, shape, dt=F32):
            return sb("ex1_" + name, shape, dt, sc)
        xe, xT = t("x", [P, 2, KS, D]), t("xT", [P, H2, SLOTS])
        b1, b2 = t("b1", [P, NE1 * FT]), t("b2", [P, NE1, D])
        hid = t("hidden", [P, FT, SLOTS])
        y = t("y", [P, 2, KS, D])
        pt = pb("ex1_turn", [P, 2, 512], sc)
        up = pb("ex1_up", [P, 2, 512], sc)
        dn = pb("ex1_down", [P, 2, 512], sc)
        with nc.Block() as block:
            @block.sync
            def _(sp):
                sp.sem_inc(s["w_free"], 2)
                for e in range(NE1):
                    b = e % 2
                    sp.wait_ge(s["w_free"], e + 1)
                    sp.dma_start(xe[:, b], buf[e * SLOTS:(e + 1) * SLOTS, :].rearrange("(k p) d -> p k d", p=P)).then_inc(s[f"in_{'ab'[b]}"], 16)
                    if e >= 2:
                        load_expert(sp, A, w1, w2, e, s[f"in_{'ab'[b]}"])
                    if e == 0:
                        sp.dma_start(b1[:], A["b1m"]).then_inc(s["bias_in"], 16)
                        sp.dma_start(b2[:], A["b2m"].partition_broadcast(P)).then_inc(s["bias_in"], 16)

            @block.gpsimd
            def _(pool):
                for e in range(NE1):
                    pool.wait_ge(s["y_free"], e + 1)
                    pool.dma_start(ybuf[e * SLOTS:(e + 1) * SLOTS, :].rearrange("(k p) d -> p k d", p=P), y[:, e % 2]).then_inc(s[f"out_{'ab'[e % 2]}"], 16)
                for b in "ab":
                    pool.wait_ge(s["out_" + b], 16 * (NE1 // 2))

            @block.tensor
            def _(pe):
                pe.wait_ge(first_in, 16 * 4)
                for e in range(NE1):
                    b = e % 2
                    pe.wait_ge(s[f"in_{'ab'[b]}"], 16 * (1 + 3 * (e // 2)))
                    for h in range(H2):
                        if e:
                            pe.wait_ge(s["turned_kept"], H2 * e)
                        for k in range(KS):
                            ins = nc.tensor.transpose(pt[:, h, k * P:(k + 1) * P], xe[:, b, k, h * P:(h + 1) * P], g["ident"][:])
                        ins.then_inc(s["turned"], 1)
                    pe.wait_ge(s["turned_kept"], H2 * (e + 1))
                    for f in range(FT):
                        n = e * FT + f
                        if n >= 2:
                            pe.wait_ge(s["hidden_ready"], n - 1)
                        for h in range(H2):
                            ins = nc.tensor.matmul(up[:, f % 2, :], w1[:, b, h, f * P:(f + 1) * P], xT[:, h, :], start=(h == 0), stop=(h == 1))
                        ins.then_inc(s["up_ready"], 1)
                    pe.wait_ge(s["hidden_ready"], (e + 1) * FT)
                    for k in range(KS):
                        n = e * KS + k
                        if n >= 2:
                            pe.wait_ge(s["added"], n - 1)
                        for f in range(FT):
                            ins = nc.tensor.matmul(dn[:, k % 2, 0:D], hid[:, f, k * P:(k + 1) * P], w2[:, b, f, :], start=(f == 0), stop=(f == FT - 1))
                        ins.then_inc(s["down_ready"], 1)
                    pe.wait_ge(s["down_ready"], (e + 1) * KS)
                    pe.sem_inc(s["w_free"], 1)

            @block.scalar
            def _(act):
                act.wait_ge(s["bias_in"], 32)
                for e in range(NE1):
                    for h in range(H2):
                        act.wait_ge(s["turned"], H2 * e + h + 1)
                        nc.scalar.copy(xT[:, h, :], pt[:, h, :]).then_inc(s["turned_kept"], 1)
                    if e:
                        act.wait_ge(s["down_ready"], e * KS)
                    for f in range(FT):
                        n = e * FT + f
                        act.wait_ge(s["up_ready"], n + 1)
                        nc.scalar.activation(hid[:, f, :], up[:, f % 2, :], ACT.Relu, bias=b1[:, n:n + 1]).then_inc(s["hidden_ready"], 1)

            @block.vector
            def _(dve):
                dve.wait_ge(s["bias_in"], 32)
                for e in range(NE1):
                    if e >= 2:
                        dve.wait_ge(s[f"out_{'ab'[e % 2]}"], 16 * (e // 2))
                    for k in range(KS):
                        n = e * KS + k
                        dve.wait_ge(s["down_ready"], n + 1)
                        nc.vector.tensor_tensor(y[:, e % 2, k, :], dn[:, k % 2, 0:D], b2[:, e, :], ALU.add).then_inc(s["added"], 1)
                    dve.wait_ge(s["added"], (e + 1) * KS)
                    dve.sem_inc(s["y_free"], 1)


def collect(nc, g, sem, sb, slot, prob, ybuf, OUT, out):
    zeroed, c_, ready, done = (sem("collect_" + k) for k in ("zeroed", "step", "ready", "out"))
    got = [sem(f"collect_rows_in_{q}") for q in range(NTT)]
    x = g["x"]
    with ExitStack() as sc:
        def t(name, shape, dt=F32):
            return sb("collect_" + name, shape, dt, sc)
        y, m, lim = t("y", [P, T, D]), t("mask", [P, T, D]), t("limits", [P, 3])
        with nc.Block() as block:
            @block.vector
            def _(dve):
                c = Count(c_)

                def link(ins):
                    dve.wait_ge(c.sem, c.mark(ins))
                nc.vector.memset(y[:], 0.0).then_inc(zeroed, 1)
                for k, v in enumerate((0.0, 10000.0, -10000.0)):
                    link(nc.vector.memset(lim[:, k:k + 1], v))
                big = 3.4028234e38
                for q in range(NTT):
                    yq, mq, xq = (a[:, q * TT:(q + 1) * TT, :] for a in (y, m, x))
                    dve.wait_ge(got[q], 16 * TT)
                    link(nc.vector.tensor_tensor(yq, yq, prob[:, q * TT:(q + 1) * TT].unsqueeze(2).broadcast_to([P, TT, D]), ALU.mult))
                    for k, (op, v) in enumerate(((None, 0.0), (ALU.is_gt, big), (ALU.is_lt, -big))):
                        if op is None:
                            link(nc.vector.tensor_tensor(mq, yq, yq, ALU.not_equal))
                        else:
                            link(nc.vector.tensor_scalar(mq, yq, v, None, op))
                        link(nc.vector.copy_predicated(yq.rearrange("p t d -> p (t d)"), mq.rearrange("p t d -> p (t d)").bitcast(I32),
                                                       lim[:, k:k + 1].broadcast_to([P, TT * D])))
                    link(nc.vector.tensor_tensor(xq, xq, yq, ALU.add))
                    dve.sem_inc(ready, 1)

            @block.gpsimd
            def _(pool):
                pool.wait_ge(zeroed, 1)
                for k in range(T):
                    nc.gpsimd.indirect_dma_start(y[:, k, :], None, ybuf[:, :], bass.IndirectOffsetOnAxis(ap=slot[:, k:k + 1], axis=0),
                                                 bounds_check=OUT - 1, oob_is_err=False).then_inc(got[k // TT], 16)

            @block.sync
            def _(sp):
                for q in range(NTT):
                    sp.wait_ge(ready, q + 1)
                    last = min((q + 1) * TT, NFULL)
                    sp.dma_start(out[q * TT * P:last * P, :].rearrange("(t p) d -> p t d", p=P), x[:, q * TT:last, :]).then_inc(done, 16)
                sp.dma_start(out[NFULL * P:N, :], x[0:NREST, NFULL, :]).then_inc(done, 16)
                sp.wait_ge(done, 16 * (NTT + 1))


_INS = {"x": "x", "src": "src", "dst": "dst", "w": "edge_weight", "W_gat": "L0_ffn_W_gat", "att_src": "L0_ffn_att_src",
        "att_dst": "L0_ffn_att_dst", "b_gat": "L0_ffn_b_gat", "ln_gamma": "L0_ffn_ln_gamma", "ln_beta": "L0_ffn_ln_beta",
        "W1": "L0_ffn_W1", "b1": "L0_ffn_b1", "W2": "L0_ffn_W2", "b2": "L0_ffn_b2", "ei": "L0_ffn_edge_index",
        "W_layer": "L1_gnn_W_layer", "b_layer": "L1_gnn_b_layer", "w_a1": "L1_gnn_w_a1", "b_a1": "L1_gnn_b_a1",
        "w_a2": "L1_gnn_w_a2", "b_a2": "L1_gnn_b_a2", "gate_w": "L1_ffn_gate_w", "gate_b": "L1_ffn_gate_b",
        "w1": "L1_ffn_w1", "b1m": "L1_ffn_b1", "w2": "L1_ffn_w2", "b2m": "L1_ffn_b2"}


def kernel(**inputs):
    import numpy as _np
    import concourse.bacc as _bacc
    from concourse import mybir as _mybir
    from concourse.bass_utils import run_bass_kernel_spmd as _run

    nc = _bacc.Bacc("TRN2", target_bir_lowering=False, num_devices=1)
    arrays, aps = {}, {}
    for short, name in _INS.items():
        a = _np.asarray(inputs[name])
        if short == "W_layer":
            a = a.T
        if short in ("b1", "b1m"):
            a = a.reshape(-1, P).T
        a = _np.ascontiguousarray(a)
        arrays[f"in_{short}"] = a
        aps[short] = nc.dram_tensor(f"in_{short}", a.shape, _mybir.dt.from_np(a.dtype), kind="ExternalInput").ap()
    out = nc.dram_tensor("out_0", (N, D), F32, kind="ExternalOutput").ap()
    build(nc, aps, out)
    r = _run(nc, [arrays], core_ids=[0])
    return r.results[0]["out_0"]
```
